# Optimizing a Trainium2 kernel written in Bass

```python
import numpy as np
import jax
import jax.numpy as jnp

def _softmax(x, axis=-1):
    return jax.nn.softmax(x, axis=axis)

def _gelu(x):
    return jax.nn.gelu(x, approximate=True)

def _silu(x):
    return jax.nn.silu(x)

def _sigmoid(x):
    return jax.nn.sigmoid(x)

def _layernorm(x, axis=-1, eps=1e-05):
    m = jnp.mean(x, axis=axis, keepdims=True)
    v = jnp.var(x, axis=axis, keepdims=True)
    return (x - m) / jnp.sqrt(v + eps)

def _scatter_add(tgt, idx, src, axis=0):
    return tgt.at[idx].add(src)

def _segment_sum(src, seg, n):
    return jax.ops.segment_sum(src, seg, n)
kernel_name = 'mk_conv_attn_hybrid_d2_conv_nchw512_r2_44bffa'

def setup_inputs(seed: int=0):
    np.random.seed(seed)
    _w = jnp.asarray

    def _rec_inputs():
        import jax
        import jax.numpy as jnp
        _gk = jax.random.key(seed)
        x = 7.22e-05 + 1 * jax.random.normal(jax.random.fold_in(_gk, 1), (4, 256, 32, 32), jnp.float32)
        return x
    x = _rec_inputs()

    def _L0_conv_setup():
        import jax, jax.numpy as jnp
        import numpy as np
        C = 256
        C8 = C // 8
        key = jax.random.key(seed)
        kx, kq, kk, kv = jax.random.split(key, 4)
        x = jax.random.normal(kx, (4, C, 32, 32), dtype=jnp.float32)
        wq = jax.random.normal(kq, (C8, C), dtype=jnp.float32) * (1.0 / np.sqrt(C))
        wk = jax.random.normal(kk, (C8, C), dtype=jnp.float32) * (1.0 / np.sqrt(C))
        wv = jax.random.normal(kv, (C, C), dtype=jnp.float32) * (1.0 / np.sqrt(C))
        gamma = jnp.full((1,), 0.1, dtype=jnp.float32)
        return {'x': x, 'wq': wq, 'wk': wk, 'wv': wv, 'gamma': gamma}
    _L0_conv_all = _L0_conv_setup()
    _L0_conv_in = {k: v for k, v in _L0_conv_all.items() if k in ('wq', 'wk', 'wv', 'gamma')}
    del _L0_conv_all

    def _L1_attn_setup():
        import jax, jax.numpy as jnp
        import numpy as np
        NUM_GROUPS = 32
        NUM_HEADS = 8
        EPS = 1e-05
        key = jax.random.key(seed)
        ks = jax.random.split(key, 4)
        B, N, C = (4, 1024, 256)
        s = 0.02
        return {'x': jax.random.normal(ks[0], (B, N, C), jnp.float32), 'gn_scale': jnp.ones((C,), jnp.float32), 'gn_bias': jnp.zeros((C,), jnp.float32), 'w_qkv': jax.random.normal(ks[1], (C, 3 * C), jnp.float32) * s, 'b_qkv': jnp.zeros((3 * C,), jnp.float32), 'w_proj': jax.random.normal(ks[2], (C, C), jnp.float32) * s, 'b_proj': jnp.zeros((C,), jnp.float32)}
    _L1_attn_all = _L1_attn_setup()
    _L1_attn_in = {k: v for k, v in _L1_attn_all.items() if k in ('gn_scale', 'gn_bias', 'w_qkv', 'b_qkv', 'w_proj', 'b_proj')}
    del _L1_attn_all

    def _L1_ffn_setup():
        import jax, jax.numpy as jnp
        import numpy as np
        E, D, H = (8, 256, 1024)
        B, N = (8, 256)
        key = jax.random.key(seed)
        ks = jax.random.split(key, 4)

        def init(k, shape, fan_in):
            return jax.random.normal(k, shape, jnp.float32) * (1.0 / np.sqrt(fan_in))
        return {'x': jax.random.normal(ks[0], (B, N, D), jnp.float32), 'Wr': init(ks[1], (D, E), D), 'br': jnp.zeros((E,), jnp.float32), 'W1': init(ks[2], (E, D, H), D), 'b1': jnp.zeros((E, H), jnp.float32), 'W2': init(ks[3], (E, H, D), H), 'b2': jnp.zeros((E, D), jnp.float32)}
    _L1_ffn_all = _L1_ffn_setup()
    _L1_ffn_in = {k: v for k, v in _L1_ffn_all.items() if k in ('Wr', 'br', 'W1', 'b1', 'W2', 'b2')}
    del _L1_ffn_all
    return {'x': x, 'L0_conv_wq': _L0_conv_in['wq'], 'L0_conv_wk': _L0_conv_in['wk'], 'L0_conv_wv': _L0_conv_in['wv'], 'L0_conv_gamma': _L0_conv_in['gamma'], 'L1_attn_gn_scale': _L1_attn_in['gn_scale'], 'L1_attn_gn_bias': _L1_attn_in['gn_bias'], 'L1_attn_w_qkv': _L1_attn_in['w_qkv'], 'L1_attn_b_qkv': _L1_attn_in['b_qkv'], 'L1_attn_w_proj': _L1_attn_in['w_proj'], 'L1_attn_b_proj': _L1_attn_in['b_proj'], 'L1_ffn_Wr': _L1_ffn_in['Wr'], 'L1_ffn_br': _L1_ffn_in['br'], 'L1_ffn_W1': _L1_ffn_in['W1'], 'L1_ffn_b1': _L1_ffn_in['b1'], 'L1_ffn_W2': _L1_ffn_in['W2'], 'L1_ffn_b2': _L1_ffn_in['b2']}

def reference(x, L0_conv_wq, L0_conv_wk, L0_conv_wv, L0_conv_gamma, L1_attn_gn_scale, L1_attn_gn_bias, L1_attn_w_qkv, L1_attn_b_qkv, L1_attn_w_proj, L1_attn_b_proj, L1_ffn_Wr, L1_ffn_br, L1_ffn_W1, L1_ffn_b1, L1_ffn_W2, L1_ffn_b2):
    import jax
    import jax.numpy as jnp

    def _L0_conv_ref(x, wq, wk, wv, gamma):
        import jax, jax.numpy as jnp
        import numpy as np
        C = 256
        C8 = C // 8
        b, c, h, w = x.shape
        hw = h * w
        xf = x.reshape(b, c, hw)
        q = jnp.einsum('oc,bcn->bno', wq, xf)
        k = jnp.einsum('oc,bcn->bon', wk, xf)
        v = jnp.einsum('oc,bcn->bon', wv, xf)
        scores = jnp.einsum('bio,boj->bij', q, k)
        attn = jax.nn.softmax(scores, axis=1)
        feats = jnp.einsum('bci,bij->bcj', v, attn)
        feats = feats.reshape(b, c, h, w)
        return gamma * feats + x

    def _L1_attn_ref(x, gn_scale, gn_bias, w_qkv, b_qkv, w_proj, b_proj):
        import jax, jax.numpy as jnp
        import numpy as np
        NUM_GROUPS = 32
        NUM_HEADS = 8
        EPS = 1e-05
        B, N, C = x.shape
        G = NUM_GROUPS
        H = NUM_HEADS
        d = C // H
        xg = x.reshape(B, N, G, C // G)
        mean = xg.mean(axis=(1, 3), keepdims=True)
        var = xg.var(axis=(1, 3), keepdims=True)
        h = ((xg - mean) * jax.lax.rsqrt(var + EPS)).reshape(B, N, C)
        h = h * gn_scale + gn_bias
        qkv = h @ w_qkv + b_qkv
        qkv = qkv.reshape(B, N, H, 3, d)
        q, k, v = (qkv[..., 0, :], qkv[..., 1, :], qkv[..., 2, :])
        scores = jnp.einsum('bnhd,bmhd->bhnm', q, k) * (1.0 / np.sqrt(d)).astype(x.dtype)
        attn = jax.nn.softmax(scores, axis=-1)
        vals = jnp.einsum('bhnm,bmhd->bnhd', attn, v).reshape(B, N, C)
        out = vals @ w_proj + b_proj
        return out + x

    def _L1_ffn_ref(x, Wr, br, W1, b1, W2, b2):
        import jax, jax.numpy as jnp
        import numpy as np
        E, D, H = (8, 256, 1024)
        B, N = (8, 256)
        b, n, d = x.shape
        xt = x.reshape(-1, d)
        route_prob = jax.nn.softmax(xt.astype(jnp.float32) @ Wr + br, axis=-1)
        routes = jnp.argmax(route_prob, axis=-1)
        p_max = jnp.max(route_prob, axis=-1)

        def expert_step(acc, inp):
            w1, bb1, w2, bb2, e = inp
            h = jax.nn.gelu(xt @ w1 + bb1, approximate=False)
            y = h @ w2 + bb2
            return (acc + y * (routes == e)[:, None].astype(y.dtype), None)
        out, _ = jax.lax.scan(expert_step, jnp.zeros_like(xt), (W1, b1, W2, b2, jnp.arange(E)))
        out = out * (p_max / jax.lax.stop_gradient(p_max))[:, None]
        return out.reshape(b, n, d)

    def _gn(v, G=32, eps=1e-05):
        B_, C_, H_, W_ = v.shape
        g = v.reshape(B_, G, C_ // G, H_, W_)
        m = jnp.mean(g, axis=(2, 3, 4), keepdims=True)
        s = jnp.var(g, axis=(2, 3, 4), keepdims=True)
        return ((g - m) / jnp.sqrt(s + eps)).reshape(v.shape)

    def _ln_c(v, eps=1e-06):
        m = jnp.mean(v, axis=1, keepdims=True)
        s = jnp.var(v, axis=1, keepdims=True)
        return (v - m) / jnp.sqrt(s + eps)

    def _ln_t(v, eps=1e-05):
        m = jnp.mean(v, axis=-1, keepdims=True)
        s = jnp.var(v, axis=-1, keepdims=True)
        return (v - m) / jnp.sqrt(s + eps)

    def _to_tokens(v):
        B_, C_, H_, W_ = v.shape
        return v.reshape(B_, C_, H_ * W_).transpose(0, 2, 1)

    def _from_tokens(t, like):
        B_, C_, H_, W_ = like.shape
        return t.transpose(0, 2, 1).reshape(B_, C_, H_, W_)
    x = _L0_conv_ref(x, L0_conv_wq, L0_conv_wk, L0_conv_wv, L0_conv_gamma)
    t = _to_tokens(x)
    t = t + _L1_attn_ref(_ln_t(t), L1_attn_gn_scale, L1_attn_gn_bias, L1_attn_w_qkv, L1_attn_b_qkv, L1_attn_w_proj, L1_attn_b_proj)
    t = t + _L1_ffn_ref(_ln_t(t), L1_ffn_Wr, L1_ffn_br, L1_ffn_W1, L1_ffn_b1, L1_ffn_W2, L1_ffn_b2)
    x = _from_tokens(t, x)
    return x

_drawn_inputs = setup_inputs


def setup_inputs(seed=0):
    import zlib

    import numpy as np

    out = dict(_drawn_inputs(seed))
    spreads = {'L1_attn_gn_scale': (1.0, 0.6),
     'L1_attn_gn_bias': (0.0, 0.277),
     'L1_attn_b_qkv': (0.0, 0.1),
     'L1_attn_b_proj': (0.0, 0.1),
     'L1_ffn_br': (0.0, 0.1),
     'L1_ffn_b1': (0.0, 0.1),
     'L1_ffn_b2': (0.0, 0.1)}
    factors = {'L1_attn_w_qkv': 2.874}
    for name, (base, spread) in spreads.items():
        noise = np.random.default_rng([zlib.crc32(name.encode()), seed]).standard_normal(out[name].shape)
        drawn = base * np.exp(spread * noise) if base else spread * noise
        out[name] = jnp.asarray(drawn.astype(out[name].dtype))
    for name, factor in factors.items():
        out[name] = (out[name] * factor).astype(out[name].dtype)
    return out
```

```python
from contextlib import ExitStack

import numpy as np

import concourse.bass as bass
from concourse import mybir

F32 = mybir.dt.float32
F32R = mybir.dt.float32r
I32 = mybir.dt.int32
ALU = mybir.AluOpType
ACT = mybir.ActivationFunctionType
AX = mybir.AxisListType

P = 128
B, C, N = 4, 256, 1024
CT = C // P
NB = N // P
HALF = 512
D = 32
NH = C // D
HG = P // D
GROUPS = 32
E, H = 8, 1024
KC = H // P
TB = B * NB
TILES = TB + E - 1
STACK = 3 * D
ROWS = STACK + 2
SLOTS = 3
LAG = 5
LN_EPS, GN_EPS = 1e-5, 1e-5
SCALE = float(1.0 / np.sqrt(D))
RSQRT_SEED = float(0x5F3759DF)

UNITS = NH + 1


class Steps:

    def __init__(self, eng, sem, base=0):
        self.eng, self.sem, self.base, self.n = eng, sem, base, 0

    def did(self, ins):
        self.n += 1
        ins.then_inc(self.sem, 1)

    def wait(self):
        self.eng.wait_ge(self.sem, self.base + self.n)


def raw(ap):
    return ap.bitcast(F32)


def flat(bank_pair):
    return bank_pair.rearrange("p a n -> p (a n)")


def rsqrt(nc, steps, out, v, tmp):
    steps.did(nc.vector.tensor_scalar(tmp.bitcast(I32), v.bitcast(I32), 1, None, ALU.logical_shift_right))
    steps.wait()
    steps.did(nc.vector.tensor_scalar(out.bitcast(I32), tmp.bitcast(I32), -1.0, RSQRT_SEED, ALU.mult, ALU.add))
    steps.wait()
    for _ in range(3):
        steps.did(nc.vector.tensor_tensor(tmp, out, out, ALU.mult))
        steps.wait()
        steps.did(nc.vector.scalar_tensor_tensor(tmp, tmp, -0.5, v, ALU.mult, ALU.mult))
        steps.wait()
        steps.did(nc.vector.scalar_tensor_tensor(out, tmp, 1.5, out, ALU.add, ALU.mult))
        steps.wait()


RSQRT_STEPS = 11
V_STEPS = NB * 4 + (1 + RSQRT_STEPS) + 2 * CT + (2 + 1 + RSQRT_STEPS + 2) + NB * 2 + (1 + RSQRT_STEPS)


def attention_phase(nc, io, keep, sems):
    with ExitStack() as ctx:
        def sb(name, shape, dt=F32):
            return ctx.enter_context(nc.sbuf_tensor(name, shape, dt))

        def ps(name, shape):
            return ctx.enter_context(nc.psum_tensor(name, shape, F32))

        def sem(name):
            return ctx.enter_context(nc.semaphore(name))

        ident, gmat = sb("ident", [P, P]), sb("gmat", [P, P])
        ones = sb("ones", [P, D])
        w_qk0, w_v0 = sb("w_qk0", [P, CT, 2 * D]), sb("w_v0", [P, CT, C])
        w_qk1, w_v1 = sb("w_qk1", [P, CT, 4, P]), sb("w_v1", [P, CT, C])
        w_pr, w_rt = sb("w_pr", [P, CT, C]), sb("w_rt", [P, CT, E])
        b_qk1, gnw = sb("b_qk1", [P, 4]), sb("gnw", [P, CT, 2])
        b_v1, b_pr = sb("b_v1", [P, C]), sb("b_pr", [P, C])
        b_rt, gamma = sb("b_rt", [P, E]), sb("gamma", [P, 1])
        x_c, x_t = sb("x_c", [P, CT, N]), sb("x_t", [P, NB, C])
        res, lnt = sb("res", [P, NB, C]), sb("lnt", [P, NB, C])
        h_c = sb("h_c", [P, CT, N])
        vals_t, vals_c, l2_c = x_t, x_c, h_c
        val = sb("val", [P, NB, C + 1])
        stk = [[sb(f"stk{s}{k}", [P, N], F32R) for k in "nm"] for s in range(SLOTS)]
        expd = sb("expd", [P, NB, N])
        hi = [sb(f"hi{s}", [P, N], F32R) for s in range(2)]
        lo = [sb(f"lo{s}", [P, N], F32R) for s in range(2)]
        vh = [sb(f"vh{s}", [P, NB, D]) for s in range(SLOTS)]
        osum = sb("osum", [P, HALF])
        nmax, msplit = sb("nmax", [P, NB]), sb("msplit", [P, 2 * NB], F32R)
        mrow = sb("mrow", [2 * NB, P], F32R)
        rc, rg, rc8 = sb("rc", [P, 1]), sb("rg", [P, 1]), sb("rc8", [P, 2, 4])
        bst, mv = sb("bst", [P, NB, 6]), sb("mv", [P, NB, 2])
        pause = sb("pause", [P, 1])
        var, rstd, tmp = sb("var", [P, NB]), sb("rstd", [P, NB]), sb("tmp", [P, NB])
        mvc, mg = sb("mvc", [P, CT, 2]), sb("mg", [P, CT])
        gdev, gw, gab = sb("gdev", [P, CT]), sb("gw", [P, CT]), sb("gab", [P, 2, CT])

        ps_m = ps("ps_m", [P, 2, HALF])
        ps_e = [ps(f"ps_e{k}", [P, 2, HALF]) for k in range(2)]
        ps_o = ps("ps_o", [P, HALF])
        ps_t = ps("ps_t", [P, HALF])

        consts_in, w1_in = sem("consts_in"), sems["w1_in"]
        x_in = sem("x_in")
        spilled = [sem(f"spilled{g}") for g in range(2)]
        stack_in = [sem(f"stack_in{s}") for s in range(SLOTS)]
        maxrow_in = [sem(f"maxrow_in{s}") for s in range(SLOTS)]
        stored = sems["stored"]
        pe_qk0, pe_v0, pe_max, pe_maxt = sem("pe_qk0"), sem("pe_v0"), sem("pe_max"), sem("pe_maxt")
        pe_exp, pe_pv0, pe_lnt, pe_gn = sem("pe_exp"), sem("pe_pv0"), sem("pe_lnt"), sem("pe_gn")
        pe_qk1, pe_v1, pe_pv, pe_ot = sem("pe_qk1"), sem("pe_v1"), sem("pe_pv"), sem("pe_ot")
        pe_vt, pe_pr, pe_l2t, pe_rt = sem("pe_vt"), sem("pe_pr"), sem("pe_l2t"), sem("pe_rt")
        a_hi0, a_v0, a_mrow, a_exp = sem("a_hi0"), sem("a_v0"), sem("a_mrow"), sem("a_exp")
        a_h, a_hi, a_vh, a_o, a_vt, a_l2t = sem("a_h"), sem("a_hi"), sem("a_vh"), sem("a_o"), sem("a_vt"), sem("a_l2t")
        v_set, v_step, v_mh, v_rc = sem("v_set"), sem("v_step"), sem("v_mh"), sem("v_rc")
        v_lo0, v_max, v_split, v_res0 = sem("v_lo0"), sem("v_max"), sem("v_split"), sem("v_res0")
        v_ln, v_gst, v_gdev, v_gab = sem("v_ln"), sem("v_gst"), sem("v_gdev"), sem("v_gab")
        v_lo, v_v1, v_norm, v_vt = sem("v_lo"), sem("v_v1"), sem("v_norm"), sem("v_vt")
        v_gd1 = sem("v_gd1")
        v_res1, v_l2, v_l2t, v_rt = sem("v_res1"), sem("v_l2"), sem("v_l2t"), sem("v_rt")
        g_res, g_zero = sem("g_res"), sem("g_zero")

        qk_scr = io["qk_scr"]
        consts = [
            (ident[:, :], io["ident"]), (gmat[:, :], io["gmat"]),
            (w_qk0[:, :, :], io["w_qk0"].rearrange("(t p) m -> p t m", p=P)),
            (w_v0[:, :, :], io["w_v0"].rearrange("(t p) m -> p t m", p=P)),
            (w_qk1[:, :, :, :], io["w_qk1"].rearrange("(t p) g m -> p t g m", p=P)),
            (w_v1[:, :, :], io["w_v1"].rearrange("(t p) m -> p t m", p=P)),
            (w_pr[:, :, :], io["w_pr"].rearrange("(t p) m -> p t m", p=P)),
            (w_rt[:, :, :], io["w_rt"].rearrange("(t p) m -> p t m", p=P)),
            (b_qk1[:, :], io["b_qk1"]), (gnw[:, :, :], io["gnw"]),
            (b_v1[:, :], io["b_v1"].partition_broadcast(P)),
            (b_pr[:, :], io["b_pr"].partition_broadcast(P)),
            (b_rt[:, :], io["b_rt"].partition_broadcast(P)),
        ]
        all_consts = 16 * len(consts)
        STACK0, STACKH, MAXROW = 6 * 16, 4 * 16, 2 * 16
        CONV = SLOTS - 1

        def slot(j):
            return j % SLOTS

        def stack_count(b, t, j):
            conv = STACK0 if slot(j) == CONV else 0
            heads = len(range(slot(j), NH, SLOTS))
            return b * (conv + heads * STACKH) + conv + (t + j // SLOTS + 1) * STACKH

        def maxrow_count(b, t, j):
            conv = MAXROW if slot(j) == CONV else 0
            heads = len(range(slot(j), NH, SLOTS))
            return b * (conv + heads * MAXROW) + conv + (t + j // SLOTS + 1) * MAXROW

        def conv_count(b, per_conv, per_head):
            return b * (per_conv + len(range(CONV, NH, SLOTS)) * per_head) + per_conv

        with nc.Block() as block:

            @block.sync
            def _(sp):
                for n, (dst, src) in enumerate(consts):
                    sp.dma_start(dst, src).then_inc(consts_in, 16)
                sp.dma_start(gamma[:, :], io["gamma"].partition_broadcast(P)).then_inc(stored, 16)
                with sp.Fori(0, B) as b:
                    sp.wait_ge(v_rt, b + 1)
                    sp.dma_start(x_c[:, :, :], io["x_c"][bass.ds(b, 1)].rearrange("o (t p) n -> p (o t) n", p=P)).then_inc(x_in, 16)
                    sp.dma_start(x_t[:, :, :], io["x_t"][bass.ds(b, 1)].rearrange("o (j p) c -> p (o j) c", p=P)).then_inc(x_in, 16)
                    sp.wait_ge(v_lo0, b + 1)
                    n_st, m_st = stk[CONV]
                    q_hi, q_lo, k_hi, k_lo = hi[0][0:D, :], lo[0][0:D, :], hi[0][D:2 * D, :], lo[0][D:2 * D, :]
                    for st, parts in ((n_st, (k_hi, k_lo, k_hi)), (m_st, (q_hi, q_hi, q_lo))):
                        for r, part in enumerate(parts):
                            sp.dma_start(raw(st[r * D:(r + 1) * D, :]), raw(part)).then_inc(stack_in[CONV], 16)
                    for it in range(4):
                        g, k = it // 2, it % 2
                        sp.wait_ge(v_lo, 4 * b + it + 1)
                        for part, s in enumerate((hi, lo)):
                            sp.dma_start(qk_scr[k, g * HG:(g + 1) * HG, part], raw(s[it % 2][:, :])).then_inc(spilled[g], 16)
                    for h in range(NH):
                        if h % HG == 0:
                            sp.wait_ge(spilled[h // HG], 64 * b + 64)
                        if h >= SLOTS:
                            sp.wait_ge(pe_exp, (b * UNITS + h - 1) * NB)
                        n_st, m_st = stk[slot(h)]
                        for dst, src in ((n_st[0:2 * D, :], qk_scr[0, h].rearrange("s d n -> (s d) n")),
                                         (n_st[2 * D:STACK, :], qk_scr[0, h, 0]),
                                         (m_st[0:D, :], qk_scr[1, h, 0]),
                                         (m_st[D:STACK, :], qk_scr[1, h].rearrange("s d n -> (s d) n"))):
                            sp.dma_start(raw(dst), src).then_inc(stack_in[slot(h)], 16)
                    sp.wait_ge(v_res1, 2 * b + 2)
                    sp.dma_start(io["t_scr"][bass.ds(b, 1)].rearrange("o (j p) c -> p (o j) c", p=P), res[:, :, :]).then_inc(stored, 16)
                    sp.wait_ge(v_l2, b + 1)
                    sp.dma_start(io["l_scr"][bass.ds(b, 1)].rearrange("o (j p) c -> p (o j) c", p=P), lnt[:, :, :]).then_inc(stored, 16)
                sp.wait_ge(stored, 16 + 32 * B)

            @block.gpsimd
            def _(pool):
                nc.gpsimd.memset(keep["zeros"][:, :], 0.0).then_inc(g_zero, 1)
                pool.wait_ge(g_zero, 1)
                nz = TILES // 3
                for t in range(3):
                    pool.dma_start(io["xs_scr"][t * nz * P:(t + 1) * nz * P, :].rearrange("(j p) c -> p j c", p=P),
                                   keep["zeros"][:, :].rearrange("p (o c) -> p o c", o=1).to_broadcast([P, nz, C])
                                   ).then_inc(sems["zeroed"], 16)
                pool.wait_ge(x_in, 32)
                for e in range(E):
                    pool.dma_start(keep["w1"][:, e], io["w1"][e].rearrange("(t p) m -> p t m", p=P)).then_inc(w1_in, 16)
                pool.wait_ge(consts_in, all_consts)
                with pool.Fori(0, B) as b:
                    pool.wait_ge(v_ln, b + 1)
                    nc.gpsimd.tensor_tensor(res[:, :, :], res[:, :, :], lnt[:, :, :], ALU.add).then_inc(g_res, 1)
                    pool.wait_ge(g_res, 2 * b + 1)
                    nc.gpsimd.tensor_tensor(res[:, :, :], res[:, :, :],
                                            b_pr[:, :].rearrange("p (o c) -> p o c", o=1).to_broadcast([P, NB, C]),
                                            ALU.add).then_inc(g_res, 1)

            @block.scalar
            def _(act):
                act.wait_ge(consts_in, all_consts)
                with act.Fori(0, B) as b:
                    def max_rows(u, s):
                        act.wait_ge(pe_maxt, b * UNITS + u + 1)
                        nc.scalar.activation(mrow[:, :], ps_t[0:2 * NB, 0:P], ACT.Copy).then_inc(a_mrow, 1)
                        act.wait_ge(a_mrow, b * UNITS + u + 1)
                        for part in range(2):
                            act.dma_start(raw(stk[s][0][STACK + part:STACK + part + 1, :]),
                                          raw(mrow[part * NB:(part + 1) * NB, :])).then_inc(maxrow_in[s], 16)

                    def exponentials(u, scale, free=None):
                        for m in range(NB):
                            act.wait_ge(pe_exp, (b * UNITS + u) * NB + m + 1)
                            if free is not None:
                                act.wait_ge(pe_pv, free + m)
                            nc.scalar.activation(expd[:, m, :], flat(ps_e[m % 2]), ACT.Exp, scale=scale).then_inc(a_exp, 1)

                    act.wait_ge(pe_qk0, b + 1)
                    nc.scalar.activation(hi[0][0:2 * D, :], flat(ps_e[0][0:2 * D]), ACT.Copy).then_inc(a_hi0, 1)
                    for t in range(2):
                        act.wait_ge(pe_v0, 2 * b + t + 1)
                        nc.scalar.activation(val[:, 4 * t:4 * t + 4, 0:C],
                                             flat((ps_e[1], ps_m)[t]).rearrange("p (j c) -> p j c", c=C),
                                             ACT.Copy).then_inc(a_v0, 1)
                    max_rows(0, CONV)
                    exponentials(0, 1.0)
                    act.wait_ge(v_gab, b + 1)
                    for t in range(CT):
                        nc.scalar.activation(h_c[:, t, :], flat(ps_e[t]), ACT.Identity,
                                             scale=gab[:, 0, t:t + 1], bias=gab[:, 1, t:t + 1]).then_inc(a_h, 1)
                    for it in range(4):
                        act.wait_ge(pe_qk1, 4 * b + it + 1)
                        if it >= 2:
                            act.wait_ge(spilled[0], 64 * b + 64)
                        nc.scalar.activation(hi[it % 2][:, :], flat(ps_e[it % 2]), ACT.Identity,
                                             bias=b_qk1[:, it:it + 1]).then_inc(a_hi, 1)

                    def head_values(t, j):
                        nc.scalar.activation(vh[slot(j)][:, :, :], val[:, :, bass.ds((t * SLOTS + j) * D, D)],
                                             ACT.Copy).then_inc(a_vh, 1)

                    def head(t, j, first=False, last=False):
                        h = t * SLOTS + j
                        exponentials(h + 1, SCALE, None if first else (b * NH + h - 1) * NB + 1)
                        if not last:
                            max_rows(h + 2, slot(j + 1))
                            head_values(t, j + 1)
                        act.wait_ge(pe_pv, (b * NH + h + 1) * NB)
                        if not first:
                            act.wait_ge(pe_ot, b * NH + h)
                        nc.scalar.activation(osum[:, :], ps_o[:, :], ACT.Copy).then_inc(a_o, 1)

                    act.wait_ge(v_v1, 2 * b + 2)
                    head_values(0, 0)
                    max_rows(1, slot(0))
                    head(0, 0, first=True)
                    with act.Fori(0, 2) as t:
                        for j in range(1, SLOTS + 1):
                            head(t, j)
                    head(2, 1, last=True)
                    act.wait_ge(pe_vt, 2 * b + 1)
                    nc.scalar.activation(vals_c[:, 0, :], flat(ps_e[0]), ACT.Copy).then_inc(a_vt, 1)
                    act.wait_ge(pe_l2t, 2 * b + 1)
                    nc.scalar.activation(l2_c[:, 0, :], flat(ps_e[0]), ACT.Copy).then_inc(a_l2t, 1)

            @block.tensor
            def _(pe):
                pe.wait_ge(consts_in, all_consts)
                pe.wait_ge(v_set, 1)
                with pe.Fori(0, B) as b:
                    E0 = b * UNITS * NB

                    def maxima(s, nb):
                        n_st, m_st = stk[s]
                        for half in range(2):
                            last = nc.tensor.matmul(ps_m[:, half, :], n_st[0:STACK, nb * P:(nb + 1) * P],
                                                    m_st[0:STACK, half * HALF:(half + 1) * HALF], start=True, stop=True)
                        last.then_inc(pe_max, 1)

                    def max_turn(u):
                        pe.wait_ge(v_split, b * UNITS + u + 1)
                        nc.tensor.transpose(ps_t[0:2 * NB, 0:P], raw(msplit[:, :]), ident[:, :]).then_inc(pe_maxt, 1)

                    def scores(s, m):
                        n_st, m_st = stk[s]
                        for half in range(2):
                            last = nc.tensor.matmul(ps_e[m % 2][:, half, :], m_st[0:ROWS, m * P:(m + 1) * P],
                                                    n_st[0:ROWS, half * HALF:(half + 1) * HALF], start=True, stop=True)
                        last.then_inc(pe_exp, 1)

                    def turn(dst, src, t):
                        for j in range(NB):
                            last = nc.tensor.transpose(dst[:, j // 4, j % 4 * P:(j % 4 + 1) * P],
                                                       src[:, j, t * P:(t + 1) * P], ident[:, :])
                        return last

                    def by_token(dst, src, w, q):
                        for j in range(4):
                            for t in range(CT):
                                last = nc.tensor.matmul(dst[:, j // 2, j % 2 * C:(j % 2 + 1) * C],
                                                        src[:, t, (4 * q + j) * P:(4 * q + j + 1) * P], w[:, t, :],
                                                        start=(t == 0), stop=(t == CT - 1))
                        return last

                    pe.wait_ge(x_in, 32 * b + 32)
                    pe.wait_ge(v_rt, b + 1)
                    for half in range(2):
                        for t in range(CT):
                            last = nc.tensor.matmul(ps_e[0][0:2 * D, half, :], w_qk0[:, t, :],
                                                    x_c[:, t, half * HALF:(half + 1) * HALF], start=(t == 0), stop=(t == CT - 1))
                    last.then_inc(pe_qk0, 1)
                    by_token(ps_e[1], x_c, w_v0, 0).then_inc(pe_v0, 1)
                    by_token(ps_m, x_c, w_v0, 1).then_inc(pe_v0, 1)
                    pe.wait_ge(stack_in[CONV], conv_count(b, STACK0, STACKH))
                    pe.wait_ge(a_v0, 2 * b + 2)
                    for nb in range(NB):
                        if nb:
                            pe.wait_ge(v_max, E0 + nb)
                        maxima(CONV, nb)
                    max_turn(0)
                    pe.wait_ge(maxrow_in[CONV], conv_count(b, MAXROW, MAXROW))
                    for m in range(NB):
                        if m >= 2:
                            pe.wait_ge(a_exp, E0 + m - 1)
                        scores(CONV, m)
                    pe.wait_ge(a_exp, E0 + NB)
                    for j in range(NB):
                        if j >= 2:
                            pe.wait_ge(v_res0, NB * b + j - 1)
                        for m in range(NB):
                            last = nc.tensor.matmul(ps_m[:, j % 2, 0:C + 1], expd[:, m, j * P:(j + 1) * P],
                                                    val[:, m, :], start=(m == 0), stop=(m == NB - 1))
                        last.then_inc(pe_pv0, 1)
                    pe.wait_ge(v_ln, b + 1)
                    for t in range(CT):
                        turn(ps_e[t], lnt, t).then_inc(pe_lnt, 1)
                    pe.wait_ge(v_gst, 2 * b + 2)
                    nc.tensor.matmul(ps_o[:, 0:CT], gmat[:, :], mvc[:, :, 0], start=True, stop=True).then_inc(pe_gn, 1)
                    pe.wait_ge(v_gdev, b + 1)
                    nc.tensor.matmul(ps_o[:, 8:8 + CT], gmat[:, :], gw[:, :], start=True, stop=True).then_inc(pe_gn, 1)
                    pe.wait_ge(a_h, 2 * b + 2)
                    for q in range(2):
                        for it in (2 * q, 2 * q + 1):
                            if it >= 2:
                                pe.wait_ge(v_lo, 4 * b + it - 1)
                            for half in range(2):
                                for t in range(CT):
                                    last = nc.tensor.matmul(ps_e[it % 2][:, half, :], w_qk1[:, t, it, :],
                                                            h_c[:, t, half * HALF:(half + 1) * HALF],
                                                            start=(t == 0), stop=(t == CT - 1))
                            last.then_inc(pe_qk1, 1)
                        if q:
                            pe.wait_ge(v_v1, 2 * b + 1)
                        by_token(ps_m, h_c, w_v1, q).then_inc(pe_v1, 1)
                    pe.wait_ge(stack_in[slot(0)], stack_count(b, 0, 0))
                    pe.wait_ge(v_v1, 2 * b + 2)
                    for nb in range(NB):
                        if nb:
                            pe.wait_ge(v_max, E0 + NB + nb)
                        maxima(slot(0), nb)
                    max_turn(1)

                    def outputs(h):
                        pe.wait_ge(a_o, b * NH + h + 1)
                        for q in range(4):
                            last = nc.tensor.transpose(ps_t[:, q * P:(q + 1) * P], osum[:, q * P:(q + 1) * P], ident[:, :])
                        last.then_inc(pe_ot, 1)

                    def head(t, j, first=False, last=False):
                        h = t * SLOTS + j
                        s, s_next = slot(j), slot(j + 1)
                        for step in range(NB + LAG):
                            if step == 0:
                                pe.wait_ge(maxrow_in[s], maxrow_count(b, t, j))
                                if first:
                                    pe.wait_ge(v_lo, 4 * b + 4)
                                if not last:
                                    pe.wait_ge(stack_in[s_next], stack_count(b, t, j + 1))
                            if step < NB:
                                pe.wait_ge(a_exp, E0 + (h + 1) * NB + (step - 1))
                                scores(s, step)
                                if not last:
                                    pe.wait_ge(v_max, E0 + (h + 2) * NB + step)
                                    maxima(s_next, step)
                            if step == 2 and not first:
                                outputs(h - 1)
                            if step == NB + 2 and not last:
                                if not first:
                                    pe.wait_ge(v_norm, b * NH + h)
                                max_turn(h + 2)
                            m = step - LAG
                            if m < 0:
                                continue
                            pe.wait_ge(a_exp, E0 + (h + 1) * NB + (m + 1))
                            if m == 0:
                                pe.wait_ge(a_vh, b * NH + h + 1)
                                if not first:
                                    pe.wait_ge(a_o, b * NH + h)
                            for half in range(2):
                                for k, w in enumerate((vh[s][:, m, :], ones[:, :])):
                                    q = (2 * half + k) * D
                                    mm = nc.tensor.matmul(ps_o[q:q + D, :], w, expd[:, m, half * HALF:(half + 1) * HALF],
                                                          start=(m == 0), stop=(m == NB - 1))
                            mm.then_inc(pe_pv, 1)

                    head(0, 0, first=True)
                    with pe.Fori(0, 2) as t:
                        for j in range(1, SLOTS + 1):
                            head(t, j)
                    head(2, 1, last=True)
                    pe.wait_ge(v_norm, b * NH + NH - 1)
                    outputs(NH - 1)
                    pe.wait_ge(v_norm, b * NH + NH)
                    for t in range(CT):
                        turn(ps_e[t], vals_t, t).then_inc(pe_vt, 1)
                    pe.wait_ge(a_vt, b + 1)
                    pe.wait_ge(v_vt, b + 1)
                    by_token(ps_m, vals_c, w_pr, 0).then_inc(pe_pr, 1)
                    by_token(ps_e[0], vals_c, w_pr, 1).then_inc(pe_pr, 1)
                    pe.wait_ge(v_l2, b + 1)
                    for t in range(CT):
                        turn(ps_e[t], lnt, t).then_inc(pe_l2t, 1)
                    pe.wait_ge(a_l2t, b + 1)
                    pe.wait_ge(v_l2t, b + 1)
                    for j in range(NB):
                        for t in range(CT):
                            last = nc.tensor.matmul(ps_o[:, j * E:(j + 1) * E], l2_c[:, t, j * P:(j + 1) * P], w_rt[:, t, :],
                                                    start=(t == 0), stop=(t == CT - 1))
                    last.then_inc(pe_rt, 1)

            @block.vector
            def _(dve):
                for s in range(SLOTS):
                    nc.vector.memset(raw(stk[s][1][STACK:ROWS, :]), 1.0)
                nc.vector.memset(val[:, :, C:C + 1], 1.0)
                nc.vector.memset(ones[:, :], 1.0).then_inc(v_set, 1)
                dve.wait_ge(consts_in, all_consts)
                nc.vector.memset(tmp[:, :], 0.0).then_inc(v_rt, 1)
                dve.wait_ge(v_rt, 1)
                with dve.Fori(0, B) as b:
                    st = Steps(dve, v_step, b * V_STEPS)

                    def block_max(u, nb):
                        dve.wait_ge(pe_max, (b * UNITS + u) * NB + nb + 1)
                        nc.vector.tensor_reduce(nmax[:, nb:nb + 1], ps_m[:, :, :], AX.XY, ALU.max, negate=True).then_inc(v_max, 1)

                    def split_max(u):
                        dve.wait_ge(v_max, (b * UNITS + u + 1) * NB)
                        nc.vector.tensor_copy(msplit[:, 0:NB], nmax[:, :]).then_inc(v_mh, 1)
                        dve.wait_ge(v_mh, b * UNITS + u + 1)
                        nc.vector.tensor_tensor(msplit[:, NB:2 * NB], nmax[:, :], raw(msplit[:, 0:NB]),
                                                ALU.subtract).then_inc(v_split, 1)

                    def layer_norm(done):
                        st.did(nc.vector.tensor_scalar(var[:, :], mv[:, :, 1], LN_EPS, None, ALU.add))
                        st.wait()
                        rsqrt(nc, st, rstd[:, :], var[:, :], tmp[:, :])
                        for j in range(NB):
                            last = nc.vector.tensor_scalar(lnt[:, j, :], res[:, j, :], mv[:, j, 0:1], rstd[:, j:j + 1],
                                                           ALU.subtract, ALU.mult)
                        last.then_inc(done, 1)

                    def moments():
                        st.wait()
                        nc.vector.memset(pause[:, :], 0.0)
                        for j in range(NB):
                            st.did(nc.vector.bn_aggr(mv[:, j, :], bst[:, j, :]))

                    dve.wait_ge(a_hi0, b + 1)
                    nc.vector.tensor_tensor(lo[0][0:2 * D, :], flat(ps_e[0][0:2 * D]), raw(hi[0][0:2 * D, :]),
                                            ALU.subtract).then_inc(v_lo0, 1)
                    for nb in range(NB):
                        block_max(0, nb)
                    split_max(0)
                    dve.wait_ge(stored, 32 * b + 16)
                    for j in range(NB):
                        dve.wait_ge(pe_pv0, NB * b + j + 1)
                        st.did(nc.vector.reciprocal(rc[:, :], ps_m[:, j % 2, C:C + 1]))
                        st.wait()
                        st.did(nc.vector.tensor_tensor(rg[:, :], rc[:, :], gamma[:, :], ALU.mult))
                        st.wait()
                        nc.vector.scalar_tensor_tensor(res[:, j, :], ps_m[:, j % 2, 0:C], rg[:, :], x_t[:, j, :],
                                                       ALU.mult, ALU.add).then_inc(v_res0, 1)
                        dve.wait_ge(v_res0, NB * b + j + 1)
                        st.did(nc.vector.bn_stats(bst[:, j, :], res[:, j, :]))
                    moments()
                    st.wait()
                    layer_norm(v_ln)
                    for t in range(CT):
                        dve.wait_ge(pe_lnt, 2 * b + t + 1)
                        for half in range(2):
                            st.did(nc.vector.bn_stats(bst[:, 2 * t + half, :], ps_e[t][:, half, :]))
                    st.wait()
                    nc.vector.memset(pause[:, :], 0.0)
                    for t in range(CT):
                        nc.vector.bn_aggr(mvc[:, t, :], bst[:, 2 * t:2 * t + 2, :].rearrange("p a s -> p (a s)")).then_inc(v_gst, 1)
                    dve.wait_ge(v_gst, 2 * b + 2)
                    dve.wait_ge(pe_gn, 2 * b + 1)
                    st.did(nc.vector.tensor_copy(mg[:, :], ps_o[:, 0:CT]))
                    st.wait()
                    nc.vector.tensor_tensor(gdev[:, :], mvc[:, :, 0], mg[:, :], ALU.subtract).then_inc(v_gd1, 1)
                    dve.wait_ge(v_gd1, b + 1)
                    st.did(nc.vector.tensor_tensor(gdev[:, :], gdev[:, :], gdev[:, :], ALU.mult))
                    st.wait()
                    nc.vector.tensor_tensor(gw[:, :], gdev[:, :], mvc[:, :, 1], ALU.add).then_inc(v_gdev, 1)
                    dve.wait_ge(pe_gn, 2 * b + 2)
                    st.did(nc.vector.tensor_scalar(var[:, 0:CT], ps_o[:, 8:8 + CT], GN_EPS, None, ALU.add))
                    st.wait()
                    rsqrt(nc, st, rstd[:, 0:CT], var[:, 0:CT], tmp[:, 0:CT])
                    st.did(nc.vector.tensor_tensor(gab[:, 0, :], rstd[:, 0:CT], gnw[:, :, 0], ALU.mult))
                    st.wait()
                    st.did(nc.vector.tensor_tensor(tmp[:, 0:CT], gab[:, 0, :], mg[:, :], ALU.mult))
                    st.wait()
                    nc.vector.tensor_tensor(gab[:, 1, :], gnw[:, :, 1], tmp[:, 0:CT], ALU.subtract).then_inc(v_gab, 1)
                    for q in range(2):
                        for it in (2 * q, 2 * q + 1):
                            dve.wait_ge(a_hi, 4 * b + it + 1)
                            if it >= 2:
                                dve.wait_ge(spilled[0], 64 * b + 64)
                            nc.vector.scalar_tensor_tensor(lo[it % 2][:, :], flat(ps_e[it % 2]), b_qk1[:, it:it + 1],
                                                           raw(hi[it % 2][:, :]), ALU.add, ALU.subtract).then_inc(v_lo, 1)
                        dve.wait_ge(pe_v1, 2 * b + q + 1)
                        nc.vector.tensor_tensor(val[:, 4 * q:4 * q + 4, 0:C], flat(ps_m).rearrange("p (j c) -> p j c", c=C),
                                                b_v1[:, :].rearrange("p (o c) -> p o c", o=1).to_broadcast([P, 4, C]),
                                                ALU.add).then_inc(v_v1, 1)
                    def norm(h, col):
                        dve.wait_ge(pe_ot, b * NH + h + 1)
                        turned = ps_t[:, :].rearrange("p (t a k d) -> p a t k d", t=4, a=2, k=2)
                        nc.vector.reciprocal(rc8[:, :, :], turned[:, :, :, 1, 0]).then_inc(v_rc, 1)
                        dve.wait_ge(v_rc, b * NH + h + 1)
                        nc.vector.tensor_tensor(vals_t[:, :, col].rearrange("p (a t) d -> p a t d", a=2),
                                                turned[:, :, :, 0, :],
                                                rc8[:, :, :].rearrange("p a (t o) -> p a t o", o=1).to_broadcast([P, 2, 4, D]),
                                                ALU.mult).then_inc(v_norm, 1)

                    for nb in range(NB):
                        block_max(1, nb)
                    split_max(1)
                    for nb in range(NB):
                        block_max(2, nb)
                    split_max(2)
                    with dve.Fori(1, NH - 1) as h:
                        for nb in range(NB):
                            block_max(h + 2, nb)
                            if nb == 4:
                                norm(h - 1, bass.ds((h - 1) * D, D))
                        split_max(h + 2)
                    norm(NH - 2, slice((NH - 2) * D, (NH - 1) * D))
                    norm(NH - 1, slice((NH - 1) * D, NH * D))
                    dve.wait_ge(pe_vt, 2 * b + 2)
                    nc.vector.tensor_copy(vals_c[:, 1, :], flat(ps_e[1])).then_inc(v_vt, 1)
                    dve.wait_ge(g_res, 2 * b + 2)
                    for q in range(2):
                        dve.wait_ge(pe_pr, 2 * b + q + 1)
                        nc.vector.tensor_tensor(res[:, 4 * q:4 * q + 4, :],
                                                flat((ps_m, ps_e[0])[q]).rearrange("p (j c) -> p j c", c=C),
                                                res[:, 4 * q:4 * q + 4, :], ALU.add).then_inc(v_res1, 1)
                        dve.wait_ge(v_res1, 2 * b + q + 1)
                        for j in range(4 * q, 4 * q + 4):
                            st.did(nc.vector.bn_stats(bst[:, j, :], res[:, j, :]))
                    moments()
                    st.wait()
                    layer_norm(v_l2)
                    dve.wait_ge(pe_l2t, 2 * b + 2)
                    nc.vector.tensor_copy(l2_c[:, 1, :], flat(ps_e[1])).then_inc(v_l2t, 1)
                    dve.wait_ge(pe_rt, b + 1)
                    nc.vector.tensor_tensor(keep["logits"][:, bass.ds(b * NB, NB), :],
                                            ps_o[:, 0:NB * E].rearrange("p (j e) -> p j e", e=E),
                                            b_rt[:, :].rearrange("p (o e) -> p o e", o=1).to_broadcast([P, NB, E]),
                                            ALU.add).then_inc(v_rt, 1)
                    assert st.n == V_STEPS, st.n


def expert_phase(nc, io, keep, sems):
    with ExitStack() as ctx:
        def sb(name, shape, dt=F32):
            return ctx.enter_context(nc.sbuf_tensor(name, shape, dt))

        def ps(name, shape):
            return ctx.enter_context(nc.psum_tensor(name, shape, F32))

        def sem(name):
            return ctx.enter_context(nc.semaphore(name))

        LOADS = 4
        AHEAD = 3
        w1, logits = keep["w1"], keep["logits"]
        w2 = sb("w2", [P, E, KC, C])
        ident, before, allones = sb("ident2", [P, P]), sb("before", [P, P]), sb("allones", [P, P])
        expert_rev, expert_of = sb("expert_rev", [P, E]), sb("expert_of", [P, 1])
        steps128, tile_no = sb("steps128", [P, TB]), sb("tile_no", [P, TILES])
        bias, bias_hi = sb("bias", [2 * E, H + C]), sb("bias_hi", [2 * E, H + C], F32R)
        bias_mask = sb("bias_mask", [2 * E, 1])
        bias_st = sb("bias_st", [2 * E, H + C], F32R)
        onehot, work, work2 = sb("onehot", [P, TB, E]), sb("work", [P, TB, E]), sb("work2", [P, TB, E])
        total, prior = sb("total", [P, TB, E]), [sb(f"prior{k}", [P, TB, E]) for k in range(2)]
        top = sb("top", [P, TB])
        count, ntile, end = sb("count", [P, E]), sb("ntile", [P, E]), sb("end", [P, E])
        base = [sb(f"base{k}", [P, E]) for k in range(2)]
        over, tiled = sb("over", [P, E, TB]), sb("tiled", [P, TILES, E])
        pos_f, pos = sb("pos_f", [P, TB]), sb("pos", [P, TB], I32)
        texp, texp_i = sb("texp", [P, TILES]), sb("texp_i", [P, TILES], I32)
        pick_all, pick = sb("pick_all", [2 * E, TILES]), [sb(f"pick{k}", [2 * E, P], F32R) for k in (1, 2)]
        rows = sb("rows", [P, NB, C])
        xs, xs_c = sb("xs", [P, C]), sb("xs_c", [P, CT, P])
        hid, hid_c, ys = sb("hid", [P, H]), sb("hid_c", [P, KC, P]), sb("ys", [P, C])
        back = [sb(f"back{k}", [P, C]) for k in range(LOADS)]
        tres = [sb(f"tres{k}", [P, C]) for k in range(LOADS)]

        ps_h, ps_t = ps("ps_h", [P, 2, HALF]), ps("ps_ht", [P, 2, HALF])
        ps_x, ps_y = ps("ps_x", [P, HALF]), ps("ps_y", [P, HALF])
        ps_r = ps("ps_r", [P, 2, HALF])

        consts_in, bias_in, w2_in = sem("consts_in2"), sem("bias_in"), sem("w2_in")
        rows_in, scattered, xs_in = sem("rows_in"), sem("scattered"), sem("xs_in")
        ys_out, out_done = sem("ys_out"), sem("out_done")
        tres_in = [sem(f"tres_in{k}") for k in range(LOADS)]
        back_in = [sem(f"back_in{k}") for k in range(LOADS)]
        out_free = [sem(f"out_free{k}") for k in range(LOADS)]
        v_step, v_onehot, v_pos, v_pick_all, v_bias = sem("v_step2"), sem("v_onehot"), sem("v_pos"), sem("v_pick_all"), sem("v_bias")
        v_xs, v_hid, v_sum = sem("v_xs"), sem("v_hid"), sem("v_sum")
        v_pick = [sem(f"v_pick{k}") for k in (1, 2)]
        pe_count, pe_xs, pe_hid, pe_hidt, pe_ys = sem("pe_count"), sem("pe_xs"), sem("pe_hid"), sem("pe_hidt"), sem("pe_ys")
        a_gelu, a_ys = sem("a_gelu"), sem("a_ys")

        consts = [(ident, "ident"), (before, "before"), (allones, "allones"), (expert_rev, "expert_rev"),
                  (expert_of, "expert_of"), (steps128, "steps128"), (tile_no, "tile_no")]
        all_consts = 16 * len(consts)

        def row_block(dram, i):
            return dram[i // NB, i % NB * P:(i % NB + 1) * P, :]

        with nc.Block() as block:

            @block.sync
            def _(sp):
                for dst, name in consts:
                    sp.dma_start(dst[:, :], io[name]).then_inc(consts_in, 16)
                for dup in range(2):
                    sp.dma_start(bias[dup * E:(dup + 1) * E, 0:H], io["b1"]).then_inc(bias_in, 16)
                    sp.dma_start(bias[dup * E:(dup + 1) * E, H:H + C], io["b2"]).then_inc(bias_in, 16)
                sp.dma_start(bias_mask[:, :], io["bias_mask"]).then_inc(bias_in, 16)
                for b in range(B):
                    if b:
                        sp.wait_ge(scattered, 16 * NB * b)
                    sp.dma_start(rows[:, :, :], io["l_scr"][b].rearrange("(j p) c -> p j c", p=P)).then_inc(rows_in, 16)
                sp.wait_ge(scattered, 16 * TB)
                def load(i):
                    sp.dma_start(xs[:, :], io["xs_scr"][bass.ds(i * P, P), :]).then_inc(xs_in, 16)

                def store(i):
                    sp.wait_ge(a_ys, i + 1)
                    sp.dma_start(io["ys_scr"][bass.ds(i * P, P), :], ys[:, :]).then_inc(ys_out, 16)

                load(0)
                for i in range(1, AHEAD):
                    sp.wait_ge(pe_xs, i)
                    load(i)
                with sp.Fori(0, TILES - AHEAD) as i:
                    sp.wait_ge(pe_xs, i + AHEAD)
                    load(i + AHEAD)
                    store(i)
                for i in range(TILES - AHEAD, TILES):
                    store(i)
                for i in range(TB):
                    k = i % LOADS
                    if i >= LOADS:
                        sp.wait_ge(v_sum, i - LOADS + 1)
                    sp.dma_start(tres[k][:, :], row_block(io["t_scr"], i)).then_inc(tres_in[k], 16)

            @block.gpsimd
            def _(pool):
                pool.wait_ge(sems["zeroed"], 48)
                pool.wait_ge(v_pos, 1)
                for i in range(TB):
                    pool.wait_ge(rows_in, 16 * (i // NB + 1))
                    pool.indirect_dma_start(io["xs_scr"][:, :], bass.IndirectOffsetOnAxis(ap=pos[:, i:i + 1], axis=0),
                                            rows[:, i % NB, :], None).then_inc(scattered, 16)
                pool.wait_ge(ys_out, 16 * TILES)
                for i in range(TB):
                    k = i % LOADS
                    if i >= LOADS:
                        pool.wait_ge(out_free[k], 16 * (i // LOADS))
                    pool.indirect_dma_start(back[k][:, :], None, io["ys_scr"][:, :],
                                            bass.IndirectOffsetOnAxis(ap=pos[:, i:i + 1], axis=0)).then_inc(back_in[k], 16)

            @block.vector
            def _(dve):
                st = Steps(dve, v_step)

                def step(ins):
                    st.did(ins)
                    st.wait()

                over_e = lambda ap, n: ap.rearrange("p (t o) -> p t o", o=1).to_broadcast([P, n, E])
                over_t = lambda ap, n: ap.rearrange("p (o e) -> p o e", o=1).to_broadcast([P, n, E])
                dve.wait_ge(consts_in, all_consts)
                step(nc.vector.tensor_reduce(top[:, :], logits[:, :, :], AX.X, ALU.max))
                step(nc.vector.tensor_tensor(work[:, :, :], logits[:, :, :], over_e(top[:, :], TB), ALU.is_ge))
                step(nc.vector.tensor_tensor(work2[:, :, :], work[:, :, :], over_t(expert_rev[:, :], TB), ALU.mult))
                step(nc.vector.tensor_reduce(top[:, :], work2[:, :, :], AX.X, ALU.max))
                nc.vector.tensor_tensor(onehot[:, :, :], work2[:, :, :], over_e(top[:, :], TB), ALU.is_equal).then_inc(v_onehot, 1)
                dve.wait_ge(pe_count, 1)
                step(nc.vector.tensor_copy(total[:, :, :], ps_r[:, 1, 0:TB * E].rearrange("p (t e) -> p t e", e=E)))
                st.did(nc.vector.memset(prior[0][:, 0:1, :], 0.0))
                step(nc.vector.tensor_copy(prior[0][:, 1:TB, :], total[:, 0:TB - 1, :]))
                a, shift = 0, 1
                while shift < TB:
                    st.did(nc.vector.tensor_copy(prior[1 - a][:, 0:shift, :], prior[a][:, 0:shift, :]))
                    step(nc.vector.tensor_tensor(prior[1 - a][:, shift:TB, :], prior[a][:, shift:TB, :],
                                                 prior[a][:, 0:TB - shift, :], ALU.add))
                    a, shift = 1 - a, 2 * shift
                step(nc.vector.tensor_tensor(count[:, :], prior[a][:, TB - 1, :], total[:, TB - 1, :], ALU.add))
                step(nc.vector.tensor_tensor(over[:, :, :], count[:, :].rearrange("p (e o) -> p e o", o=1).to_broadcast([P, E, TB]),
                                             steps128[:, :].rearrange("p (o t) -> p o t", o=1).to_broadcast([P, E, TB]), ALU.is_gt))
                step(nc.vector.tensor_reduce(ntile[:, :], over[:, :, :], AX.X, ALU.add))
                st.did(nc.vector.memset(base[0][:, 0:1], 0.0))
                step(nc.vector.tensor_copy(base[0][:, 1:E], ntile[:, 0:E - 1]))
                c, shift = 0, 1
                while shift < E:
                    st.did(nc.vector.tensor_copy(base[1 - c][:, 0:shift], base[c][:, 0:shift]))
                    step(nc.vector.tensor_tensor(base[1 - c][:, shift:E], base[c][:, shift:E], base[c][:, 0:E - shift], ALU.add))
                    c, shift = 1 - c, 2 * shift
                step(nc.vector.tensor_scalar(end[:, :], base[c][:, :], float(P), None, ALU.mult))
                step(nc.vector.tensor_tensor(work[:, :, :], ps_r[:, 0, 0:TB * E].rearrange("p (t e) -> p t e", e=E),
                                             prior[a][:, :, :], ALU.add))
                step(nc.vector.tensor_tensor(work2[:, :, :], work[:, :, :], over_t(end[:, :], TB), ALU.add))
                step(nc.vector.tensor_tensor(work[:, :, :], work2[:, :, :], onehot[:, :, :], ALU.mult))
                step(nc.vector.tensor_reduce(pos_f[:, :], work[:, :, :], AX.X, ALU.add))
                nc.vector.tensor_copy(pos[:, :], pos_f[:, :]).then_inc(v_pos, 1)
                step(nc.vector.tensor_tensor(end[:, :], base[c][:, :], ntile[:, :], ALU.add))
                step(nc.vector.tensor_tensor(tiled[:, :, :], over_e(tile_no[:, :], TILES), over_t(end[:, :], TILES), ALU.is_ge))
                step(nc.vector.tensor_reduce(texp[:, :], tiled[:, :, :], AX.X, ALU.add))
                step(nc.vector.tensor_scalar(texp[:, :], texp[:, :], float(E - 1), None, ALU.min))
                st.did(nc.vector.tensor_scalar(pick_all[:, :], texp[0:2 * E, :], expert_of[0:2 * E, :], None, ALU.is_equal))
                nc.vector.tensor_copy(texp_i[:, :], texp[:, :]).then_inc(v_pick_all, 1)
                st.wait()
                dve.wait_ge(bias_in, 80)
                step(nc.vector.tensor_copy(bias_hi[:, :], bias[:, :]))
                nc.vector.scalar_tensor_tensor(bias_st[:, :], raw(bias_hi[:, :]), bias_mask[:, :], bias[:, :],
                                               ALU.mult, ALU.add).then_inc(v_bias, 1)

                def picked(k, i):
                    nc.vector.tensor_copy(pick[k][:, :], pick_all[:, bass.ds(i, 1)].to_broadcast([2 * E, P])).then_inc(v_pick[k], 1)

                def tokens(i):
                    dve.wait_ge(pe_xs, i + 1)
                    nc.vector.tensor_copy(xs_c[:, :, :], ps_x[:, 0:C].rearrange("p (t n) -> p t n", t=CT)).then_inc(v_xs, 1)

                def tile(i, first=False, ahead=True):
                    dve.wait_ge(pe_hidt, i + 1)
                    if not first:
                        dve.wait_ge(pe_ys, i)
                    nc.vector.tensor_copy(hid_c[:, :, :], flat(ps_t).rearrange("p (k n) -> p k n", n=P)).then_inc(v_hid, 1)
                    picked(1, i)
                    if ahead:
                        dve.wait_ge(pe_hid, i + 2)
                        picked(0, i + 2)
                        tokens(i + 2)

                dve.wait_ge(v_pick_all, 1)
                picked(0, 0)
                tokens(0)
                dve.wait_ge(pe_hid, 1)
                picked(0, 1)
                tokens(1)
                tile(0, first=True)
                with dve.Fori(1, TILES - 2) as i:
                    tile(i)
                tile(TILES - 2, ahead=False)
                tile(TILES - 1, ahead=False)
                for i in range(TB):
                    k = i % LOADS
                    dve.wait_ge(back_in[k], 16 * (i // LOADS + 1))
                    dve.wait_ge(tres_in[k], 16 * (i // LOADS + 1))
                    nc.vector.tensor_tensor(back[k][:, :], back[k][:, :], tres[k][:, :], ALU.add).then_inc(v_sum, 1)

            @block.tensor
            def _(pe):
                pe.wait_ge(consts_in, all_consts)
                pe.wait_ge(v_onehot, 1)
                oh = onehot[:, :, :].rearrange("p t e -> p (t e)")
                nc.tensor.matmul(ps_r[:, 0, 0:TB * E], before[:, :], oh, start=True, stop=True)
                nc.tensor.matmul(ps_r[:, 1, 0:TB * E], allones[:, :], oh, start=True, stop=True).then_inc(pe_count, 1)
                pe.wait_ge(sems["w1_in"], 16 * E)
                pe.wait_ge(w2_in, 16 * E)
                pe.wait_ge(v_bias, 1)
                pe.wait_ge(v_pick_all, 1)

                def tokens(i):
                    pe.wait_ge(xs_in, 16 * i + 16)
                    for t in range(CT):
                        last = nc.tensor.transpose(ps_x[:, t * P:(t + 1) * P], xs[:, t * P:(t + 1) * P], ident[:, :])
                    last.then_inc(pe_xs, 1)

                def first_layer(i):
                    e = pe.value_load(texp_i[0:1, bass.ds(i, 1)], min_val=0, max_val=E - 1)
                    pe.wait_ge(v_pick[0], i + 1)
                    pe.wait_ge(v_xs, i + 1)
                    for half in range(2):
                        cols = slice(half * HALF, (half + 1) * HALF)
                        nc.tensor.matmul(ps_h[:, half, :], pick[0][:, :], bias_st[:, cols], start=True, stop=False)
                        for t in range(CT):
                            last = nc.tensor.matmul(ps_h[:, half, :], xs_c[:, t, :],
                                                    w1[:, bass.ds(e, 1), t, cols].rearrange("p o n -> p (o n)"),
                                                    start=False, stop=(t == CT - 1))
                    last.then_inc(pe_hid, 1)

                def turn_hidden(i):
                    pe.wait_ge(a_gelu, i + 1)
                    for k in range(KC):
                        last = nc.tensor.transpose(ps_t[:, k // 4, k % 4 * P:(k % 4 + 1) * P], hid[:, k * P:(k + 1) * P], ident[:, :])
                    last.then_inc(pe_hidt, 1)

                def second_layer(i, first=False):
                    e = pe.value_load(texp_i[0:1, bass.ds(i, 1)], min_val=0, max_val=E - 1)
                    if not first:
                        pe.wait_ge(a_ys, i)
                    pe.wait_ge(v_pick[1], i + 1)
                    nc.tensor.matmul(ps_y[:, 0:C], pick[1][:, :], bias_st[:, H:H + C], start=True, stop=False)
                    pe.wait_ge(v_hid, i + 1)
                    for k in range(KC):
                        last = nc.tensor.matmul(ps_y[:, 0:C], hid_c[:, k, :],
                                                w2[:, bass.ds(e, 1), k, :].rearrange("p o n -> p (o n)"),
                                                start=False, stop=(k == KC - 1))
                    last.then_inc(pe_ys, 1)

                def tile(i, first=False, next_tile=True, ahead=True):
                    turn_hidden(i)
                    if next_tile:
                        first_layer(i + 1)
                    if ahead:
                        tokens(i + 2)
                    second_layer(i, first)

                tokens(0)
                first_layer(0)
                tokens(1)
                tile(0, first=True)
                with pe.Fori(1, TILES - 2) as i:
                    tile(i)
                tile(TILES - 2, ahead=False)
                tile(TILES - 1, next_tile=False, ahead=False)

            @block.scalar
            def _(act):
                for e in range(E):
                    act.dma_start(w2[:, e], io["w2"][e].rearrange("(k p) m -> p k m", p=P)).then_inc(w2_in, 16)

                def gelu(i, first=False):
                    act.wait_ge(pe_hid, i + 1)
                    if not first:
                        act.wait_ge(pe_hidt, i)
                    nc.scalar.activation(hid[:, :], flat(ps_h), ACT.Gelu).then_inc(a_gelu, 1)

                def result(i, first=False):
                    act.wait_ge(pe_ys, i + 1)
                    if not first:
                        act.wait_ge(ys_out, 16 * i)
                    nc.scalar.activation(ys[:, :], ps_y[:, 0:C], ACT.Copy).then_inc(a_ys, 1)

                gelu(0, first=True)
                gelu(1)
                result(0, first=True)
                with act.Fori(1, TILES - 1) as i:
                    gelu(i + 1)
                    result(i)
                result(TILES - 1)
                for i in range(TB):
                    k = i % LOADS
                    act.wait_ge(v_sum, i + 1)
                    act.dma_start(row_block(io["out"], i), back[k][:, :]).then_inc(out_free[k], 16)
                for k in range(LOADS):
                    act.wait_ge(out_free[k], 16 * TB // LOADS)


def program(nc, io):
    with ExitStack() as ctx:
        names = ("stored", "zeroed", "w1_in")
        sems = {n: ctx.enter_context(nc.semaphore(n)) for n in names}
        keep = {n: ctx.enter_context(nc.sbuf_tensor(n, shape, F32)) for n, shape in
                (("w1", [P, E, CT, H]), ("logits", [P, TB, E]), ("zeros", [P, C]))}
        for n, shape in (("qk_scr", [2, NH, 2, D, N]),):
            io[n] = nc.dram_tensor(n, shape, F32, kind="Internal").ap()
        for n, shape in (("t_scr", [B, N, C]), ("l_scr", [B, N, C]), ("xs_scr", [TILES * P, C]), ("ys_scr", [TILES * P, C])):
            io[n] = nc.dram_tensor(n, shape, F32, kind="Internal").ap()
        attention_phase(nc, io, keep, sems)
        expert_phase(nc, io, keep, sems)


def kernel(**inputs):
    import numpy as _np
    import concourse.bacc as _bacc
    from concourse import mybir as _mybir
    from concourse.bass_utils import run_bass_kernel_spmd as _run

    x = _np.asarray(inputs["x"]).reshape(B, C, N)
    get = lambda n: _np.asarray(inputs[n])
    wqkv = get("L1_attn_w_qkv").reshape(C, NH, 3, D)
    bqkv = get("L1_attn_b_qkv").reshape(NH, 3, D)
    part = _np.arange(P)
    f = _np.float32
    arrays = {
        "x_c": x, "x_t": x.transpose(0, 2, 1),
        "w_qk0": _np.concatenate([get("L0_conv_wq"), get("L0_conv_wk")]).T, "w_v0": get("L0_conv_wv").T,
        "gamma": get("L0_conv_gamma"),
        "w_qk1": wqkv[:, :, 0:2].reshape(C, 2, HG, 2, D).transpose(0, 1, 3, 2, 4).reshape(C, 4, P),
        "b_qk1": bqkv[:, 0:2].reshape(2, HG, 2, D).transpose(0, 2, 1, 3).reshape(4, P).T,
        "w_v1": wqkv[:, :, 2].reshape(C, C), "b_v1": bqkv[:, 2].reshape(C),
        "gnw": _np.stack([get("L1_attn_gn_scale").reshape(CT, P), get("L1_attn_gn_bias").reshape(CT, P)], -1).transpose(1, 0, 2),
        "w_pr": get("L1_attn_w_proj"), "b_pr": get("L1_attn_b_proj"),
        "w_rt": get("L1_ffn_Wr"), "b_rt": get("L1_ffn_br"),
        "w1": get("L1_ffn_W1"), "b1": get("L1_ffn_b1"), "w2": get("L1_ffn_W2"), "b2": get("L1_ffn_b2"),
        "ident": _np.eye(P, dtype=f),
        "gmat": (part[:, None] // (C // GROUPS) == part[None, :] // (C // GROUPS)).astype(f) / f(C // GROUPS),
        "before": (part[:, None] < part[None, :]).astype(f), "allones": _np.ones((P, P), f),
        "expert_rev": _np.tile(_np.arange(E, 0, -1, dtype=f), (P, 1)),
        "expert_of": (part % E).astype(f)[:, None],
        "bias_mask": -(_np.arange(2 * E) >= E).astype(f)[:, None],
        "steps128": _np.tile(_np.arange(TB, dtype=f) * P, (P, 1)),
        "tile_no": _np.tile(_np.arange(TILES, dtype=f), (P, 1)),
    }
    nc = _bacc.Bacc("TRN2", target_bir_lowering=False, num_devices=1)
    feed, io = {}, {}
    for name, a in arrays.items():
        a = _np.ascontiguousarray(a)
        feed[f"in_{name}"] = a
        io[name] = nc.dram_tensor(f"in_{name}", a.shape, _mybir.dt.from_np(a.dtype), kind="ExternalInput").ap()
    io["out"] = nc.dram_tensor("out_tokens", (B, N, C), F32, kind="ExternalOutput").ap()
    program(nc, io)
    r = _run(nc, [feed], core_ids=[0])
    out = r.results[0]["out_tokens"]
    return out.transpose(0, 2, 1).reshape(B, C, 32, 32)
```

```python
from contextlib import ExitStack

import numpy as np

import concourse.bass as bass
from concourse import mybir

F32 = mybir.dt.float32
F32R = mybir.dt.float32r
I32 = mybir.dt.int32
ALU = mybir.AluOpType
ACT = mybir.ActivationFunctionType
AX = mybir.AxisListType

P = 128
B, C, N = 4, 256, 1024
CT = C // P
NB = N // P
HALF = 512
D = 32
NH = C // D
HG = P // D
GROUPS = 32
E, H = 8, 1024
KC = H // P
TB = B * NB
TILES = TB + E - 1
STACK = 3 * D
ROWS = STACK + 2
LN_EPS, GN_EPS = 1e-5, 1e-5
SCALE = float(1.0 / np.sqrt(D))
RSQRT_SEED = float(0x5F3759DF)


class Steps:

    def __init__(self, eng, sem, base=0):
        self.eng, self.sem, self.base, self.n = eng, sem, base, 0

    def did(self, ins):
        self.n += 1
        ins.then_inc(self.sem, 1)

    def wait(self):
        self.eng.wait_ge(self.sem, self.base + self.n)


def raw(ap):
    return ap.bitcast(F32)


def flat(bank_pair):
    return bank_pair.rearrange("p a n -> p (a n)")


def rsqrt(nc, steps, out, v, tmp):
    steps.did(nc.vector.tensor_scalar(tmp.bitcast(I32), v.bitcast(I32), 1, None, ALU.logical_shift_right))
    steps.wait()
    steps.did(nc.vector.tensor_scalar(out.bitcast(I32), tmp.bitcast(I32), -1.0, RSQRT_SEED, ALU.mult, ALU.add))
    steps.wait()
    for _ in range(3):
        steps.did(nc.vector.tensor_tensor(tmp, out, out, ALU.mult))
        steps.wait()
        steps.did(nc.vector.scalar_tensor_tensor(tmp, tmp, -0.5, v, ALU.mult, ALU.mult))
        steps.wait()
        steps.did(nc.vector.scalar_tensor_tensor(out, tmp, 1.5, out, ALU.add, ALU.mult))
        steps.wait()


RSQRT_STEPS = 11
A_STEPS = NB * 4 + (1 + RSQRT_STEPS) + 2 * CT + (2 + 1 + RSQRT_STEPS + 2)
C_STEPS = NB * 2 + (1 + RSQRT_STEPS)


class Phase:

    def __init__(self, nc, ctx, tag):
        self.nc, self.ctx, self.tag = nc, ctx, tag

    def sb(self, name, shape, dt=F32):
        return self.ctx.enter_context(self.nc.sbuf_tensor(self.tag + name, shape, dt))

    def ps(self, name, shape):
        return self.ctx.enter_context(self.nc.psum_tensor(self.tag + name, shape, F32))

    def sems(self, *names):
        got = [self.ctx.enter_context(self.nc.semaphore(self.tag + n)) for n in names]
        return got if len(got) > 1 else got[0]


def over_blocks(row, n):
    return row.rearrange("p (o c) -> p o c", o=1).to_broadcast([P, n, row.shape[-1]])


def layer_norm(nc, st, done, lnt, res, mv, var, rstd, tmp):
    st.did(nc.vector.tensor_scalar(var[:, :], mv[:, :, 1], LN_EPS, None, ALU.add))
    st.wait()
    rsqrt(nc, st, rstd[:, :], var[:, :], tmp[:, :])
    for j in range(NB):
        last = nc.vector.tensor_scalar(lnt[:, j, :], res[:, j, :], mv[:, j, 0:1], rstd[:, j:j + 1],
                                       ALU.subtract, ALU.mult)
    last.then_inc(done, 1)


def moments(nc, st, mv, bst, pause):
    st.wait()
    nc.vector.memset(pause[:, :], 0.0)
    for j in range(NB):
        st.did(nc.vector.bn_aggr(mv[:, j, :], bst[:, j, :]))


def turn(nc, dst, blocks, ident):
    for j in range(NB):
        last = nc.tensor.transpose(dst[:, j // 4, j % 4 * P:(j % 4 + 1) * P], blocks(j), ident[:, :])
    return last


def by_token(nc, dst, src, w, q):
    for j in range(4):
        for t in range(CT):
            last = nc.tensor.matmul(dst[:, j // 2, j % 2 * C:(j % 2 + 1) * C],
                                    src[:, t, (4 * q + j) * P:(4 * q + j + 1) * P], w[:, t, :],
                                    start=(t == 0), stop=(t == CT - 1))
    return last


def conv_phase(nc, io):
    with ExitStack() as ctx:
        ph = Phase(nc, ctx, "a_")
        sb, ps, sem = ph.sb, ph.ps, ph.sems
        ident, gmat = sb("ident", [P, P]), sb("gmat", [P, P])
        w_qk0, w_v0 = sb("w_qk0", [P, CT, 2 * D]), sb("w_v0", [P, CT, C])
        w_qk1, w_v1 = sb("w_qk1", [P, CT, 4, P]), sb("w_v1", [P, CT, C])
        b_qk1, gnw = sb("b_qk1", [P, 4]), sb("gnw", [P, CT, 2])
        b_v1, b_pr, gamma = sb("b_v1", [P, C]), sb("b_pr", [P, C]), sb("gamma", [P, 1])
        x_c, x_t = sb("x_c", [P, CT, N]), sb("x_t", [P, NB, C])
        res, lnt, h_c = sb("res", [P, NB, C]), sb("lnt", [P, NB, C]), sb("h_c", [P, CT, N])
        val, vhead = sb("val", [P, NB, C + 1]), sb("vhead", [P, NH, NB, D])
        n_st, m_st = sb("n_st", [P, N], F32R), sb("m_st", [P, N], F32R)
        expd = sb("expd", [P, NB, N])
        hi0, lo0 = sb("conv_hi", [2 * D, N], F32R), sb("conv_lo", [2 * D, N], F32R)
        hi = [sb(f"head_hi{s}", [P, N], F32R) for s in range(4)]
        lo = [sb(f"head_lo{s}", [P, N], F32R) for s in range(4)]
        nmax, msplit = sb("nmax", [P, NB]), sb("msplit", [P, 2 * NB], F32R)
        mrow = sb("mrow", [2 * NB, P], F32R)
        rc, rg = sb("rc", [P, 1]), sb("rg", [P, 1])
        bst, mv = sb("bst", [P, NB, 6]), sb("mv", [P, NB, 2])
        pause = sb("pause", [P, 1])
        var, rstd, tmp = sb("var", [P, NB]), sb("rstd", [P, NB]), sb("tmp", [P, NB])
        mvc, mg = sb("mvc", [P, CT, 2]), sb("mg", [P, CT])
        gdev, gw, gab = sb("gdev", [P, CT]), sb("gw", [P, CT]), sb("gab", [P, 2, CT])
        ps_m = ps("ps_m", [P, 2, HALF])
        ps_e = [ps(f"ps_e{k}", [P, 2, HALF]) for k in range(2)]
        ps_t = ps("ps_t", [P, HALF])

        consts_in, x_in, stack_in, maxrow_in = sem("consts_in", "x_in", "stack_in", "maxrow_in")
        spilled, v_stored, r_stored = sem("spilled", "v_stored", "r_stored")
        pe_qk0, pe_v0, pe_max, pe_maxt = sem("pe_qk0", "pe_v0", "pe_max", "pe_maxt")
        pe_exp, pe_pv0, pe_lnt, pe_gn, pe_qk1, pe_v1 = sem("pe_exp", "pe_pv0", "pe_lnt", "pe_gn", "pe_qk1", "pe_v1")
        a_hi0, a_v0, a_mrow, a_exp, a_h, a_hi = sem("a_hi0", "a_v0", "a_mrow", "a_exp", "a_h", "a_hi")
        v_set, v_step, v_mh, v_lo0, v_max, v_split = sem("v_set", "v_step", "v_mh", "v_lo0", "v_max", "v_split")
        v_res0, v_ln, v_gst, v_gd1, v_gdev, v_gab = sem("v_res0", "v_ln", "v_gst", "v_gd1", "v_gdev", "v_gab")
        v_lo, v_v1, g_res = sem("v_lo", "v_v1", "g_res")

        consts = [
            (ident[:, :], io["ident"]), (gmat[:, :], io["gmat"]),
            (w_qk0[:, :, :], io["w_qk0"].rearrange("(t p) m -> p t m", p=P)),
            (w_v0[:, :, :], io["w_v0"].rearrange("(t p) m -> p t m", p=P)),
            (w_qk1[:, :, :, :], io["w_qk1"].rearrange("(t p) g m -> p t g m", p=P)),
            (w_v1[:, :, :], io["w_v1"].rearrange("(t p) m -> p t m", p=P)),
            (b_qk1[:, :], io["b_qk1"]), (gnw[:, :, :], io["gnw"]),
            (b_v1[:, :], io["b_v1"].partition_broadcast(P)),
            (b_pr[:, :], io["b_pr"].partition_broadcast(P)),
            (gamma[:, :], io["gamma"].partition_broadcast(P)),
        ]
        all_consts = 16 * len(consts)

        with nc.Block() as block:

            @block.sync
            def _(sp):
                for dst, src in consts:
                    sp.dma_start(dst, src).then_inc(consts_in, 16)

                def image_in(b):
                    sp.dma_start(x_c[:, :, :], io["x_c"][bass.ds(b, 1)].rearrange("o (t p) n -> p (o t) n", p=P)).then_inc(x_in, 16)
                    sp.dma_start(x_t[:, :, :], io["x_t"][bass.ds(b, 1)].rearrange("o (j p) c -> p (o j) c", p=P)).then_inc(x_in, 16)

                def image(b, last=False):
                    sp.wait_ge(v_lo0, b + 1)
                    q_hi, q_lo, k_hi, k_lo = hi0[0:D, :], lo0[0:D, :], hi0[D:2 * D, :], lo0[D:2 * D, :]
                    for st, parts in ((n_st, (k_hi, k_lo, k_hi)), (m_st, (q_hi, q_hi, q_lo))):
                        for r, part in enumerate(parts):
                            sp.dma_start(raw(st[r * D:(r + 1) * D, :]), raw(part)).then_inc(stack_in, 16)
                    sp.wait_ge(a_mrow, b + 1)
                    for part in range(2):
                        sp.dma_start(raw(n_st[STACK + part:STACK + part + 1, :]),
                                     raw(mrow[part * NB:(part + 1) * NB, :])).then_inc(maxrow_in, 16)
                    if not last:
                        sp.wait_ge(pe_v0, 2 * b + 2)
                        sp.wait_ge(v_res0, NB * b + NB)
                        image_in(b + 1)
                    sp.wait_ge(g_res, 2 * b + 2)
                    sp.dma_start(io["r_scr"][bass.ds(b, 1)].rearrange("o (j p) c -> p (o j) c", p=P), res[:, :, :]).then_inc(r_stored, 16)
                    for it in range(4):
                        g, k = it // 2, it % 2
                        sp.wait_ge(v_lo, 4 * b + it + 1)
                        for part, s in enumerate((hi, lo)):
                            sp.dma_start(io["qk_scr"][k, bass.ds(b * NH + g * HG, HG), part], raw(s[it][:, :])).then_inc(spilled, 16)
                    sp.wait_ge(v_v1, 2 * b + 2)
                    sp.dma_start(io["v_scr"][bass.ds(b * NH, NH)].rearrange("h p x -> p h x"),
                                 vhead[:, :, :, :].rearrange("p h j d -> p h (j d)")).then_inc(v_stored, 16)

                image_in(0)
                with sp.Fori(0, B - 1) as b:
                    image(b)
                image(B - 1, last=True)
                sp.wait_ge(r_stored, 16 * B)
                sp.wait_ge(v_stored, 16 * B)
                sp.wait_ge(spilled, 16 * 8 * B)

            @block.gpsimd
            def _(pool):
                pool.wait_ge(consts_in, all_consts)
                with pool.Fori(0, B) as b:
                    pool.wait_ge(v_ln, b + 1)
                    nc.gpsimd.tensor_tensor(res[:, :, :], res[:, :, :], lnt[:, :, :], ALU.add).then_inc(g_res, 1)
                    pool.wait_ge(g_res, 2 * b + 1)
                    nc.gpsimd.tensor_tensor(res[:, :, :], res[:, :, :], over_blocks(b_pr[:, :], NB), ALU.add).then_inc(g_res, 1)

            @block.scalar
            def _(act):
                act.wait_ge(consts_in, all_consts)

                def image(b, first=False):
                    act.wait_ge(pe_qk0, b + 1)
                    if not first:
                        act.wait_ge(stack_in, 96 * b)
                        act.wait_ge(pe_pv0, NB * b)
                    nc.scalar.activation(hi0[:, :], flat(ps_e[0][0:2 * D]), ACT.Copy).then_inc(a_hi0, 1)
                    for t in range(2):
                        act.wait_ge(pe_v0, 2 * b + t + 1)
                        nc.scalar.activation(val[:, 4 * t:4 * t + 4, 0:C],
                                             flat((ps_e[1], ps_m)[t]).rearrange("p (j c) -> p j c", c=C),
                                             ACT.Copy).then_inc(a_v0, 1)
                    act.wait_ge(pe_maxt, b + 1)
                    if not first:
                        act.wait_ge(maxrow_in, 32 * b)
                    nc.scalar.activation(mrow[:, :], ps_t[0:2 * NB, 0:P], ACT.Copy).then_inc(a_mrow, 1)
                    for m in range(NB):
                        act.wait_ge(pe_exp, b * NB + m + 1)
                        nc.scalar.activation(expd[:, m, :], flat(ps_e[m % 2]), ACT.Exp).then_inc(a_exp, 1)
                    act.wait_ge(v_gab, b + 1)
                    for t in range(CT):
                        nc.scalar.activation(h_c[:, t, :], flat(ps_e[t]), ACT.Identity,
                                             scale=gab[:, 0, t:t + 1], bias=gab[:, 1, t:t + 1]).then_inc(a_h, 1)
                    for it in range(4):
                        act.wait_ge(pe_qk1, 4 * b + it + 1)
                        if not first:
                            act.wait_ge(spilled, 128 * b)
                        nc.scalar.activation(hi[it][:, :], flat(ps_e[it % 2]), ACT.Identity,
                                             bias=b_qk1[:, it:it + 1]).then_inc(a_hi, 1)

                image(0, first=True)
                with act.Fori(1, B) as b:
                    image(b)

            @block.tensor
            def _(pe):
                pe.wait_ge(consts_in, all_consts)
                pe.wait_ge(v_set, 1)

                def image(b, first=False):
                    pe.wait_ge(x_in, 32 * b + 32)
                    if not first:
                        pe.wait_ge(v_lo, 4 * b)
                        pe.wait_ge(v_v1, 2 * b)
                    for half in range(2):
                        for t in range(CT):
                            last = nc.tensor.matmul(ps_e[0][0:2 * D, half, :], w_qk0[:, t, :],
                                                    x_c[:, t, half * HALF:(half + 1) * HALF], start=(t == 0), stop=(t == CT - 1))
                    last.then_inc(pe_qk0, 1)
                    by_token(nc, ps_e[1], x_c, w_v0, 0).then_inc(pe_v0, 1)
                    by_token(nc, ps_m, x_c, w_v0, 1).then_inc(pe_v0, 1)
                    pe.wait_ge(stack_in, 96 * b + 96)
                    pe.wait_ge(a_v0, 2 * b + 2)
                    for nb in range(NB):
                        if nb:
                            pe.wait_ge(v_max, b * NB + nb)
                        for half in range(2):
                            last = nc.tensor.matmul(ps_m[:, half, :], n_st[0:STACK, nb * P:(nb + 1) * P],
                                                    m_st[0:STACK, half * HALF:(half + 1) * HALF], start=True, stop=True)
                        last.then_inc(pe_max, 1)
                    pe.wait_ge(v_split, b + 1)
                    nc.tensor.transpose(ps_t[0:2 * NB, 0:P], raw(msplit[:, :]), ident[:, :]).then_inc(pe_maxt, 1)
                    pe.wait_ge(maxrow_in, 32 * b + 32)
                    for m in range(NB):
                        if m >= 2:
                            pe.wait_ge(a_exp, b * NB + m - 1)
                        for half in range(2):
                            last = nc.tensor.matmul(ps_e[m % 2][:, half, :], m_st[0:ROWS, m * P:(m + 1) * P],
                                                    n_st[0:ROWS, half * HALF:(half + 1) * HALF], start=True, stop=True)
                        last.then_inc(pe_exp, 1)
                    pe.wait_ge(a_exp, b * NB + NB)
                    for j in range(NB):
                        if j >= 2:
                            pe.wait_ge(v_res0, NB * b + j - 1)
                        for m in range(NB):
                            last = nc.tensor.matmul(ps_m[:, j % 2, 0:C + 1], expd[:, m, j * P:(j + 1) * P],
                                                    val[:, m, :], start=(m == 0), stop=(m == NB - 1))
                        last.then_inc(pe_pv0, 1)
                    pe.wait_ge(v_ln, b + 1)
                    for t in range(CT):
                        turn(nc, ps_e[t], lambda j: lnt[:, j, t * P:(t + 1) * P], ident).then_inc(pe_lnt, 1)
                    pe.wait_ge(v_gst, 2 * b + 2)
                    nc.tensor.matmul(ps_t[:, 0:CT], gmat[:, :], mvc[:, :, 0], start=True, stop=True).then_inc(pe_gn, 1)
                    pe.wait_ge(v_gdev, b + 1)
                    nc.tensor.matmul(ps_t[:, 8:8 + CT], gmat[:, :], gw[:, :], start=True, stop=True).then_inc(pe_gn, 1)
                    pe.wait_ge(a_h, 2 * b + 2)
                    for q in range(2):
                        for it in (2 * q, 2 * q + 1):
                            if it >= 2:
                                pe.wait_ge(v_lo, 4 * b + it - 1)
                            for half in range(2):
                                for t in range(CT):
                                    last = nc.tensor.matmul(ps_e[it % 2][:, half, :], w_qk1[:, t, it, :],
                                                            h_c[:, t, half * HALF:(half + 1) * HALF],
                                                            start=(t == 0), stop=(t == CT - 1))
                            last.then_inc(pe_qk1, 1)
                        if q:
                            pe.wait_ge(v_v1, 2 * b + 1)
                        by_token(nc, ps_m, h_c, w_v1, q).then_inc(pe_v1, 1)

                image(0, first=True)
                with pe.Fori(1, B) as b:
                    image(b)

            @block.vector
            def _(dve):
                nc.vector.memset(raw(m_st[STACK:ROWS, :]), 1.0)
                nc.vector.memset(val[:, :, C:C + 1], 1.0).then_inc(v_set, 1)
                dve.wait_ge(consts_in, all_consts)

                def image(b, first=False):
                    st = Steps(dve, v_step, b * A_STEPS)
                    dve.wait_ge(a_hi0, b + 1)
                    nc.vector.tensor_tensor(lo0[:, :], flat(ps_e[0][0:2 * D]), raw(hi0[:, :]), ALU.subtract).then_inc(v_lo0, 1)
                    for nb in range(NB):
                        dve.wait_ge(pe_max, b * NB + nb + 1)
                        nc.vector.tensor_reduce(nmax[:, nb:nb + 1], ps_m[:, :, :], AX.XY, ALU.max, negate=True).then_inc(v_max, 1)
                    dve.wait_ge(v_max, b * NB + NB)
                    nc.vector.tensor_copy(msplit[:, 0:NB], nmax[:, :]).then_inc(v_mh, 1)
                    dve.wait_ge(v_mh, b + 1)
                    nc.vector.tensor_tensor(msplit[:, NB:2 * NB], nmax[:, :], raw(msplit[:, 0:NB]), ALU.subtract).then_inc(v_split, 1)
                    if not first:
                        dve.wait_ge(r_stored, 16 * b)
                    for j in range(NB):
                        dve.wait_ge(pe_pv0, NB * b + j + 1)
                        st.did(nc.vector.reciprocal(rc[:, :], ps_m[:, j % 2, C:C + 1]))
                        st.wait()
                        st.did(nc.vector.tensor_tensor(rg[:, :], rc[:, :], gamma[:, :], ALU.mult))
                        st.wait()
                        nc.vector.scalar_tensor_tensor(res[:, j, :], ps_m[:, j % 2, 0:C], rg[:, :], x_t[:, j, :],
                                                       ALU.mult, ALU.add).then_inc(v_res0, 1)
                        dve.wait_ge(v_res0, NB * b + j + 1)
                        st.did(nc.vector.bn_stats(bst[:, j, :], res[:, j, :]))
                    moments(nc, st, mv, bst, pause)
                    st.wait()
                    layer_norm(nc, st, v_ln, lnt, res, mv, var, rstd, tmp)
                    for t in range(CT):
                        dve.wait_ge(pe_lnt, 2 * b + t + 1)
                        for half in range(2):
                            st.did(nc.vector.bn_stats(bst[:, 2 * t + half, :], ps_e[t][:, half, :]))
                    st.wait()
                    nc.vector.memset(pause[:, :], 0.0)
                    for t in range(CT):
                        nc.vector.bn_aggr(mvc[:, t, :], bst[:, 2 * t:2 * t + 2, :].rearrange("p a s -> p (a s)")).then_inc(v_gst, 1)
                    dve.wait_ge(v_gst, 2 * b + 2)
                    dve.wait_ge(pe_gn, 2 * b + 1)
                    st.did(nc.vector.tensor_copy(mg[:, :], ps_t[:, 0:CT]))
                    st.wait()
                    nc.vector.tensor_tensor(gdev[:, :], mvc[:, :, 0], mg[:, :], ALU.subtract).then_inc(v_gd1, 1)
                    dve.wait_ge(v_gd1, b + 1)
                    st.did(nc.vector.tensor_tensor(gdev[:, :], gdev[:, :], gdev[:, :], ALU.mult))
                    st.wait()
                    nc.vector.tensor_tensor(gw[:, :], gdev[:, :], mvc[:, :, 1], ALU.add).then_inc(v_gdev, 1)
                    dve.wait_ge(pe_gn, 2 * b + 2)
                    st.did(nc.vector.tensor_scalar(var[:, 0:CT], ps_t[:, 8:8 + CT], GN_EPS, None, ALU.add))
                    st.wait()
                    rsqrt(nc, st, rstd[:, 0:CT], var[:, 0:CT], tmp[:, 0:CT])
                    st.did(nc.vector.tensor_tensor(gab[:, 0, :], rstd[:, 0:CT], gnw[:, :, 0], ALU.mult))
                    st.wait()
                    st.did(nc.vector.tensor_tensor(tmp[:, 0:CT], gab[:, 0, :], mg[:, :], ALU.mult))
                    st.wait()
                    nc.vector.tensor_tensor(gab[:, 1, :], gnw[:, :, 1], tmp[:, 0:CT], ALU.subtract).then_inc(v_gab, 1)
                    for q in range(2):
                        for it in (2 * q, 2 * q + 1):
                            dve.wait_ge(a_hi, 4 * b + it + 1)
                            nc.vector.scalar_tensor_tensor(lo[it][:, :], flat(ps_e[it % 2]), b_qk1[:, it:it + 1],
                                                           raw(hi[it][:, :]), ALU.add, ALU.subtract).then_inc(v_lo, 1)
                        dve.wait_ge(pe_v1, 2 * b + q + 1)
                        if not first:
                            dve.wait_ge(v_stored, 16 * b)
                        nc.vector.tensor_tensor(vhead[:, :, 4 * q:4 * q + 4, :].rearrange("p h j d -> p j h d"),
                                                flat(ps_m).rearrange("p (j h d) -> p j h d", h=NH, d=D),
                                                b_v1[:, :].rearrange("p (o h d) -> p o h d", o=1, d=D).to_broadcast([P, 4, NH, D]),
                                                ALU.add).then_inc(v_v1, 1)
                    return st.n

                n = image(0, first=True)
                assert n == A_STEPS, n
                with dve.Fori(1, B) as b:
                    image(b)


def head_phase(nc, io, keep, sems):
    with ExitStack() as ctx:
        ph = Phase(nc, ctx, "h_")
        sb, ps, sem = ph.sb, ph.ps, ph.sems
        HEADS = B * NH
        SLOTS = HG
        LEAD, LAG = NB // 2 + NB, 2
        ident, ones = sb("ident", [P, P]), sb("ones", [P, D])
        stk = [[sb(f"stk{s}{k}", [ROWS, N], F32R) for k in "nm"] for s in range(SLOTS)]
        vh = [sb(f"vh{s}", [P, NB, D]) for s in range(SLOTS)]
        expd = sb("expd", [P, NB, N])
        osum = sb("osum", [P, HALF])
        outh = [sb(f"outh{k}", [P, NB, D]) for k in range(2)]
        nmax = [sb(f"nmax{k}", [P, NB]) for k in range(2)]
        msplit = sb("msplit", [P, 2 * NB], F32R)
        mrow = sb("mrow", [2 * NB, P], F32R)
        rc8 = [sb(f"rc8{k}", [P, 2, 4]) for k in range(2)]
        ps_m = ps("ps_m", [P, 2, HALF])
        ps_e = [ps(f"ps_e{k}", [P, 2, HALF]) for k in range(2)]
        ps_o = [ps(f"ps_o{k}", [P, HALF]) for k in range(2)]

        stack_in = [sem(f"stack_in{s}") for s in range(SLOTS)]
        maxrow_in = [sem(f"maxrow_in{s}") for s in range(SLOTS)]
        out_stored = [sem(f"out_stored{k}") for k in range(2)]
        pe_max, pe_maxt, pe_exp, pe_pv, pe_ot = sem("pe_max", "pe_maxt", "pe_exp", "pe_pv", "pe_ot")
        a_mrow, a_exp, a_o = sem("a_mrow", "a_exp", "a_o")
        v_set, v_max, v_mh, v_split, v_rc, v_norm = sem("v_set", "v_max", "v_mh", "v_split", "v_rc", "v_norm")
        g_zero = sem("g_zero")
        STACK_DMAS = 5

        def loaded(sem_of, per, t, j):
            return sem_of[j % SLOTS], (t + j // SLOTS + 1) * per

        def stream(eng, head):
            head(0, 0, first=True)
            with eng.Fori(0, HEADS // SLOTS - 1) as t:
                for j in range(1, SLOTS + 1):
                    head(t, j)
            for j in range(1, SLOTS):
                head(HEADS // SLOTS - 1, j, left=SLOTS - 1 - j)

        with nc.Block() as block:

            @block.sync
            def _(sp):
                sp.dma_start(ident[:, :], io["ident"]).then_inc(out_stored[0], 16)
                sp.dma_start(ones[:, :], io["allones"][:, 0:D]).then_inc(out_stored[1], 16)

                def load(t, j):
                    h, s = SLOTS * t + j, j % SLOTS
                    q, k = (io["qk_scr"][i, bass.ds(h, 1)].rearrange("o s d n -> (o s d) n") for i in range(2))
                    for dst, src in ((stk[s][0][0:2 * D, :], q), (stk[s][0][2 * D:STACK, :], q[0:D, :]),
                                     (stk[s][1][0:D, :], k[0:D, :]), (stk[s][1][D:STACK, :], k)):
                        sp.dma_start(raw(dst), src).then_inc(stack_in[s], 16)
                    sp.dma_start(vh[s][:, :, :], io["v_scr"][bass.ds(h, 1)].rearrange("o p (j d) -> p (o j) d", d=D)).then_inc(stack_in[s], 16)

                def max_rows(t, j):
                    sp.wait_ge(a_mrow, SLOTS * t + j + 1)
                    for part in range(2):
                        sp.dma_start(raw(stk[j % SLOTS][0][STACK + part:STACK + part + 1, :]),
                                     raw(mrow[part * NB:(part + 1) * NB, :])).then_inc(maxrow_in[j % SLOTS], 16)

                def store(t, j):
                    h = SLOTS * t + j
                    sp.wait_ge(v_norm, h + 1)
                    sp.dma_start(io["o_scr"][bass.ds(t + j // HG, 1), :, :, j % HG * D:(j % HG + 1) * D].rearrange("o p j d -> p (o j) d"),
                                 outh[j % 2][:, :, :]).then_inc(out_stored[j % 2], 16)

                def head(t, j, first=False, left=SLOTS):
                    h = SLOTS * t + j
                    if not first:
                        if left >= SLOTS - 1:
                            sp.wait_ge(pe_exp, NB * h)
                            sp.wait_ge(pe_pv, NB * h)
                            load(t, j + SLOTS - 1)
                        store(t, j - 1)
                    if left >= 1:
                        max_rows(t, j + 1)

                for j in range(SLOTS - 1):
                    load(0, j)
                load(0, SLOTS - 1)
                max_rows(0, 0)
                stream(sp, head)
                store(HEADS // SLOTS - 1, SLOTS - 1)
                for k in range(2):
                    sp.wait_ge(out_stored[k], 16 * (HEADS // 2 + 1))

            @block.gpsimd
            def _(pool):
                nc.gpsimd.memset(keep["zeros"][:, :], 0.0).then_inc(g_zero, 1)
                pool.wait_ge(g_zero, 1)
                nz = TILES // 3
                for t in range(3):
                    pool.dma_start(io["xs_scr"][t * nz * P:(t + 1) * nz * P, :].rearrange("(j p) c -> p j c", p=P),
                                   keep["zeros"][:, :].rearrange("p (o c) -> p o c", o=1).to_broadcast([P, nz, C])
                                   ).then_inc(sems["zeroed"], 16)
                for e in range(E):
                    pool.wait_ge(pe_exp, NB * (2 * e + 2))
                    pool.dma_start(keep["w1"][:, e], io["w1"][e].rearrange("(t p) m -> p t m", p=P)).then_inc(sems["w_in"], 16)
                    pool.dma_start(keep["w2"][:, e], io["w2"][e].rearrange("(k p) m -> p k m", p=P)).then_inc(sems["w_in"], 16)

            @block.scalar
            def _(act):
                def outputs(t, j):
                    h = SLOTS * t + j
                    act.wait_ge(pe_pv, NB * h + NB)
                    act.wait_ge(pe_ot, h + 1)
                    nc.scalar.activation(osum[:, :], ps_o[j % 2][:, :], ACT.Copy).then_inc(a_o, 1)

                def next_rows(t, j, first=False):
                    act.wait_ge(pe_maxt, SLOTS * t + j + 1)
                    if not first:
                        act.wait_ge(*loaded(maxrow_in, 32, t, j - 1))
                    nc.scalar.activation(mrow[:, :], ps_o[j % 2][0:2 * NB, 0:P], ACT.Copy).then_inc(a_mrow, 1)

                def head(t, j, first=False, left=SLOTS):
                    h = SLOTS * t + j
                    for m in range(NB):
                        act.wait_ge(pe_exp, NB * h + m + 1)
                        if not first:
                            act.wait_ge(pe_pv, NB * (h - 1) + m + 1)
                        nc.scalar.activation(expd[:, m, :], flat(ps_e[m % 2]), ACT.Exp, scale=SCALE).then_inc(a_exp, 1)
                        if m == 1 and not first:
                            outputs(t, j - 1)
                        if m == 4 and left >= 1:
                            next_rows(t, j + 1)

                next_rows(0, 0, first=True)
                stream(act, head)
                outputs(HEADS // SLOTS - 1, SLOTS - 1)

            @block.tensor
            def _(pe):
                for k in range(2):
                    pe.wait_ge(out_stored[k], 16)
                pe.wait_ge(v_set, 1)
                nc.tensor.transpose(ps_o[1][:, 0:P], ident[:, :], ident[:, :]).then_inc(pe_ot, 1)

                def maxima(s, nb):
                    n_st, m_st = stk[s]
                    for half in range(2):
                        last = nc.tensor.matmul(ps_m[:, half, :], n_st[0:STACK, nb * P:(nb + 1) * P],
                                                m_st[0:STACK, half * HALF:(half + 1) * HALF], start=True, stop=True)
                    last.then_inc(pe_max, 1)

                def scores(s, m):
                    n_st, m_st = stk[s]
                    for half in range(2):
                        last = nc.tensor.matmul(ps_e[m % 2][:, half, :], m_st[:, m * P:(m + 1) * P],
                                                n_st[:, half * HALF:(half + 1) * HALF], start=True, stop=True)
                    last.then_inc(pe_exp, 1)

                def max_turn(t, j):
                    pe.wait_ge(v_split, SLOTS * t + j + 1)
                    nc.tensor.transpose(ps_o[j % 2][0:2 * NB, 0:P], raw(msplit[:, :]), ident[:, :]).then_inc(pe_maxt, 1)

                def outputs(t, j):
                    pe.wait_ge(a_o, SLOTS * t + j + 1)
                    for q in range(4):
                        last = nc.tensor.transpose(ps_o[j % 2][:, q * P:(q + 1) * P], osum[:, q * P:(q + 1) * P], ident[:, :])
                    last.then_inc(pe_ot, 1)

                def values(s, k, m):
                    for half in range(2):
                        for kind, w in enumerate((vh[s][:, m, :], ones[:, :])):
                            c = (2 * half + kind) * D
                            mm = nc.tensor.matmul(ps_o[k][c:c + D, :], w, expd[:, m, half * HALF:(half + 1) * HALF],
                                                  start=(m == 0), stop=(m == NB - 1))
                    mm.then_inc(pe_pv, 1)

                def head(t, j, first=False, left=SLOTS):
                    h = SLOTS * t + j
                    for i in range(NB):
                        if i == 0:
                            pe.wait_ge(*loaded(maxrow_in, 32, t, j))
                        if not (first and i < 2):
                            pe.wait_ge(a_exp, NB * h + i - 1)
                        scores(j % SLOTS, i)
                        ahead = 1 if i < NB // 2 else 2
                        if left >= ahead:
                            if i == NB // 2:
                                pe.wait_ge(*loaded(stack_in, 16 * STACK_DMAS, t, j + 2))
                            pe.wait_ge(v_max, NB * h + LEAD + i)
                            maxima((j + ahead) % SLOTS, (i + NB // 2) % NB)
                        if not (first and i < LAG):
                            values(j % SLOTS if i >= LAG else (j - 1) % SLOTS,
                                   j % 2 if i >= LAG else (j - 1) % 2, (i - LAG) % NB)
                        if i == 3 and not first:
                            outputs(t, j - 1)
                        if i == 4 and left >= 1:
                            if not first:
                                pe.wait_ge(v_norm, h)
                            max_turn(t, j + 1)

                for g in range(LEAD):
                    if g % NB == 0:
                        pe.wait_ge(*loaded(stack_in, 16 * STACK_DMAS, 0, g // NB))
                    if g:
                        pe.wait_ge(v_max, g)
                    maxima(g // NB, g % NB)
                    if g == NB:
                        max_turn(0, 0)
                stream(pe, head)
                for m in range(NB - LAG, NB):
                    pe.wait_ge(a_exp, NB * (HEADS - 1) + m + 1)
                    values(SLOTS - 1, 1, m)
                outputs(HEADS // SLOTS - 1, SLOTS - 1)

            @block.vector
            def _(dve):
                for s in range(SLOTS):
                    last = nc.vector.memset(raw(stk[s][1][STACK:ROWS, :]), 1.0)
                last.then_inc(v_set, 1)

                def block_max(g, k, nb):
                    dve.wait_ge(pe_max, g + 1)
                    nc.vector.tensor_reduce(nmax[k][:, nb:nb + 1], ps_m[:, :, :], AX.XY, ALU.max, negate=True).then_inc(v_max, 1)

                def split_max(t, j, first=False):
                    h, nm = SLOTS * t + j, nmax[j % 2]
                    dve.wait_ge(v_max, NB * h + NB)
                    if not first:
                        dve.wait_ge(pe_maxt, h)
                    nc.vector.tensor_copy(msplit[:, 0:NB], nm[:, :]).then_inc(v_mh, 1)
                    dve.wait_ge(v_mh, h + 1)
                    nc.vector.tensor_tensor(msplit[:, NB:2 * NB], nm[:, :], raw(msplit[:, 0:NB]),
                                            ALU.subtract).then_inc(v_split, 1)

                def norm(t, j):
                    h = SLOTS * t + j
                    dve.wait_ge(pe_ot, h + 2)
                    turned = ps_o[j % 2][:, :].rearrange("p (t a k d) -> p a t k d", t=4, a=2, k=2)
                    nc.vector.reciprocal(rc8[j % 2][:, :, :], turned[:, :, :, 1, 0]).then_inc(v_rc, 1)
                    dve.wait_ge(v_rc, h + 1)
                    dve.wait_ge(out_stored[j % 2], 16 * (SLOTS // 2 * t + j // 2 + 1))
                    nc.vector.tensor_tensor(outh[j % 2][:, :, :].rearrange("p (a t) d -> p a t d", a=2),
                                            turned[:, :, :, 0, :],
                                            rc8[j % 2][:, :, :].rearrange("p a (t o) -> p a t o", o=1).to_broadcast([P, 2, 4, D]),
                                            ALU.mult).then_inc(v_norm, 1)

                def head(t, j, first=False, left=SLOTS):
                    h = SLOTS * t + j
                    for i in range(NB):
                        ahead = 1 if i < NB // 2 else 2
                        if left >= ahead:
                            block_max(NB * h + LEAD + i, (j + ahead) % 2, (i + NB // 2) % NB)
                        if i == 3:
                            if left >= 1:
                                split_max(t, j + 1)
                            if not first:
                                norm(t, j - 1)

                for g in range(LEAD):
                    block_max(g, g // NB, g % NB)
                    if g == NB - 1:
                        split_max(0, 0, first=True)
                stream(dve, head)
                norm(HEADS // SLOTS - 1, SLOTS - 1)


def output_phase(nc, io, keep):
    with ExitStack() as ctx:
        ph = Phase(nc, ctx, "c_")
        sb, ps, sem = ph.sb, ph.ps, ph.sems
        ident, b_rt = sb("ident", [P, P]), sb("b_rt", [P, E])
        w_pr, w_rt = sb("w_pr", [P, CT, C]), sb("w_rt", [P, CT, E])
        vals_t, vals_c = sb("vals_t", [P, CT, NB, P]), sb("vals_c", [P, CT, N])
        l2_c = sb("l2_c", [P, CT, HALF])
        res, lnt = [sb(f"res{k}", [P, NB, C]) for k in range(2)], keep["lnt"]
        bst, mv = sb("bst", [P, NB, 6]), sb("mv", [P, NB, 2])
        pause = sb("pause", [P, 1])
        var, rstd, tmp = sb("var", [P, NB]), sb("rstd", [P, NB]), sb("tmp", [P, NB])
        ps_v = [ps(f"ps_v{k}", [P, 2, HALF]) for k in range(2)]
        ps_l = [ps(f"ps_l{k}", [P, HALF]) for k in range(2)]
        ps_r = ps("ps_r", [P, HALF])
        consts_in, t_stored = sem("consts_in", "t_stored")
        vals_in, res_in = sem("vals_in"), [sem(f"res_in{k}") for k in range(2)]
        pe_vt, pe_pr, pe_l2t, pe_rt = sem("pe_vt", "pe_pr", "pe_l2t", "pe_rt")
        a_vt, a_l2t = sem("a_vt", "a_l2t")
        v_step, v_res1, v_l2, v_rt = sem("v_step", "v_res1", "v_l2", "v_rt")
        consts = [(ident[:, :], io["ident"]), (b_rt[:, :], io["b_rt"].partition_broadcast(P)),
                  (w_pr[:, :, :], io["w_pr"].rearrange("(t p) m -> p t m", p=P)),
                  (w_rt[:, :, :], io["w_rt"].rearrange("(t p) m -> p t m", p=P))]
        all_consts = 16 * len(consts)

        with nc.Block() as block:

            @block.sync
            def _(sp):
                def vals_load(b):
                    sp.dma_start(vals_t[:, :, :, :], io["o_scr"][b * CT:(b + 1) * CT].rearrange("t p j c -> p t j c")).then_inc(vals_in, 16)

                def res_load(b):
                    sp.dma_start(res[b % 2][:, :, :], io["r_scr"][b].rearrange("(j p) c -> p j c", p=P)).then_inc(res_in[b % 2], 16)

                for dst, src in consts:
                    sp.dma_start(dst, src).then_inc(consts_in, 16)
                vals_load(0)
                res_load(0)
                res_load(1)
                for b in range(B):
                    if b + 1 < B:
                        sp.wait_ge(pe_vt, 2 * b + 2)
                        vals_load(b + 1)
                    sp.wait_ge(v_res1, 2 * b + 2)
                    sp.dma_start(io["t_scr"][b].rearrange("(j p) c -> p j c", p=P), res[b % 2][:, :, :]).then_inc(t_stored, 16)
                    if b + 2 < B:
                        sp.wait_ge(t_stored, 16 * b + 16)
                        sp.wait_ge(v_l2, b + 1)
                        res_load(b + 2)
                sp.wait_ge(t_stored, 16 * B)

            @block.scalar
            def _(act):
                def outputs(b):
                    for t in range(CT):
                        act.wait_ge(pe_vt, CT * b + t + 1)
                        if b:
                            act.wait_ge(pe_pr, 2 * b)
                        nc.scalar.activation(vals_c[:, t, :], flat(ps_v[t]), ACT.Copy).then_inc(a_vt, 1)

                outputs(0)
                for b in range(B):
                    if b + 1 < B:
                        outputs(b + 1)
                    for n in range(2 * b, 2 * b + 2):
                        for t in range(CT):
                            act.wait_ge(pe_l2t, 2 * n + t + 1)
                            if n:
                                act.wait_ge(pe_rt, n)
                            nc.scalar.activation(l2_c[:, t, :], ps_l[t][:, :], ACT.Copy).then_inc(a_l2t, 1)

            @block.tensor
            def _(pe):
                pe.wait_ge(consts_in, all_consts)

                def project(b):
                    pe.wait_ge(vals_in, 16 * b + 16)
                    if b:
                        pe.wait_ge(v_res1, 2 * b)
                    for t in range(CT):
                        turn(nc, ps_v[t], lambda j: vals_t[:, t, j, :], ident).then_inc(pe_vt, 1)
                    pe.wait_ge(a_vt, CT * b + CT)
                    for q in range(2):
                        by_token(nc, ps_v[q], vals_c, w_pr, q).then_inc(pe_pr, 1)

                def route(b):
                    pe.wait_ge(v_l2, b + 1)
                    if b:
                        pe.wait_ge(v_rt, b)
                    for half in range(2):
                        n = 2 * b + half
                        for t in range(CT):
                            if n:
                                pe.wait_ge(a_l2t, 2 * n + t - 1)
                            for j in range(4):
                                last = nc.tensor.transpose(ps_l[t][:, j * P:(j + 1) * P],
                                                           lnt[:, b * NB + 4 * half + j, t * P:(t + 1) * P], ident[:, :])
                            last.then_inc(pe_l2t, 1)
                        pe.wait_ge(a_l2t, 2 * n + 2)
                        for j in range(4):
                            for t in range(CT):
                                last = nc.tensor.matmul(ps_r[:, (4 * half + j) * E:(4 * half + j + 1) * E],
                                                        l2_c[:, t, j * P:(j + 1) * P], w_rt[:, t, :],
                                                        start=(t == 0), stop=(t == CT - 1))
                        last.then_inc(pe_rt, 1)

                project(0)
                for b in range(B):
                    if b + 1 < B:
                        project(b + 1)
                    route(b)

            @block.vector
            def _(dve):
                dve.wait_ge(consts_in, all_consts)
                st = Steps(dve, v_step)

                def residual(b):
                    r = res[b % 2]
                    for q in range(2):
                        dve.wait_ge(pe_pr, 2 * b + q + 1)
                        dve.wait_ge(res_in[b % 2], 16 * (b // 2 + 1))
                        nc.vector.tensor_tensor(r[:, 4 * q:4 * q + 4, :], flat(ps_v[q]).rearrange("p (j c) -> p j c", c=C),
                                                r[:, 4 * q:4 * q + 4, :], ALU.add).then_inc(v_res1, 1)
                        dve.wait_ge(v_res1, 2 * b + q + 1)
                        for j in range(4 * q, 4 * q + 4):
                            st.did(nc.vector.bn_stats(bst[:, j, :], r[:, j, :]))
                    moments(nc, st, mv, bst, pause)
                    st.wait()
                    layer_norm(nc, st, v_l2, lnt[:, b * NB:(b + 1) * NB, :], r, mv, var, rstd, tmp)

                def logits(b):
                    dve.wait_ge(pe_rt, 2 * b + 2)
                    nc.vector.tensor_tensor(keep["logits"][:, b * NB:(b + 1) * NB, :],
                                            ps_r[:, 0:NB * E].rearrange("p (j e) -> p j e", e=E),
                                            over_blocks(b_rt[:, :], NB), ALU.add).then_inc(v_rt, 1)

                residual(0)
                for b in range(B):
                    if b + 1 < B:
                        residual(b + 1)
                    logits(b)


def expert_phase(nc, io, keep, sems):
    with ExitStack() as ctx:
        def sb(name, shape, dt=F32):
            return ctx.enter_context(nc.sbuf_tensor(name, shape, dt))

        def ps(name, shape):
            return ctx.enter_context(nc.psum_tensor(name, shape, F32))

        def sem(name):
            return ctx.enter_context(nc.semaphore(name))

        LOADS = 6
        OUT = 4
        AHEAD = 3
        w1, w2, logits, lnt = keep["w1"], keep["w2"], keep["logits"], keep["lnt"]
        ident, before, allones = sb("ident2", [P, P]), sb("before", [P, P]), sb("allones", [P, P])
        expert_rev, expert_of = sb("expert_rev", [P, E]), sb("expert_of", [P, 1])
        steps128, tile_no = sb("steps128", [P, TB]), sb("tile_no", [P, TILES])
        bias, bias_hi = sb("bias", [2 * E, H + C]), sb("bias_hi", [2 * E, H + C], F32R)
        bias_mask = sb("bias_mask", [2 * E, 1])
        bias_st = sb("bias_st", [2 * E, H + C], F32R)
        onehot, work, work2 = sb("onehot", [P, TB, E]), sb("work", [P, TB, E]), sb("work2", [P, TB, E])
        total, prior = sb("total", [P, TB, E]), [sb(f"prior{k}", [P, TB, E]) for k in range(2)]
        top = sb("top", [P, TB])
        count, ntile, end = sb("count", [P, E]), sb("ntile", [P, E]), sb("end", [P, E])
        base = [sb(f"base{k}", [P, E]) for k in range(2)]
        over, tiled = sb("over", [P, E, TB]), sb("tiled", [P, TILES, E])
        pos_f, pos = sb("pos_f", [P, TB]), sb("pos", [P, TB], I32)
        texp, texp_i = sb("texp", [P, TILES]), sb("texp_i", [P, TILES], I32)
        pick_all, pick = sb("pick_all", [2 * E, TILES]), [sb(f"pick{k}", [2 * E, P], F32R) for k in (1, 2)]
        xs, xs_c = sb("xs", [P, C]), sb("xs_c", [P, CT, P])
        hid, hid_c, ys = sb("hid", [P, H]), sb("hid_c", [P, KC, P]), sb("ys", [P, C])
        back = [sb(f"back{k}", [P, C]) for k in range(LOADS)]
        total_rows = lnt

        ps_h, ps_t = ps("ps_h", [P, 2, HALF]), ps("ps_ht", [P, 2, HALF])
        ps_x, ps_y = ps("ps_x", [P, HALF]), ps("ps_y", [P, HALF])
        ps_r = ps("ps_r", [P, 2, HALF])

        consts_in, bias_in = sem("consts_in2"), sem("bias_in")
        scattered, xs_in = sem("scattered"), sem("xs_in")
        ys_out = sem("ys_out")
        t_in = sem("t_in")
        back_in = [sem(f"back_in{k}") for k in range(LOADS)]
        out_stored = sem("out_stored")
        v_step, v_onehot, v_pos, v_pick_all, v_bias = sem("v_step2"), sem("v_onehot"), sem("v_pos"), sem("v_pick_all"), sem("v_bias")
        v_xs, v_hid, v_sum = sem("v_xs"), sem("v_hid"), sem("v_sum")
        v_pick = [sem(f"v_pick{k}") for k in (1, 2)]
        pe_count, pe_xs, pe_hid, pe_hidt, pe_ys = sem("pe_count"), sem("pe_xs"), sem("pe_hid"), sem("pe_hidt"), sem("pe_ys")
        a_gelu, a_ys = sem("a_gelu"), sem("a_ys")

        consts = [(ident, "ident"), (before, "before"), (allones, "allones"), (expert_rev, "expert_rev"),
                  (expert_of, "expert_of"), (steps128, "steps128"), (tile_no, "tile_no")]
        all_consts = 16 * len(consts)

        with nc.Block() as block:

            @block.sync
            def _(sp):
                for dst, name in consts:
                    sp.dma_start(dst[:, :], io[name]).then_inc(consts_in, 16)
                for dup in range(2):
                    sp.dma_start(bias[dup * E:(dup + 1) * E, 0:H], io["b1"]).then_inc(bias_in, 16)
                    sp.dma_start(bias[dup * E:(dup + 1) * E, H:H + C], io["b2"]).then_inc(bias_in, 16)
                sp.dma_start(bias_mask[:, :], io["bias_mask"]).then_inc(bias_in, 16)
                sp.wait_ge(scattered, 16 * TB)
                def load(i):
                    sp.dma_start(xs[:, :], io["xs_scr"][bass.ds(i * P, P), :]).then_inc(xs_in, 16)

                def store(i):
                    sp.wait_ge(a_ys, i + 1)
                    sp.dma_start(io["ys_scr"][bass.ds(i * P, P), :], ys[:, :]).then_inc(ys_out, 16)

                load(0)
                for i in range(1, AHEAD):
                    sp.wait_ge(pe_xs, i)
                    load(i)
                with sp.Fori(0, TILES - AHEAD) as i:
                    sp.wait_ge(pe_xs, i + AHEAD)
                    load(i + AHEAD)
                    store(i)
                for i in range(TILES - AHEAD, TILES):
                    store(i)
                for n in range(TB // OUT):
                    sp.wait_ge(v_sum, OUT * n + OUT)
                    b, j = OUT * n // NB, OUT * n % NB
                    sp.dma_start(io["out"][b, j * P:(j + OUT) * P, :].rearrange("(j p) c -> p j c", p=P),
                                 total_rows[:, OUT * n:OUT * (n + 1), :]).then_inc(out_stored, 16)
                sp.wait_ge(out_stored, 16 * TB // OUT)

            @block.gpsimd
            def _(pool):
                pool.wait_ge(sems["zeroed"], 48)
                pool.wait_ge(v_pos, 1)
                for i in range(TB):
                    pool.indirect_dma_start(io["xs_scr"][:, :], bass.IndirectOffsetOnAxis(ap=pos[:, i:i + 1], axis=0),
                                            lnt[:, i, :], None).then_inc(scattered, 16)
                pool.wait_ge(ys_out, 16 * TILES)
                for i in range(TB):
                    k = i % LOADS
                    if i >= LOADS:
                        pool.wait_ge(v_sum, i - LOADS + 1)
                    pool.indirect_dma_start(back[k][:, :], None, io["ys_scr"][:, :],
                                            bass.IndirectOffsetOnAxis(ap=pos[:, i:i + 1], axis=0)).then_inc(back_in[k], 16)

            @block.vector
            def _(dve):
                st = Steps(dve, v_step)

                def step(ins):
                    st.did(ins)
                    st.wait()

                over_e = lambda ap, n: ap.rearrange("p (t o) -> p t o", o=1).to_broadcast([P, n, E])
                over_t = lambda ap, n: ap.rearrange("p (o e) -> p o e", o=1).to_broadcast([P, n, E])
                dve.wait_ge(consts_in, all_consts)
                step(nc.vector.tensor_reduce(top[:, :], logits[:, :, :], AX.X, ALU.max))
                step(nc.vector.tensor_tensor(work[:, :, :], logits[:, :, :], over_e(top[:, :], TB), ALU.is_ge))
                step(nc.vector.tensor_tensor(work2[:, :, :], work[:, :, :], over_t(expert_rev[:, :], TB), ALU.mult))
                step(nc.vector.tensor_reduce(top[:, :], work2[:, :, :], AX.X, ALU.max))
                nc.vector.tensor_tensor(onehot[:, :, :], work2[:, :, :], over_e(top[:, :], TB), ALU.is_equal).then_inc(v_onehot, 1)
                dve.wait_ge(pe_count, 1)
                step(nc.vector.tensor_copy(total[:, :, :], ps_r[:, 1, 0:TB * E].rearrange("p (t e) -> p t e", e=E)))
                st.did(nc.vector.memset(prior[0][:, 0:1, :], 0.0))
                step(nc.vector.tensor_copy(prior[0][:, 1:TB, :], total[:, 0:TB - 1, :]))
                a, shift = 0, 1
                while shift < TB:
                    st.did(nc.vector.tensor_copy(prior[1 - a][:, 0:shift, :], prior[a][:, 0:shift, :]))
                    step(nc.vector.tensor_tensor(prior[1 - a][:, shift:TB, :], prior[a][:, shift:TB, :],
                                                 prior[a][:, 0:TB - shift, :], ALU.add))
                    a, shift = 1 - a, 2 * shift
                step(nc.vector.tensor_tensor(count[:, :], prior[a][:, TB - 1, :], total[:, TB - 1, :], ALU.add))
                step(nc.vector.tensor_tensor(over[:, :, :], count[:, :].rearrange("p (e o) -> p e o", o=1).to_broadcast([P, E, TB]),
                                             steps128[:, :].rearrange("p (o t) -> p o t", o=1).to_broadcast([P, E, TB]), ALU.is_gt))
                step(nc.vector.tensor_reduce(ntile[:, :], over[:, :, :], AX.X, ALU.add))
                st.did(nc.vector.memset(base[0][:, 0:1], 0.0))
                step(nc.vector.tensor_copy(base[0][:, 1:E], ntile[:, 0:E - 1]))
                c, shift = 0, 1
                while shift < E:
                    st.did(nc.vector.tensor_copy(base[1 - c][:, 0:shift], base[c][:, 0:shift]))
                    step(nc.vector.tensor_tensor(base[1 - c][:, shift:E], base[c][:, shift:E], base[c][:, 0:E - shift], ALU.add))
                    c, shift = 1 - c, 2 * shift
                step(nc.vector.tensor_scalar(end[:, :], base[c][:, :], float(P), None, ALU.mult))
                step(nc.vector.tensor_tensor(work[:, :, :], ps_r[:, 0, 0:TB * E].rearrange("p (t e) -> p t e", e=E),
                                             prior[a][:, :, :], ALU.add))
                step(nc.vector.tensor_tensor(work2[:, :, :], work[:, :, :], over_t(end[:, :], TB), ALU.add))
                step(nc.vector.tensor_tensor(work[:, :, :], work2[:, :, :], onehot[:, :, :], ALU.mult))
                step(nc.vector.tensor_reduce(pos_f[:, :], work[:, :, :], AX.X, ALU.add))
                nc.vector.tensor_copy(pos[:, :], pos_f[:, :]).then_inc(v_pos, 1)
                step(nc.vector.tensor_tensor(end[:, :], base[c][:, :], ntile[:, :], ALU.add))
                step(nc.vector.tensor_tensor(tiled[:, :, :], over_e(tile_no[:, :], TILES), over_t(end[:, :], TILES), ALU.is_ge))
                step(nc.vector.tensor_reduce(texp[:, :], tiled[:, :, :], AX.X, ALU.add))
                step(nc.vector.tensor_scalar(texp[:, :], texp[:, :], float(E - 1), None, ALU.min))
                st.did(nc.vector.tensor_scalar(pick_all[:, :], texp[0:2 * E, :], expert_of[0:2 * E, :], None, ALU.is_equal))
                nc.vector.tensor_copy(texp_i[:, :], texp[:, :]).then_inc(v_pick_all, 1)
                st.wait()
                dve.wait_ge(bias_in, 80)
                step(nc.vector.tensor_copy(bias_hi[:, :], bias[:, :]))
                nc.vector.scalar_tensor_tensor(bias_st[:, :], raw(bias_hi[:, :]), bias_mask[:, :], bias[:, :],
                                               ALU.mult, ALU.add).then_inc(v_bias, 1)

                def picked(k, i):
                    nc.vector.tensor_copy(pick[k][:, :], pick_all[:, bass.ds(i, 1)].to_broadcast([2 * E, P])).then_inc(v_pick[k], 1)

                def tokens(i):
                    dve.wait_ge(pe_xs, i + 1)
                    nc.vector.tensor_copy(xs_c[:, :, :], ps_x[:, 0:C].rearrange("p (t n) -> p t n", t=CT)).then_inc(v_xs, 1)

                def tile(i, first=False, ahead=True):
                    dve.wait_ge(pe_hidt, i + 1)
                    if not first:
                        dve.wait_ge(pe_ys, i)
                    nc.vector.tensor_copy(hid_c[:, :, :], flat(ps_t).rearrange("p (k n) -> p k n", n=P)).then_inc(v_hid, 1)
                    picked(1, i)
                    if ahead:
                        dve.wait_ge(pe_hid, i + 2)
                        picked(0, i + 2)
                        tokens(i + 2)

                dve.wait_ge(v_pick_all, 1)
                picked(0, 0)
                tokens(0)
                dve.wait_ge(pe_hid, 1)
                picked(0, 1)
                tokens(1)
                tile(0, first=True)
                with dve.Fori(1, TILES - 2) as i:
                    tile(i)
                tile(TILES - 2, ahead=False)
                tile(TILES - 1, ahead=False)
                for i in range(TB):
                    k = i % LOADS
                    dve.wait_ge(back_in[k], 16 * (i // LOADS + 1))
                    dve.wait_ge(t_in, 16 * B)
                    nc.vector.tensor_tensor(total_rows[:, i, :], back[k][:, :], total_rows[:, i, :], ALU.add).then_inc(v_sum, 1)

            @block.tensor
            def _(pe):
                pe.wait_ge(consts_in, all_consts)
                pe.wait_ge(v_onehot, 1)
                oh = onehot[:, :, :].rearrange("p t e -> p (t e)")
                nc.tensor.matmul(ps_r[:, 0, 0:TB * E], before[:, :], oh, start=True, stop=True)
                nc.tensor.matmul(ps_r[:, 1, 0:TB * E], allones[:, :], oh, start=True, stop=True).then_inc(pe_count, 1)
                pe.wait_ge(sems["w_in"], 32 * E)
                pe.wait_ge(v_bias, 1)
                pe.wait_ge(v_pick_all, 1)

                def tokens(i):
                    pe.wait_ge(xs_in, 16 * i + 16)
                    for t in range(CT):
                        last = nc.tensor.transpose(ps_x[:, t * P:(t + 1) * P], xs[:, t * P:(t + 1) * P], ident[:, :])
                    last.then_inc(pe_xs, 1)

                def first_layer(i):
                    e = pe.value_load(texp_i[0:1, bass.ds(i, 1)], min_val=0, max_val=E - 1)
                    pe.wait_ge(v_pick[0], i + 1)
                    pe.wait_ge(v_xs, i + 1)
                    for half in range(2):
                        cols = slice(half * HALF, (half + 1) * HALF)
                        nc.tensor.matmul(ps_h[:, half, :], pick[0][:, :], bias_st[:, cols], start=True, stop=False)
                        for t in range(CT):
                            last = nc.tensor.matmul(ps_h[:, half, :], xs_c[:, t, :],
                                                    w1[:, bass.ds(e, 1), t, cols].rearrange("p o n -> p (o n)"),
                                                    start=False, stop=(t == CT - 1))
                    last.then_inc(pe_hid, 1)

                def turn_hidden(i):
                    pe.wait_ge(a_gelu, i + 1)
                    for k in range(KC):
                        last = nc.tensor.transpose(ps_t[:, k // 4, k % 4 * P:(k % 4 + 1) * P], hid[:, k * P:(k + 1) * P], ident[:, :])
                    last.then_inc(pe_hidt, 1)

                def second_layer(i, first=False):
                    e = pe.value_load(texp_i[0:1, bass.ds(i, 1)], min_val=0, max_val=E - 1)
                    if not first:
                        pe.wait_ge(a_ys, i)
                    pe.wait_ge(v_pick[1], i + 1)
                    nc.tensor.matmul(ps_y[:, 0:C], pick[1][:, :], bias_st[:, H:H + C], start=True, stop=False)
                    pe.wait_ge(v_hid, i + 1)
                    for k in range(KC):
                        last = nc.tensor.matmul(ps_y[:, 0:C], hid_c[:, k, :],
                                                w2[:, bass.ds(e, 1), k, :].rearrange("p o n -> p (o n)"),
                                                start=False, stop=(k == KC - 1))
                    last.then_inc(pe_ys, 1)

                def tile(i, first=False, next_tile=True, ahead=True):
                    turn_hidden(i)
                    if next_tile:
                        first_layer(i + 1)
                    if ahead:
                        tokens(i + 2)
                    second_layer(i, first)

                tokens(0)
                first_layer(0)
                tokens(1)
                tile(0, first=True)
                with pe.Fori(1, TILES - 2) as i:
                    tile(i)
                tile(TILES - 2, ahead=False)
                tile(TILES - 1, next_tile=False, ahead=False)

            @block.scalar
            def _(act):
                act.wait_ge(scattered, 16 * TB)
                for b in range(B):
                    act.dma_start(total_rows[:, b * NB:(b + 1) * NB, :],
                                  io["t_scr"][b].rearrange("(j p) c -> p j c", p=P)).then_inc(t_in, 16)

                def gelu(i, first=False):
                    act.wait_ge(pe_hid, i + 1)
                    if not first:
                        act.wait_ge(pe_hidt, i)
                    nc.scalar.activation(hid[:, :], flat(ps_h), ACT.Gelu).then_inc(a_gelu, 1)

                def result(i, first=False):
                    act.wait_ge(pe_ys, i + 1)
                    if not first:
                        act.wait_ge(ys_out, 16 * i)
                    nc.scalar.activation(ys[:, :], ps_y[:, 0:C], ACT.Copy).then_inc(a_ys, 1)

                gelu(0, first=True)
                gelu(1)
                result(0, first=True)
                with act.Fori(1, TILES - 1) as i:
                    gelu(i + 1)
                    result(i)
                result(TILES - 1)


def program(nc, io):
    for n, shape in (("qk_scr", [2, B * NH, 2, D, N]),
                     ("v_scr", [B * NH, P, NB * D]), ("o_scr", [B * CT, P, NB, P]),
                     ("r_scr", [B, N, C]), ("t_scr", [B, N, C]),
                     ("xs_scr", [TILES * P, C]), ("ys_scr", [TILES * P, C])):
        io[n] = nc.dram_tensor(n, shape, F32, kind="Internal").ap()
    conv_phase(nc, io)
    with ExitStack() as ctx:
        def kept(names):
            return {n: ctx.enter_context(nc.sbuf_tensor(n, shape, F32)) for n, shape in names}

        sems = {n: ctx.enter_context(nc.semaphore(n)) for n in ("zeroed", "w_in")}
        keep = kept((("w1", [P, E, CT, H]), ("w2", [P, E, KC, C]), ("zeros", [P, C])))
        head_phase(nc, io, keep, sems)
        keep.update(kept((("logits", [P, TB, E]), ("lnt", [P, TB, C]))))
        output_phase(nc, io, keep)
        expert_phase(nc, io, keep, sems)


def kernel(**inputs):
    import numpy as _np
    import concourse.bacc as _bacc
    from concourse import mybir as _mybir
    from concourse.bass_utils import run_bass_kernel_spmd as _run

    x = _np.asarray(inputs["x"]).reshape(B, C, N)
    get = lambda n: _np.asarray(inputs[n])
    wqkv = get("L1_attn_w_qkv").reshape(C, NH, 3, D)
    bqkv = get("L1_attn_b_qkv").reshape(NH, 3, D)
    part = _np.arange(P)
    f = _np.float32
    arrays = {
        "x_c": x, "x_t": x.transpose(0, 2, 1),
        "w_qk0": _np.concatenate([get("L0_conv_wq"), get("L0_conv_wk")]).T, "w_v0": get("L0_conv_wv").T,
        "gamma": get("L0_conv_gamma"),
        "w_qk1": wqkv[:, :, 0:2].reshape(C, 2, HG, 2, D).transpose(0, 1, 3, 2, 4).reshape(C, 4, P),
        "b_qk1": bqkv[:, 0:2].reshape(2, HG, 2, D).transpose(0, 2, 1, 3).reshape(4, P).T,
        "w_v1": wqkv[:, :, 2].reshape(C, C), "b_v1": bqkv[:, 2].reshape(C),
        "gnw": _np.stack([get("L1_attn_gn_scale").reshape(CT, P), get("L1_attn_gn_bias").reshape(CT, P)], -1).transpose(1, 0, 2),
        "w_pr": get("L1_attn_w_proj"), "b_pr": get("L1_attn_b_proj"),
        "w_rt": get("L1_ffn_Wr"), "b_rt": get("L1_ffn_br"),
        "w1": get("L1_ffn_W1"), "b1": get("L1_ffn_b1"), "w2": get("L1_ffn_W2"), "b2": get("L1_ffn_b2"),
        "ident": _np.eye(P, dtype=f),
        "gmat": (part[:, None] // (C // GROUPS) == part[None, :] // (C // GROUPS)).astype(f) / f(C // GROUPS),
        "before": (part[:, None] < part[None, :]).astype(f), "allones": _np.ones((P, P), f),
        "expert_rev": _np.tile(_np.arange(E, 0, -1, dtype=f), (P, 1)),
        "expert_of": (part % E).astype(f)[:, None],
        "bias_mask": -(_np.arange(2 * E) >= E).astype(f)[:, None],
        "steps128": _np.tile(_np.arange(TB, dtype=f) * P, (P, 1)),
        "tile_no": _np.tile(_np.arange(TILES, dtype=f), (P, 1)),
    }
    nc = _bacc.Bacc("TRN2", target_bir_lowering=False, num_devices=1)
    feed, io = {}, {}
    for name, a in arrays.items():
        a = _np.ascontiguousarray(a)
        feed[f"in_{name}"] = a
        io[name] = nc.dram_tensor(f"in_{name}", a.shape, _mybir.dt.from_np(a.dtype), kind="ExternalInput").ap()
    io["out"] = nc.dram_tensor("out_tokens", (B, N, C), F32, kind="ExternalOutput").ap()
    program(nc, io)
    r = _run(nc, [feed], core_ids=[0])
    out = r.results[0]["out_tokens"]
    return out.transpose(0, 2, 1).reshape(B, C, 32, 32)
```

```python
from contextlib import ExitStack

import numpy as np

import concourse.bass as bass
from concourse import mybir

F32 = mybir.dt.float32
F32R = mybir.dt.float32r
I32 = mybir.dt.int32
ALU = mybir.AluOpType
ACT = mybir.ActivationFunctionType
AX = mybir.AxisListType

P = 128
B, C, N = 4, 256, 1024
CT = C // P
NB = N // P
HALF = 512
D = 32
NH = C // D
HG = P // D
GROUPS = 32
E, H = 8, 1024
KC = H // P
TB = B * NB
TILES = TB + E - 1
REGION = TB * P + P
STACK = 3 * D
ROWS = STACK + 2
LN_EPS, GN_EPS = 1e-5, 1e-5
SCALE = float(1.0 / np.sqrt(D))
RSQRT_SEED = float(0x5F3759DF)


class Steps:

    def __init__(self, eng, sem, base=0):
        self.eng, self.sem, self.base, self.n = eng, sem, base, 0

    def did(self, ins):
        self.n += 1
        ins.then_inc(self.sem, 1)

    def wait(self):
        self.eng.wait_ge(self.sem, self.base + self.n)


def raw(ap):
    return ap.bitcast(F32)


def flat(bank_pair):
    return bank_pair.rearrange("p a n -> p (a n)")


def rsqrt(nc, steps, out, v, tmp):
    steps.did(nc.vector.tensor_scalar(tmp.bitcast(I32), v.bitcast(I32), 1, None, ALU.logical_shift_right))
    steps.wait()
    steps.did(nc.vector.tensor_scalar(out.bitcast(I32), tmp.bitcast(I32), -1.0, RSQRT_SEED, ALU.mult, ALU.add))
    steps.wait()
    for _ in range(3):
        steps.did(nc.vector.tensor_tensor(tmp, out, out, ALU.mult))
        steps.wait()
        steps.did(nc.vector.scalar_tensor_tensor(tmp, tmp, -0.5, v, ALU.mult, ALU.mult))
        steps.wait()
        steps.did(nc.vector.scalar_tensor_tensor(out, tmp, 1.5, out, ALU.add, ALU.mult))
        steps.wait()




class Phase:

    def __init__(self, nc, ctx, tag):
        self.nc, self.ctx, self.tag = nc, ctx, tag

    def sb(self, name, shape, dt=F32):
        return self.ctx.enter_context(self.nc.sbuf_tensor(self.tag + name, shape, dt))

    def ps(self, name, shape):
        return self.ctx.enter_context(self.nc.psum_tensor(self.tag + name, shape, F32))

    def sems(self, *names):
        got = [self.ctx.enter_context(self.nc.semaphore(self.tag + n)) for n in names]
        return got if len(got) > 1 else got[0]


def over_blocks(row, n):
    return row.rearrange("p (o c) -> p o c", o=1).to_broadcast([P, n, row.shape[-1]])


def layer_norm(nc, st, done, lnt, res, mv, var, rstd, tmp):
    st.did(nc.vector.tensor_scalar(var[:, :], mv[:, :, 1], LN_EPS, None, ALU.add))
    st.wait()
    rsqrt(nc, st, rstd[:, :], var[:, :], tmp[:, :])
    for j in range(NB):
        last = nc.vector.tensor_scalar(lnt[:, j, :], res[:, j, :], mv[:, j, 0:1], rstd[:, j:j + 1],
                                       ALU.subtract, ALU.mult)
    last.then_inc(done, 1)


def moments(nc, st, mv, bst, pause):
    st.wait()
    nc.vector.memset(pause[:, :], 0.0)
    for j in range(NB):
        st.did(nc.vector.bn_aggr(mv[:, j, :], bst[:, j, :]))


def turn(nc, dst, blocks, ident):
    for j in range(NB):
        last = nc.tensor.transpose(dst[:, j // 4, j % 4 * P:(j % 4 + 1) * P], blocks(j), ident[:, :])
    return last


def by_token(nc, dst, src, w, q):
    for j in range(4):
        for t in range(CT):
            last = nc.tensor.matmul(dst[:, j // 2, j % 2 * C:(j % 2 + 1) * C],
                                    src[:, t, (4 * q + j) * P:(4 * q + j + 1) * P], w[:, t, :],
                                    start=(t == 0), stop=(t == CT - 1))
    return last


SLOTS = HG
LEAD = NB + NB // 2
EARLY = 2
STACK_DMAS = 5


class Heads:

    def __init__(self, nc, ctx, memory):
        self.nc, self.memory, sems = nc, memory, Phase(nc, ctx, "s_")
        self.stk, self.vh = [], []
        self.slots(range(EARLY))
        self.nmax = [self.sb(f"nmax{k}", [P, NB, 2]) for k in range(2)]
        self.nmaxes, self.msplit = self.sb("nmaxes", [P, NB]), self.sb("msplit", [P, 2 * NB], F32R)
        self.mrow = self.sb("mrow", [2 * NB, P], F32R)
        self.v_stored = sems.sems("v_stored")
        self.stack_in = [sems.sems(f"stack_in{s}") for s in range(SLOTS)]
        self.maxrow_in = [sems.sems(f"maxrow_in{s}") for s in range(SLOTS)]
        self.pe_max, self.pe_maxt, self.a_mrow = sems.sems("pe_max", "pe_maxt", "a_mrow")
        self.v_max, self.v_mh, self.v_split = sems.sems("v_max", "v_mh", "v_split")

    def sb(self, name, shape, dt=F32):
        return self.memory.enter_context(self.nc.sbuf_tensor("s_" + name, shape, dt, side="right"))

    def slots(self, which):
        for s in which:
            self.stk.append([self.sb(f"stk{s}{k}", [ROWS, N], F32R) for k in "nm"])
            self.vh.append(self.sb(f"vh{s}", [P, NB, D]))

    def loaded(self, sem_of, per, t, j):
        return sem_of[j % SLOTS], (t + j // SLOTS + 1) * per

    def load(self, sp, io, t, j):
        h, s = SLOTS * t + j, j % SLOTS
        q, k = (io["qk_scr"][i, bass.ds(h, 1)].rearrange("o s d n -> (o s d) n") for i in range(2))
        for dst, src in ((self.stk[s][0][0:2 * D, :], q), (self.stk[s][0][2 * D:STACK, :], q[0:D, :]),
                         (self.stk[s][1][0:D, :], k[0:D, :]), (self.stk[s][1][D:STACK, :], k)):
            sp.dma_start(raw(dst), src).then_inc(self.stack_in[s], 16)
        sp.dma_start(self.vh[s][:, :, :],
                     io["v_scr"][bass.ds(h, 1)].rearrange("o p (j d) -> p (o j) d", d=D)).then_inc(self.stack_in[s], 16)

    def maxima(self, pe, ps_m, g, s, nb, first=False):
        n_st, m_st = self.stk[s]
        for half in range(2):
            if not first:
                pe.wait_ge(self.v_max, 2 * g + half - 1)
            self.nc.tensor.matmul(ps_m[:, half, :], n_st[0:STACK, nb * P:(nb + 1) * P],
                                  m_st[0:STACK, half * HALF:(half + 1) * HALF], start=True, stop=True).then_inc(self.pe_max, 1)

    def block_max(self, dve, ps_m, g, k, nb):
        for half in range(2):
            dve.wait_ge(self.pe_max, 2 * g + half + 1)
            self.nc.vector.tensor_reduce(self.nmax[k][:, nb, half:half + 1], ps_m[:, half, :], AX.X, ALU.max,
                                         negate=True).then_inc(self.v_max, 1)

    def split_max(self, dve, t, j, first=False):
        h, nm, msplit = SLOTS * t + j, self.nmax[j % 2], self.msplit
        dve.wait_ge(self.v_max, 2 * NB * (h + 1))
        if not first:
            dve.wait_ge(self.pe_maxt, h)
        self.nc.vector.tensor_tensor(self.nmaxes[:, :], nm[:, :, 0], nm[:, :, 1], ALU.min).then_inc(self.v_mh, 1)
        dve.wait_ge(self.v_mh, 2 * h + 1)
        self.nc.vector.tensor_copy(msplit[:, 0:NB], self.nmaxes[:, :]).then_inc(self.v_mh, 1)
        dve.wait_ge(self.v_mh, 2 * h + 2)
        self.nc.vector.tensor_tensor(msplit[:, NB:2 * NB], self.nmaxes[:, :], raw(msplit[:, 0:NB]),
                                     ALU.subtract).then_inc(self.v_split, 1)

    def max_turn(self, pe, dst, ident, t, j):
        pe.wait_ge(self.v_split, SLOTS * t + j + 1)
        self.nc.tensor.transpose(dst[0:2 * NB, 0:P], raw(self.msplit[:, :]), ident[:, :]).then_inc(self.pe_maxt, 1)

    def next_rows(self, act, src, t, j, first=False):
        act.wait_ge(self.pe_maxt, SLOTS * t + j + 1)
        if not first:
            act.wait_ge(*self.loaded(self.maxrow_in, 32, t, j - 1))
        self.nc.scalar.activation(self.mrow[:, :], src[0:2 * NB, 0:P], ACT.Copy).then_inc(self.a_mrow, 1)

    def max_rows(self, sp, t, j):
        sp.wait_ge(self.a_mrow, SLOTS * t + j + 1)
        for part in range(2):
            sp.dma_start(raw(self.stk[j % SLOTS][0][STACK + part:STACK + part + 1, :]),
                         raw(self.mrow[part * NB:(part + 1) * NB, :])).then_inc(self.maxrow_in[j % SLOTS], 16)


def conv_phase(nc, io, keep, hd):
    with ExitStack() as ctx:
        ph = Phase(nc, ctx, "a_")
        sb, ps, sem = ph.sb, ph.ps, ph.sems
        ident, gmat = keep["ident"], sb("gmat", [P, P])
        w_qk0, w_v0 = sb("w_qk0", [P, CT, 2 * D]), sb("w_v0", [P, CT, C])
        w_qk1, w_v1 = sb("w_qk1", [P, CT, 4, P]), sb("w_v1", [P, CT, C])
        b_qk1, gnw = sb("b_qk1", [P, 4]), sb("gnw", [P, CT, 2])
        b_v1, b_pr, gamma = sb("b_v1", [P, C]), sb("b_pr", [P, C]), sb("gamma", [P, 1])
        x_c, x_t = sb("x_c", [P, CT, N]), [sb(f"x_t{k}", [P, NB, C]) for k in range(2)]
        res, lnt = [sb(f"res{k}", [P, NB, C]) for k in range(2)], sb("lnt", [P, NB, C])
        h_c = sb("h_c", [P, CT, N])
        vhead = keep["res0"][:, :, :].rearrange("p j c -> p (j c)").rearrange("p (h j d) -> p h j d", h=NH, j=NB)
        val = [sb(f"val{k}", [P, NB, C + 1]) for k in range(2)]
        stk = [[sb(f"stk{k}{x}", [ROWS, N], F32R) for x in "nm"] for k in range(2)]
        expd = sb("expd", [P, NB, N])
        hi0, lo0 = sb("conv_hi", [2 * D, N], F32R), sb("conv_lo", [2 * D, N], F32R)
        hi = [sb(f"head_hi{s}", [P, N], F32R) for s in range(4)]
        lo = [sb(f"head_lo{s}", [P, N], F32R) for s in range(4)]
        nmax = [sb(f"nmax{k}", [P, NB, 2]) for k in range(2)]
        nmaxes, msplit = sb("nmaxes", [P, NB]), sb("msplit", [P, 2 * NB], F32R)
        mrow = sb("mrow", [2 * NB, P], F32R)
        rc, rg = sb("rc", [P, 1]), sb("rg", [P, 1])
        bst, mv, gst = sb("bst", [P, NB, 6]), sb("mv", [P, NB, 2]), sb("gst", [P, CT, 2, 6])
        pause = sb("pause", [P, 1])
        var, rstd, tmp = sb("var", [P, NB]), sb("rstd", [P, NB]), sb("tmp", [P, NB])
        mvc, mg = sb("mvc", [P, CT, 2]), sb("mg", [P, CT])
        gdev, gw, gab = sb("gdev", [P, CT]), sb("gw", [P, CT]), sb("gab", [P, 2, CT])
        ps_e = [ps(f"ps_e{k}", [P, 2, HALF]) for k in range(2)]
        ps_m = ps("ps_m", [P, 2, HALF])
        ps_v = ps("ps_v", [P, 2, HALF])
        turned_max, sums = ps_v[0:2 * NB, 0, 0:P], ps_m[:, 0, 0:CT]

        qk0_in, v0_in, xc_half_in = sem("qk0_in", "v0_in", "xc_half_in")
        consts_in, xc_in, stack_in, maxrow_in = sem("consts_in", "xc_in", "stack_in", "maxrow_in")
        xt_in = [sem(f"xt_in{k}") for k in range(2)]
        spilled, v_stored = sem("spilled"), hd.v_stored
        r_stored = [sem(f"r_stored{k}") for k in range(2)]
        pe_qk0, pe_v0, pe_max, pe_maxt = sem("pe_qk0", "pe_v0", "pe_max", "pe_maxt")
        pe_exp, pe_pv0, pe_lnt, pe_gn, pe_qk1, pe_v1 = sem("pe_exp", "pe_pv0", "pe_lnt", "pe_gn", "pe_qk1", "pe_v1")
        a_hi0, a_v0, a_mrow, a_exp, a_h, a_hi = sem("a_hi0", "a_v0", "a_mrow", "a_exp", "a_h", "a_hi")
        v_set, v_step, v_mh, v_lo0, v_max, v_split = sem("v_set", "v_step", "v_mh", "v_lo0", "v_max", "v_split")
        v_res0, v_ln, v_gst, v_gd1, v_gdev, v_gab = sem("v_res0", "v_ln", "v_gst", "v_gd1", "v_gdev", "v_gab")
        v_lo, v_v1, v_sums, g_res = sem("v_lo", "v_v1", "v_sums", "g_res")
        PIECES = 4
        HEAD_BLOCKS = (2, 2, 2, 1, 1, 1, 1, 1, 1)
        assert sum(HEAD_BLOCKS) == LEAD

        consts = [
            (ident[:, :], io["ident"]), (gmat[:, :], io["gmat"]),
            (w_qk1[:, :, :, :], io["w_qk1"].rearrange("(t p) g m -> p t g m", p=P)),
            (w_v1[:, :, :], io["w_v1"].rearrange("(t p) m -> p t m", p=P)),
            (b_qk1[:, :], io["b_qk1"]), (gnw[:, :, :], io["gnw"]),
            (b_v1[:, :], io["b_v1"].partition_broadcast(P)),
            (b_pr[:, :], io["b_pr"].partition_broadcast(P)),
            (gamma[:, :], io["gamma"].partition_broadcast(P)),
        ]
        all_consts = 16 * len(consts)

        with nc.Block() as block:

            @block.sync
            def _(sp):
                def image_in(b):
                    sp.dma_start(x_c[:, :, :], io["x_c"][b].rearrange("(t p) n -> p t n", p=P)).then_inc(xc_in, 16)

                def stacks(b):
                    sp.wait_ge(v_lo0, b + 1)
                    if b >= 2:
                        sp.wait_ge(pe_exp, NB * (b - 1))
                    n_st, m_st = stk[b % 2]
                    q_hi, q_lo, k_hi, k_lo = hi0[0:D, :], lo0[0:D, :], hi0[D:2 * D, :], lo0[D:2 * D, :]
                    for st, parts in ((n_st, (k_hi, k_lo, k_hi)), (m_st, (q_hi, q_hi, q_lo))):
                        for r, part in enumerate(parts):
                            sp.dma_start(raw(st[r * D:(r + 1) * D, :]), raw(part)).then_inc(stack_in, 16)

                def max_rows(b):
                    sp.wait_ge(a_mrow, b + 1)
                    for part in range(2):
                        sp.dma_start(raw(stk[b % 2][0][STACK + part:STACK + part + 1, :]),
                                     raw(mrow[part * NB:(part + 1) * NB, :])).then_inc(maxrow_in, 16)

                def next_image(b):
                    if b < B:
                        sp.wait_ge(pe_v0, PIECES * b)
                        image_in(b)

                def heads_out(b):
                    for it in range(4):
                        g, k = it // 2, it % 2
                        if b == B - 1 and it == 3:
                            hd.max_rows(sp, 0, 0)
                        sp.wait_ge(v_lo, 4 * b + it + 1)
                        for part, s in enumerate((hi, lo)):
                            sp.dma_start(io["qk_scr"][k, b * NH + g * HG:b * NH + (g + 1) * HG, part], raw(s[it][:, :])).then_inc(spilled, 16)
                    if b + 2 < B:
                        max_rows(b + 2)
                    sp.wait_ge(v_v1, 2 * b + 2)
                    sp.dma_start(io["v_scr"][b * NH:(b + 1) * NH].rearrange("h p x -> p h x"),
                                 vhead[:, :, :, :].rearrange("p h j d -> p h (j d)")).then_inc(v_stored, 16)

                sp.dma_start(w_qk0[:, :, :], io["w_qk0"].rearrange("(t p) m -> p t m", p=P)).then_inc(qk0_in, 16)
                for half, arrived in enumerate((xc_half_in, xc_in)):
                    cols = slice(half * HALF, (half + 1) * HALF)
                    sp.dma_start(x_c[:, :, cols], io["x_c"][0, :, cols].rearrange("(t p) n -> p t n", p=P)).then_inc(arrived, 16)
                sp.dma_start(w_v0[:, :, :], io["w_v0"].rearrange("(t p) m -> p t m", p=P)).then_inc(v0_in, 16)
                for dst, src in consts:
                    sp.dma_start(dst, src).then_inc(consts_in, 16)
                stacks(0)
                next_image(1)
                max_rows(0)
                stacks(1)
                next_image(2)
                for b in range(B):
                    if b == 2:
                        sp.wait_ge(spilled, 128)
                        sp.wait_ge(v_stored, 16)
                        for j in range(EARLY):
                            hd.load(sp, io, 0, j)
                    if b:
                        heads_out(b - 1)
                    else:
                        max_rows(1)
                    if b + 2 < B:
                        stacks(b + 2)
                        next_image(b + 3)
                heads_out(B - 1)
                for k in range(2):
                    sp.wait_ge(r_stored[k], 16 * B // 2)
                sp.wait_ge(spilled, 16 * 8 * B)

            @block.gpsimd
            def _(pool):
                def image_in(b):
                    pool.dma_start(x_t[b % 2][:, :, :], io["x_t"][b].rearrange("(j p) c -> p j c", p=P)).then_inc(xt_in[b % 2], 16)

                pool.wait_ge(v0_in, 16)
                image_in(0)
                image_in(1)
                pool.wait_ge(consts_in, all_consts)
                for b in range(B):
                    r = res[b % 2]
                    pool.wait_ge(v_ln, b + 1)
                    nc.gpsimd.tensor_tensor(r[:, :, :], r[:, :, :], lnt[:, :, :], ALU.add).then_inc(g_res, 1)
                    pool.wait_ge(g_res, 2 * b + 1)
                    nc.gpsimd.tensor_tensor(r[:, :, :], r[:, :, :], over_blocks(b_pr[:, :], NB), ALU.add).then_inc(g_res, 1)
                    pool.wait_ge(g_res, 2 * b + 2)
                    pool.dma_start(io["r_scr"][b].rearrange("(j p) c -> p j c", p=P), r[:, :, :]).then_inc(r_stored[b % 2], 16)
                    if b + 2 < B:
                        pool.wait_ge(v_res0, NB * b + NB)
                        image_in(b + 2)

            @block.scalar
            def _(act):
                def project(b):
                    act.wait_ge(pe_qk0, b + 1)
                    if b:
                        act.wait_ge(stack_in, 96 * b)
                    nc.scalar.activation(hi0[:, :], flat(ps_m[0:2 * D]), ACT.Copy).then_inc(a_hi0, 1)

                def values_piece(b, n):
                    act.wait_ge(pe_v0, PIECES * b + n + 1)
                    if b >= 2:
                        act.wait_ge(pe_pv0, NB * (b - 1))
                    nc.scalar.activation(val[b % 2][:, 2 * n:2 * n + 2, 0:C],
                                         ps_v[:, n % 2, :].rearrange("p (j c) -> p j c", c=C), ACT.Copy).then_inc(a_v0, 1)

                def max_rows(b):
                    act.wait_ge(pe_maxt, b + 1)
                    if b:
                        act.wait_ge(maxrow_in, 32 * b)
                    nc.scalar.activation(mrow[:, :], turned_max, ACT.Copy).then_inc(a_mrow, 1)

                def exponentials(b, after):
                    for m in range(NB):
                        act.wait_ge(pe_exp, b * NB + m + 1)
                        if b:
                            act.wait_ge(pe_pv0, NB * b)
                        nc.scalar.activation(expd[:, m, :], flat(ps_e[m % 2]), ACT.Exp).then_inc(a_exp, 1)
                        if after and 1 <= m <= PIECES:
                            values_piece(b + 1, m - 1)

                def heads_in(b):
                    act.wait_ge(v_gab, b + 1)
                    if b:
                        act.wait_ge(pe_v1, 2 * b)
                    for t in range(CT):
                        nc.scalar.activation(h_c[:, t, :], flat(ps_e[t]), ACT.Identity,
                                             scale=gab[:, 0, t:t + 1], bias=gab[:, 1, t:t + 1]).then_inc(a_h, 1)
                    for it in range(4):
                        if b == B - 1 and it == 3:
                            hd.next_rows(act, ps_v[:, 0, :], 0, 0, first=True)
                        act.wait_ge(pe_qk1, 4 * b + it + 1)
                        if b:
                            act.wait_ge(spilled, 128 * b)
                        nc.scalar.activation(hi[it][:, :], flat(ps_e[it % 2]), ACT.Identity,
                                             bias=b_qk1[:, it:it + 1]).then_inc(a_hi, 1)

                project(0)
                for n in range(PIECES):
                    values_piece(0, n)
                act.wait_ge(consts_in, all_consts)
                for b in range(-1, B):
                    if b >= 1:
                        heads_in(b - 1)
                    if b + 1 < B:
                        max_rows(b + 1)
                        if b + 2 < B:
                            project(b + 2)
                        exponentials(b + 1, after=(b + 2 < B))
                heads_in(B - 1)

            @block.tensor
            def _(pe):
                def project(b):
                    if b == 0:
                        pe.wait_ge(xc_half_in, 16)
                    else:
                        pe.wait_ge(xc_in, 16 * b + 16)
                    if b:
                        pe.wait_ge(v_max, 2 * NB * b)
                    for half in range(2):
                        if b == 0 and half == 1:
                            pe.wait_ge(xc_in, 16)
                        for t in range(CT):
                            last = nc.tensor.matmul(ps_m[0:2 * D, half, :], w_qk0[:, t, :],
                                                    x_c[:, t, half * HALF:(half + 1) * HALF], start=(t == 0), stop=(t == CT - 1))
                    last.then_inc(pe_qk0, 1)

                def values_piece(b, n):
                    if b and n < 2:
                        pe.wait_ge(a_v0, PIECES * b)
                        pe.wait_ge(a_mrow, b)
                        if b >= 2:
                            pe.wait_ge(v_res0, NB * (b - 1))
                    if n >= 2:
                        pe.wait_ge(a_v0, PIECES * b + n - 1)
                    for j in range(2):
                        for t in range(CT):
                            last = nc.tensor.matmul(ps_v[:, n % 2, j * C:(j + 1) * C],
                                                    x_c[:, t, (2 * n + j) * P:(2 * n + j + 1) * P], w_v0[:, t, :],
                                                    start=(t == 0), stop=(t == CT - 1))
                    last.then_inc(pe_v0, 1)

                def maxima(b, nb):
                    n_st, m_st = stk[b % 2]
                    if nb == 0:
                        pe.wait_ge(stack_in, 96 * b + 96)
                    for half in range(2):
                        if b + nb:
                            pe.wait_ge(v_max, 2 * (b * NB + nb) + half - 1)
                        nc.tensor.matmul(ps_m[:, half, :], n_st[0:STACK, nb * P:(nb + 1) * P],
                                         m_st[0:STACK, half * HALF:(half + 1) * HALF], start=True, stop=True).then_inc(pe_max, 1)

                def max_turn(b):
                    pe.wait_ge(v_split, b + 1)
                    if b == 0:
                        pe.wait_ge(a_v0, PIECES)
                    else:
                        pe.wait_ge(v_res0, NB * b - 1)
                    nc.tensor.transpose(turned_max, raw(msplit[:, :]), ident[:, :]).then_inc(pe_maxt, 1)

                def scores(b, m):
                    n_st, m_st = stk[b % 2]
                    if m == 0:
                        pe.wait_ge(maxrow_in, 32 * b + 32)
                        if b >= 2:
                            pe.wait_ge(v_v1, 2 * (b - 1))
                    if m >= 2:
                        pe.wait_ge(a_exp, b * NB + m - 1)
                    elif b:
                        pe.wait_ge(a_exp, b * NB)
                    for half in range(2):
                        last = nc.tensor.matmul(ps_e[m % 2][:, half, :], m_st[:, m * P:(m + 1) * P],
                                                n_st[:, half * HALF:(half + 1) * HALF], start=True, stop=True)
                    last.then_inc(pe_exp, 1)

                def outputs(b, j):
                    if j == 0:
                        pe.wait_ge(a_exp, b * NB + NB)
                        pe.wait_ge(a_v0, PIECES * min(b + 2, B))
                    if j >= 2:
                        pe.wait_ge(v_res0, NB * b + j - 1)
                    elif b == B - 1:
                        pe.wait_ge(v_res0, NB * b + j - 1)
                    for m in range(NB):
                        last = nc.tensor.matmul(ps_v[:, j % 2, 0:C + 1], expd[:, m, j * P:(j + 1) * P],
                                                val[b % 2][:, m, :], start=(m == 0), stop=(m == NB - 1))
                    last.then_inc(pe_pv0, 1)

                def norms(b, part):
                    if part == 0:
                        pe.wait_ge(v_ln, b + 1)
                        for t in range(CT):
                            turn(nc, ps_e[t], lambda j: lnt[:, j, t * P:(t + 1) * P], ident).then_inc(pe_lnt, 1)
                    else:
                        if b + 2 < B:
                            pe.wait_ge(v_max, 2 * (NB * (b + 2) + part + 1))
                        elif b == B - 1:
                            pe.wait_ge(hd.v_max, 2 * sum(HEAD_BLOCKS[:part]))
                        pe.wait_ge(*((v_gst, 2 * b + 2), (v_gdev, b + 1))[part - 1])
                        nc.tensor.matmul(sums, gmat[:, :], (mvc[:, :, 0], gw[:, :])[part - 1], start=True, stop=True).then_inc(pe_gn, 1)
                        pe.wait_ge(v_sums, 2 * b + part)

                def heads_qk(b, it):
                    pe.wait_ge(a_h, 2 * b + 2)
                    if it >= 2:
                        pe.wait_ge(v_lo, 4 * b + it - 1)
                    for half in range(2):
                        for t in range(CT):
                            last = nc.tensor.matmul(ps_e[it % 2][:, half, :], w_qk1[:, t, it, :],
                                                    h_c[:, t, half * HALF:(half + 1) * HALF],
                                                    start=(t == 0), stop=(t == CT - 1))
                    last.then_inc(pe_qk1, 1)

                def heads_v(b, q):
                    pe.wait_ge(v_lo, 4 * b + 3 + q)
                    by_token(nc, ps_e[q], h_c, w_v1, q).then_inc(pe_v1, 1)

                precedes = {2: [(norms, 1)], 3: [(norms, 2)]}
                follows = {0: [(norms, 0)], 5: [(heads_qk, 0), (heads_qk, 1)], 6: [(heads_qk, 2), (heads_qk, 3)],
                           7: [(heads_v, 0), (heads_v, 1)]}

                pe.wait_ge(qk0_in, 16)
                project(0)
                pe.wait_ge(v0_in, 16)
                for n in range(PIECES):
                    values_piece(0, n)
                pe.wait_ge(v_set, 1)
                for nb in range(NB):
                    maxima(0, nb)
                pe.wait_ge(consts_in, all_consts)
                for b in range(-1, B):
                    for j in range(NB if b >= 0 else 0):
                        outputs(b, j)
                        if b:
                            for part, n in precedes.get(j, ()):
                                part(b - 1, n)
                        if b + 1 < B and not (b and j == NB - 1):
                            maxima(b + 1, j)
                        if b and b + 1 < B and j == NB - 1:
                            max_turn(b + 1)
                        if b:
                            for part, n in follows.get(j, ()):
                                part(b - 1, n)
                            if b + 1 < B and j == NB - 2:
                                maxima(b + 1, NB - 1)
                    if b + 1 < B:
                        if b < 1:
                            max_turn(b + 1)
                        if b + 2 < B:
                            project(b + 2)
                        for m in range(NB):
                            scores(b + 1, m)
                            if 1 <= m <= PIECES and b + 2 < B:
                                values_piece(b + 2, m - 1)
                last_image = [(norms, n) for n in range(3)] + [(heads_qk, n) for n in range(4)] + [(heads_v, n) for n in range(2)]
                for i, (part, n) in enumerate(last_image):
                    part(B - 1, n)
                    first = sum(HEAD_BLOCKS[:i])
                    for g in range(first, first + HEAD_BLOCKS[i]):
                        if g % NB == 0:
                            pe.wait_ge(*hd.loaded(hd.stack_in, 16 * STACK_DMAS, 0, g // NB))
                        if g == 0:
                            pe.wait_ge(v_max, 2 * NB * B)
                        hd.maxima(pe, ps_m, g, g // NB, g % NB, first=(g == 0))
                    if (part, n) == (heads_qk, 2):
                        pe.wait_ge(v_res0, NB * B)
                        hd.max_turn(pe, ps_v[:, 0, :], ident, 0, 0)

            @block.vector
            def _(dve):
                for s in range(EARLY):
                    nc.vector.memset(raw(hd.stk[s][1][STACK:ROWS, :]), 1.0)
                for k in range(2):
                    nc.vector.memset(raw(stk[k][1][STACK:ROWS, :]), 1.0)
                    last = nc.vector.memset(val[k][:, :, C:C + 1], 1.0)
                last.then_inc(v_set, 1)
                st = Steps(dve, v_step)

                def project(b):
                    dve.wait_ge(a_hi0, b + 1)
                    nc.vector.tensor_tensor(lo0[:, :], flat(ps_m[0:2 * D]), raw(hi0[:, :]), ALU.subtract).then_inc(v_lo0, 1)

                def block_max(b, nb):
                    for half in range(2):
                        dve.wait_ge(pe_max, 2 * (b * NB + nb) + half + 1)
                        nc.vector.tensor_reduce(nmax[b % 2][:, nb, half:half + 1], ps_m[:, half, :], AX.X, ALU.max,
                                                negate=True).then_inc(v_max, 1)

                def split_max(b):
                    dve.wait_ge(v_max, 2 * (b * NB + NB))
                    if b:
                        dve.wait_ge(pe_maxt, b)
                    nm = nmax[b % 2]
                    nc.vector.tensor_tensor(nmaxes[:, :], nm[:, :, 0], nm[:, :, 1], ALU.min).then_inc(v_mh, 1)
                    dve.wait_ge(v_mh, 2 * b + 1)
                    nc.vector.tensor_copy(msplit[:, 0:NB], nmaxes[:, :]).then_inc(v_mh, 1)
                    dve.wait_ge(v_mh, 2 * b + 2)
                    nc.vector.tensor_tensor(msplit[:, NB:2 * NB], nmaxes[:, :], raw(msplit[:, 0:NB]), ALU.subtract).then_inc(v_split, 1)

                def residual(b, j):
                    if j == 0:
                        dve.wait_ge(xt_in[b % 2], 16 * (b // 2 + 1))
                        if b >= 2:
                            dve.wait_ge(r_stored[b % 2], 16 * (b // 2))
                    dve.wait_ge(pe_pv0, NB * b + j + 1)
                    st.did(nc.vector.reciprocal(rc[:, :], ps_v[:, j % 2, C:C + 1]))
                    st.wait()
                    st.did(nc.vector.tensor_tensor(rg[:, :], rc[:, :], gamma[:, :], ALU.mult))
                    st.wait()
                    nc.vector.scalar_tensor_tensor(res[b % 2][:, j, :], ps_v[:, j % 2, 0:C], rg[:, :], x_t[b % 2][:, j, :],
                                                   ALU.mult, ALU.add).then_inc(v_res0, 1)
                    dve.wait_ge(v_res0, NB * b + j + 1)
                    st.did(nc.vector.bn_stats(bst[:, j, :], res[b % 2][:, j, :]))

                def first_norm(b):
                    moments(nc, st, mv, bst, pause)
                    st.wait()
                    if b:
                        dve.wait_ge(g_res, 2 * b - 1)
                    layer_norm(nc, st, v_ln, lnt, res[b % 2], mv, var, rstd, tmp)

                def norms(b, part):
                    if part == 0:
                        for t in range(CT):
                            dve.wait_ge(pe_lnt, 2 * b + t + 1)
                            for half in range(2):
                                st.did(nc.vector.bn_stats(gst[:, t, half, :], ps_e[t][:, half, :]))
                        st.wait()
                        nc.vector.memset(pause[:, :], 0.0)
                        for t in range(CT):
                            nc.vector.bn_aggr(mvc[:, t, :], gst[:, t, :, :].rearrange("p a s -> p (a s)")).then_inc(v_gst, 1)
                        dve.wait_ge(v_gst, 2 * b + 2)
                    elif part == 1:
                        dve.wait_ge(pe_gn, 2 * b + 1)
                        nc.vector.tensor_copy(mg[:, :], sums).then_inc(v_sums, 1)
                        dve.wait_ge(v_sums, 2 * b + 1)
                        nc.vector.tensor_tensor(gdev[:, :], mvc[:, :, 0], mg[:, :], ALU.subtract).then_inc(v_gd1, 1)
                        dve.wait_ge(v_gd1, b + 1)
                        st.did(nc.vector.tensor_tensor(gdev[:, :], gdev[:, :], gdev[:, :], ALU.mult))
                        st.wait()
                        nc.vector.tensor_tensor(gw[:, :], gdev[:, :], mvc[:, :, 1], ALU.add).then_inc(v_gdev, 1)
                    else:
                        dve.wait_ge(pe_gn, 2 * b + 2)
                        nc.vector.tensor_scalar(var[:, 0:CT], sums, GN_EPS, None, ALU.add).then_inc(v_sums, 1)
                        dve.wait_ge(v_sums, 2 * b + 2)
                        rsqrt(nc, st, rstd[:, 0:CT], var[:, 0:CT], tmp[:, 0:CT])
                        st.did(nc.vector.tensor_tensor(gab[:, 0, :], rstd[:, 0:CT], gnw[:, :, 0], ALU.mult))
                        st.wait()
                        st.did(nc.vector.tensor_tensor(tmp[:, 0:CT], gab[:, 0, :], mg[:, :], ALU.mult))
                        st.wait()
                        nc.vector.tensor_tensor(gab[:, 1, :], gnw[:, :, 1], tmp[:, 0:CT], ALU.subtract).then_inc(v_gab, 1)

                def heads_qk(b, it):
                    dve.wait_ge(a_hi, 4 * b + it + 1)
                    nc.vector.scalar_tensor_tensor(lo[it][:, :], flat(ps_e[it % 2]), b_qk1[:, it:it + 1],
                                                   raw(hi[it][:, :]), ALU.add, ALU.subtract).then_inc(v_lo, 1)

                def heads_v(b, q):
                    dve.wait_ge(pe_v1, 2 * b + q + 1)
                    if b:
                        dve.wait_ge(v_stored, 16 * b)
                    nc.vector.tensor_tensor(vhead[:, :, 4 * q:4 * q + 4, :].rearrange("p h j d -> p j h d"),
                                            flat(ps_e[q]).rearrange("p (j h d) -> p j h d", h=NH, d=D),
                                            b_v1[:, :].rearrange("p (o h d) -> p o h d", o=1, d=D).to_broadcast([P, 4, NH, D]),
                                            ALU.add).then_inc(v_v1, 1)

                precedes = {2: [(norms, 1)], 3: [(norms, 2)]}
                follows = {0: [(norms, 0)], 5: [(heads_qk, 0), (heads_qk, 1)], 6: [(heads_qk, 2), (heads_qk, 3)],
                           7: [(heads_v, 0), (heads_v, 1)]}

                project(0)
                for nb in range(NB):
                    block_max(0, nb)
                split_max(0)
                dve.wait_ge(consts_in, all_consts)
                project(1)
                for b in range(B):
                    for j in range(NB):
                        if b:
                            for part, n in precedes.get(j, ()):
                                part(b - 1, n)
                        if b + 1 < B and not (b and j == NB - 1):
                            block_max(b + 1, j)
                            if j == NB - 1:
                                split_max(b + 1)
                        residual(b, j)
                        if b:
                            for part, n in follows.get(j, ()):
                                part(b - 1, n)
                            if b + 1 < B and j == NB - 2:
                                block_max(b + 1, NB - 1)
                                split_max(b + 1)
                    first_norm(b)
                    if b + 2 < B:
                        project(b + 2)
                last_image = [(norms, n) for n in range(3)] + [(heads_qk, n) for n in range(4)] + [(heads_v, n) for n in range(2)]
                for i, (part, n) in enumerate(last_image):
                    part(B - 1, n)
                    first = sum(HEAD_BLOCKS[:i])
                    for g in range(first, first + HEAD_BLOCKS[i]):
                        hd.block_max(dve, ps_m, g, g // NB, g % NB)
                        if g == NB - 1:
                            hd.split_max(dve, 0, 0, first=True)


def head_phase(nc, io, keep, sems, hd):
    with ExitStack() as ctx:
        ph = Phase(nc, ctx, "h_")
        sb, ps, sem = ph.sb, ph.ps, ph.sems
        HEADS = B * NH
        LAG = 2
        RING = 4
        ident, ones, spare_ones = keep["ident"], sb("ones", [P, D]), sb("spare_ones", [P, D])
        hd.slots(range(EARLY, SLOTS))
        stk, vh = hd.stk, hd.vh
        expd = sb("expd", [P, RING, N])
        osum = sb("osum", [P, HALF])
        outh = [keep[f"outh{k}"] for k in range(2)]
        padding = keep["padding"]
        rc8 = [sb(f"rc8{k}", [P, 2, 4]) for k in range(2)]
        ps_m = ps("ps_m", [P, 2, HALF])
        ps_e = [ps(f"ps_e{k}", [P, 2, HALF]) for k in range(2)]
        ps_o = [ps(f"ps_o{k}", [P, HALF]) for k in range(2)]

        stack_in, maxrow_in = hd.stack_in, hd.maxrow_in
        out_stored = [sems[f"o_stored{k}"] for k in range(2)]
        pe_exp, pe_pv, pe_ot = sem("pe_exp", "pe_pv", "pe_ot")
        a_exp, a_o = sem("a_exp", "a_o")
        v_rc, v_norm = sem("v_rc", "v_norm")
        g_set, g_zero, pad_in = sem("g_set", "g_zero", "pad_in")
        consts = [(keep["b_rt"][:, :], io["b_rt"].partition_broadcast(P)),
                  (keep["w_pr"][:, :, :], io["w_pr"].rearrange("(t p) m -> p t m", p=P)),
                  (keep["w_rt"][:, :, :], io["w_rt"].rearrange("(t p) m -> p t m", p=P))]

        def stream(eng, head):
            head(0, 0, first=True)
            with eng.Fori(0, HEADS // SLOTS - 1) as t:
                for j in range(1, SLOTS + 1):
                    head(t, j)
            for j in range(1, SLOTS):
                head(HEADS // SLOTS - 1, j, left=SLOTS - 1 - j)

        with nc.Block() as block:

            @block.sync
            def _(sp):
                for k, tile in enumerate((ones, spare_ones)):
                    sp.dma_start(tile[:, :], io["allones"][:, 0:D]).then_inc(out_stored[k], 16)

                def store(t, j):
                    h = SLOTS * t + j
                    sp.wait_ge(v_norm, h + 1)
                    sp.dma_start(io["o_scr"][bass.ds(t + j // HG, 1), :, :, j % HG * D:(j % HG + 1) * D].rearrange("o p j d -> p (o j) d"),
                                 outh[j % 2][:, :, :]).then_inc(out_stored[j % 2], 16)

                def head(t, j, first=False, left=SLOTS):
                    h = SLOTS * t + j
                    if not first:
                        if left >= SLOTS - 1:
                            sp.wait_ge(pe_exp, NB * h)
                            sp.wait_ge(pe_pv, NB * h)
                            hd.load(sp, io, t, j + SLOTS - 1)
                        store(t, j - 1)
                    if left >= 1:
                        hd.max_rows(sp, t, j + 1)

                for j in range(EARLY, SLOTS):
                    hd.load(sp, io, 0, j)
                sp.wait_ge(hd.v_stored, 16 * B)
                stream(sp, head)
                for dst, src in consts:
                    sp.dma_start(dst, src).then_inc(sems["consts_in"], 16)
                vals_load(sp, io, keep, sems, 0)
                res_load(sp, io, keep, sems, 0)
                store(HEADS // SLOTS - 1, SLOTS - 1)

            @block.gpsimd
            def _(pool):
                for s in range(EARLY, SLOTS):
                    nc.gpsimd.memset(raw(stk[s][1][STACK:ROWS, :]), 1.0).then_inc(g_set, 1)
                    pool.wait_ge(g_set, s - EARLY + 1)
                nc.gpsimd.memset(padding[:, 0:C], 0.0).then_inc(g_zero, 1)
                pool.dma_start(padding[:, C:C + 1].bitcast(I32), io["pad_id"]).then_inc(pad_in, 16)
                pool.wait_ge(g_zero, 1)
                pool.wait_ge(pad_in, 16)
                pool.dma_start(io["t_scr"][B * N:B * N + P, :], padding[:, 0:C]).then_inc(sems["zeroed"], 16)
                for e in range(E):
                    pool.wait_ge(pe_exp, NB * (3 * e + 2))
                    pool.dma_start(keep["w1"][:, e], io["w1"][e].rearrange("(t p) m -> p t m", p=P)).then_inc(sems["w_in"], 16)
                    pool.dma_start(keep["w2"][:, e], io["w2"][e].rearrange("(k p) m -> p k m", p=P)).then_inc(sems["w_in"], 16)

            @block.scalar
            def _(act):
                def outputs(t, j):
                    h = SLOTS * t + j
                    act.wait_ge(pe_pv, NB * h + NB)
                    act.wait_ge(pe_ot, h + 1)
                    nc.scalar.activation(osum[:, :], ps_o[j % 2][:, :], ACT.Copy).then_inc(a_o, 1)

                def head(t, j, first=False, left=SLOTS):
                    h = SLOTS * t + j
                    for m in range(NB):
                        act.wait_ge(pe_exp, NB * h + m + 1)
                        if not first or m >= RING:
                            act.wait_ge(pe_pv, NB * h + m - RING + 1)
                        nc.scalar.activation(expd[:, m % RING, :], flat(ps_e[m % 2]), ACT.Exp, scale=SCALE).then_inc(a_exp, 1)
                        if m == 1 and not first:
                            outputs(t, j - 1)
                        if m == 4 and left >= 1:
                            hd.next_rows(act, ps_o[(j + 1) % 2], t, j + 1)

                stream(act, head)
                outputs(HEADS // SLOTS - 1, SLOTS - 1)

            @block.tensor
            def _(pe):
                nc.tensor.transpose(ps_o[1][:, 0:P], ident[:, :], ident[:, :]).then_inc(pe_ot, 1)

                def scores(s, m):
                    n_st, m_st = stk[s]
                    for half in range(2):
                        last = nc.tensor.matmul(ps_e[m % 2][:, half, :], m_st[:, m * P:(m + 1) * P],
                                                n_st[:, half * HALF:(half + 1) * HALF], start=True, stop=True)
                    last.then_inc(pe_exp, 1)

                def outputs(t, j):
                    pe.wait_ge(a_o, SLOTS * t + j + 1)
                    for q in range(4):
                        last = nc.tensor.transpose(ps_o[j % 2][:, q * P:(q + 1) * P], osum[:, q * P:(q + 1) * P], ident[:, :])
                    last.then_inc(pe_ot, 1)

                def values(s, k, m):
                    for half in range(2):
                        for kind, w in enumerate((vh[s][:, m, :], ones[:, :])):
                            c = (2 * half + kind) * D
                            mm = nc.tensor.matmul(ps_o[k][c:c + D, :], w, expd[:, m % RING, half * HALF:(half + 1) * HALF],
                                                  start=(m == 0), stop=(m == NB - 1))
                    mm.then_inc(pe_pv, 1)

                def head(t, j, first=False, left=SLOTS):
                    h = SLOTS * t + j
                    for i in range(NB):
                        if i == 0:
                            pe.wait_ge(*hd.loaded(maxrow_in, 32, t, j))
                        if not (first and i < 2):
                            pe.wait_ge(a_exp, NB * h + i - 1)
                        scores(j % SLOTS, i)
                        ahead = 1 if i < NB // 2 else 2
                        if left >= ahead:
                            if i == NB // 2:
                                if first:
                                    pe.wait_ge(g_set, SLOTS - EARLY)
                                pe.wait_ge(*hd.loaded(stack_in, 16 * STACK_DMAS, t, j + 2))
                            hd.maxima(pe, ps_m, NB * h + LEAD + i, (j + ahead) % SLOTS, (i + NB // 2) % NB)
                        if first and i == LAG:
                            pe.wait_ge(out_stored[0], 16)
                        if not (first and i < LAG):
                            values(j % SLOTS if i >= LAG else (j - 1) % SLOTS,
                                   j % 2 if i >= LAG else (j - 1) % 2, (i - LAG) % NB)
                        if i == 3 and not first:
                            outputs(t, j - 1)
                        if i == 4 and left >= 1:
                            if not first:
                                pe.wait_ge(v_norm, h)
                            hd.max_turn(pe, ps_o[(j + 1) % 2], ident, t, j + 1)

                stream(pe, head)
                for m in range(NB - LAG, NB):
                    pe.wait_ge(a_exp, NB * (HEADS - 1) + m + 1)
                    values(SLOTS - 1, 1, m)
                outputs(HEADS // SLOTS - 1, SLOTS - 1)

            @block.vector
            def _(dve):
                def norm(t, j):
                    h = SLOTS * t + j
                    dve.wait_ge(pe_ot, h + 2)
                    turned = ps_o[j % 2][:, :].rearrange("p (t a k d) -> p a t k d", t=4, a=2, k=2)
                    nc.vector.reciprocal(rc8[j % 2][:, :, :], turned[:, :, :, 1, 0]).then_inc(v_rc, 1)
                    dve.wait_ge(v_rc, h + 1)
                    dve.wait_ge(out_stored[j % 2], 16 * (SLOTS // 2 * t + j // 2 + 1))
                    nc.vector.tensor_tensor(outh[j % 2][:, :, :].rearrange("p (a t) d -> p a t d", a=2),
                                            turned[:, :, :, 0, :],
                                            rc8[j % 2][:, :, :].rearrange("p a (t o) -> p a t o", o=1).to_broadcast([P, 2, 4, D]),
                                            ALU.mult).then_inc(v_norm, 1)

                def head(t, j, first=False, left=SLOTS):
                    h = SLOTS * t + j
                    for i in range(NB):
                        ahead = 1 if i < NB // 2 else 2
                        if left >= ahead:
                            hd.block_max(dve, ps_m, NB * h + LEAD + i, (j + ahead) % 2, (i + NB // 2) % NB)
                        if i == 3:
                            if left >= 1:
                                hd.split_max(dve, t, j + 1)
                            if not first:
                                norm(t, j - 1)

                stream(dve, head)
                norm(HEADS // SLOTS - 1, SLOTS - 1)


def vals_load(sp, io, keep, sems, b):
    sp.dma_start(keep["vals_t"][:, :, :, :], io["o_scr"][b * CT:(b + 1) * CT].rearrange("t p j c -> p t j c")).then_inc(sems["vals_in"], 16)


def res_load(sp, io, keep, sems, b):
    sp.dma_start(keep[f"res{b % 2}"][:, :, :], io["r_scr"][b].rearrange("(j p) c -> p j c", p=P)).then_inc(sems[f"res_in{b % 2}"], 16)


def bias_rows(keep):
    return keep["res0"][:, :, :].rearrange("p j c -> p (j c)")[0:2 * E, 0:H + C]


TABLE_CONSTS = (("expert_no", [P, E]), ("region", [P, E]), ("expert_of", [P, 1]), ("steps128", [P, TB]), ("tile_no", [P, TILES]))


def rows_out(pool, io, keep, sems, b):
    done = sems["last_scattered" if b == B - 1 else "scattered"]
    for i in range(b * NB, (b + 1) * NB):
        pool.indirect_dma_start(io["xs_scr"][:, :], bass.IndirectOffsetOnAxis(ap=keep["pos"][:, i:i + 1], axis=0),
                                keep["lnt"][:, i, :], None).then_inc(done, 16)


def output_phase(nc, io, keep, sems):
    with ExitStack() as ctx:
        ph = Phase(nc, ctx, "c_")
        sb, ps, sem = ph.sb, ph.ps, ph.sems
        ident, b_rt, w_pr, w_rt, vals_t, lnt = (keep[n] for n in ("ident", "b_rt", "w_pr", "w_rt", "vals_t", "lnt"))
        token_id = sb("token_id", [P, TB], I32)
        before, allones = sb("before", [P, P]), sb("allones", [P, P])
        expert_rev, logits = sb("expert_rev", [P, E]), sb("logits", [P, NB, E])
        onehot, work, work2 = sb("onehot", [P, NB, E]), sb("work", [P, NB, E]), sb("work2", [P, NB, E])
        top, pos_f = sb("top", [P, NB]), sb("pos_f", [P, NB])
        pos, prior = keep["pos"], keep["prior"]
        vals_c, l2_c = sb("vals_c", [P, CT, N]), sb("l2_c", [P, CT, HALF])
        keep["res1"] = sb("res1", [P, NB, C])
        res = [keep["res0"], keep["res1"]]
        bst, mv = sb("bst", [P, NB, 6]), sb("mv", [P, NB, 2])
        pause = sb("pause", [P, 1])
        var, rstd, tmp = sb("var", [P, NB]), sb("rstd", [P, NB]), sb("tmp", [P, NB])
        ps_v = [ps(f"ps_v{k}", [P, 2, HALF]) for k in range(2)]
        ps_l = [ps(f"ps_l{k}", [P, HALF]) for k in range(2)]
        ps_r = ps("ps_r", [P, HALF])
        ps_k = ps("ps_k", [P, 2, NB, E])
        t_stored, ids_in, g_ids, region_in = sem("t_stored", "ids_in", "g_ids", "region_in")
        v_onehot, pe_count = sem("v_onehot", "pe_count")
        consts_in, vals_in, res_in = sems["consts_in"], sems["vals_in"], [sems[f"res_in{k}"] for k in range(2)]
        pe_vt, pe_pr, pe_l2t, pe_rt = sem("pe_vt", "pe_pr", "pe_l2t", "pe_rt")
        a_vt, a_l2t = sem("a_vt", "a_l2t")
        v_step, v_res1, v_l2, v_rt = sem("v_step", "v_res1", "v_l2", "v_rt")
        all_consts = 16 * 3

        with nc.Block() as block:

            @block.sync
            def _(sp):
                res_load(sp, io, keep, sems, 1)
                sp.dma_start(token_id[:, :], io["token_id"]).then_inc(ids_in, 16)
                for dst, name in ((before[:, :], "before"), (allones[:, :], "allones"), (expert_rev[:, :], "expert_rev"),
                                  (prior[:, 0, :], "region")):
                    sp.dma_start(dst, io[name]).then_inc(region_in, 16)
                for name, _ in TABLE_CONSTS:
                    sp.dma_start(keep[name][:, :], io[name]).then_inc(sems["table_in"], 16)
                for name in ("bias_mask", "row_expert"):
                    sp.dma_start(keep[name][:, :], io[name]).then_inc(sems["bias_in"], 16)
                for b in range(B):
                    sp.wait_ge(v_res1, 2 * b + 2)
                    sp.dma_start(io["t_scr"][b * N:(b + 1) * N, :].rearrange("(j p) c -> p j c", p=P), res[b % 2][:, :, :]).then_inc(t_stored, 16)
                    if b + 2 < B:
                        sp.wait_ge(t_stored, 16 * b + 16)
                        sp.wait_ge(v_l2, b + 1)
                        res_load(sp, io, keep, sems, b + 2)
                    elif b == B - 2:
                        sp.wait_ge(t_stored, 16 * b + 16)
                        sp.wait_ge(v_l2, b + 1)
                        for dup in range(2):
                            rows = bias_rows(keep)[dup * E:(dup + 1) * E]
                            sp.dma_start(rows[:, 0:H], io["b1"]).then_inc(sems["bias_in"], 16)
                            sp.dma_start(rows[:, H:H + C], io["b2"]).then_inc(sems["bias_in"], 16)
                sp.wait_ge(t_stored, 16 * B)

            @block.gpsimd
            def _(pool):
                pool.wait_ge(ids_in, 16)
                nc.gpsimd.tensor_copy(lnt[:, :, C].bitcast(I32), token_id[:, :]).then_inc(g_ids, 1)
                pool.wait_ge(g_ids, 1)
                for b in range(B - 1):
                    pool.wait_ge(sems["v_pos"], b + 1)
                    rows_out(pool, io, keep, sems, b)

            @block.scalar
            def _(act):
                def outputs(b):
                    for t in range(CT):
                        act.wait_ge(pe_vt, CT * b + t + 1)
                        if b:
                            act.wait_ge(pe_pr, 2 * b)
                        nc.scalar.activation(vals_c[:, t, :], flat(ps_v[t]), ACT.Copy).then_inc(a_vt, 1)
                    if b + 1 == B - 1:
                        for k in range(2):
                            act.wait_ge(sems[f"o_stored{k}"], 16 * (B * NH // 2 + 1))
                    if b + 1 < B:
                        vals_load(act, io, keep, sems, b + 1)

                outputs(0)
                outputs(1)
                for b in range(B):
                    for n in range(2 * b, 2 * b + 2):
                        for t in range(CT):
                            act.wait_ge(pe_l2t, 2 * n + t + 1)
                            if n:
                                act.wait_ge(pe_rt, n)
                            nc.scalar.activation(l2_c[:, t, :], ps_l[t][:, :], ACT.Copy).then_inc(a_l2t, 1)
                    if b + 2 < B:
                        outputs(b + 2)

            @block.tensor
            def _(pe):
                pe.wait_ge(consts_in, all_consts)

                def turn_vals(b):
                    pe.wait_ge(vals_in, 16 * b + 16)
                    if b:
                        pe.wait_ge(v_res1, 2 * b)
                    for t in range(CT):
                        turn(nc, ps_v[t], lambda j: vals_t[:, t, j, :], ident).then_inc(pe_vt, 1)

                def project(b, q):
                    pe.wait_ge(a_vt, CT * b + CT)
                    by_token(nc, ps_v[q], vals_c, w_pr, q).then_inc(pe_pr, 1)

                def turn_norm(b, half):
                    n = 2 * b + half
                    pe.wait_ge(v_l2, b + 1)
                    for t in range(CT):
                        if n:
                            pe.wait_ge(a_l2t, 2 * n + t - 1)
                        for j in range(4):
                            last = nc.tensor.transpose(ps_l[t][:, j * P:(j + 1) * P],
                                                       lnt[:, b * NB + 4 * half + j, t * P:(t + 1) * P], ident[:, :])
                        last.then_inc(pe_l2t, 1)

                def route(b, half):
                    if b and half == 0:
                        pe.wait_ge(v_rt, b)
                    pe.wait_ge(a_l2t, 4 * b + 2 * half + 2)
                    for j in range(4):
                        for t in range(CT):
                            last = nc.tensor.matmul(ps_r[:, (4 * half + j) * E:(4 * half + j + 1) * E],
                                                    l2_c[:, t, j * P:(j + 1) * P], w_rt[:, t, :],
                                                    start=(t == 0), stop=(t == CT - 1))
                    last.then_inc(pe_rt, 1)

                def count(b):
                    oh = onehot[:, :, :].rearrange("p t e -> p (t e)")
                    pe.wait_ge(v_onehot, b + 1)
                    for n, w in enumerate((before, allones)):
                        last = nc.tensor.matmul(ps_k[:, n, :, :].rearrange("p t e -> p (t e)"), w[:, :], oh, start=True, stop=True)
                    last.then_inc(pe_count, 1)

                turn_vals(0)
                project(0, 0)
                project(0, 1)
                turn_vals(1)
                pe.wait_ge(region_in, 64)
                for b in range(B):
                    if b + 1 < B:
                        project(b + 1, 0)
                    turn_norm(b, 0)
                    if b + 1 < B:
                        project(b + 1, 1)
                    if b:
                        count(b - 1)
                    route(b, 0)
                    turn_norm(b, 1)
                    if b + 2 < B:
                        turn_vals(b + 2)
                    route(b, 1)
                count(B - 1)

            @block.vector
            def _(dve):
                dve.wait_ge(consts_in, all_consts)
                dve.wait_ge(region_in, 64)
                st = Steps(dve, v_step)

                def step(ins):
                    st.did(ins)
                    st.wait()

                over_e = lambda ap: ap.rearrange("p (t o) -> p t o", o=1).to_broadcast([P, NB, E])

                def residual(b):
                    r = res[b % 2]
                    for q in range(2):
                        dve.wait_ge(pe_pr, 2 * b + q + 1)
                        dve.wait_ge(res_in[b % 2], 16 * (b // 2 + 1))
                        nc.vector.tensor_tensor(r[:, 4 * q:4 * q + 4, :], flat(ps_v[q]).rearrange("p (j c) -> p j c", c=C),
                                                r[:, 4 * q:4 * q + 4, :], ALU.add).then_inc(v_res1, 1)
                        dve.wait_ge(v_res1, 2 * b + q + 1)
                        for j in range(4 * q, 4 * q + 4):
                            st.did(nc.vector.bn_stats(bst[:, j, :], r[:, j, :]))
                    moments(nc, st, mv, bst, pause)
                    st.wait()
                    layer_norm(nc, st, v_l2, lnt[:, b * NB:(b + 1) * NB, 0:C], r, mv, var, rstd, tmp)

                def router(b):
                    dve.wait_ge(pe_rt, 2 * b + 2)
                    nc.vector.tensor_tensor(logits[:, :, :], ps_r[:, 0:NB * E].rearrange("p (j e) -> p j e", e=E),
                                            over_blocks(b_rt[:, :], NB), ALU.add).then_inc(v_rt, 1)
                    dve.wait_ge(v_rt, b + 1)
                    step(nc.vector.tensor_reduce(top[:, :], logits[:, :, :], AX.X, ALU.max))
                    step(nc.vector.tensor_tensor(work[:, :, :], logits[:, :, :], over_e(top[:, :]), ALU.is_ge))
                    step(nc.vector.tensor_tensor(work2[:, :, :], work[:, :, :], over_blocks(expert_rev[:, :], NB), ALU.mult))
                    step(nc.vector.tensor_reduce(top[:, :], work2[:, :, :], AX.X, ALU.max))
                    nc.vector.tensor_tensor(onehot[:, :, :], work2[:, :, :], over_e(top[:, :]), ALU.is_equal).then_inc(v_onehot, 1)
                    dve.wait_ge(v_onehot, b + 1)

                def positions(b):
                    dve.wait_ge(pe_count, b + 1)
                    first = b * NB
                    for j in range(first, first + NB):
                        step(nc.vector.tensor_tensor(prior[:, j + 1, :], ps_k[:, 1, j - first, :], prior[:, j, :], ALU.add))
                    step(nc.vector.tensor_tensor(work[:, :, :], ps_k[:, 0, :, :], prior[:, first:first + NB, :], ALU.add))
                    step(nc.vector.tensor_tensor(work2[:, :, :], work[:, :, :], onehot[:, :, :], ALU.mult))
                    step(nc.vector.tensor_reduce(pos_f[:, :], work2[:, :, :], AX.X, ALU.add))
                    nc.vector.tensor_copy(pos[:, first:first + NB], pos_f[:, :]).then_inc(sems["v_pos"], 1)
                    dve.wait_ge(sems["v_pos"], b + 1)

                residual(0)
                for b in range(B):
                    if b + 1 < B:
                        residual(b + 1)
                    if b:
                        positions(b - 1)
                    router(b)
                positions(B - 1)


def expert_phase(nc, io, keep, sems):
    with ExitStack() as ctx:
        def sb(name, shape, dt=F32):
            return ctx.enter_context(nc.sbuf_tensor(name, shape, dt))

        def ps(name, shape):
            return ctx.enter_context(nc.psum_tensor(name, shape, F32))

        def sem(name):
            return ctx.enter_context(nc.semaphore(name))

        w1, w2, prior = keep["w1"], keep["w2"], keep["prior"]
        ident = keep["ident"]
        expert_no, region, expert_of, steps128, tile_no = (keep[n] for n, _ in TABLE_CONSTS)
        bias, bias_mask, row_expert = bias_rows(keep), keep["bias_mask"], keep["row_expert"]
        bias_hi = keep["vals_t"][:, :, :, :].rearrange("p t j c -> p (t j c)")[0:2 * E, 0:H + C].bitcast(F32R)
        bias_st = sb("bias_st", [2 * E, H + C], F32R)
        count, ntile, end = sb("count", [P, E]), sb("ntile", [P, E]), sb("end", [P, E])
        base = [sb(f"base{k}", [P, E]) for k in range(2)]
        over = sb("over", [P, E, TB])
        tiled, tiled2 = sb("tiled", [P, TILES, E]), sb("tiled2", [P, TILES, E])
        pad_pos = sb("pad_pos", [P, E], I32)
        start, start_i = sb("start", [P, TILES]), sb("start_i", [P, TILES], I32)
        texp, texp_i = sb("texp", [P, TILES]), sb("texp_i", [P, TILES], I32)
        pick_all, pick = sb("pick_all", [2 * E, TILES]), sb("pick", [2 * E, P], F32R)
        bias1 = keep["lnt"][:, :, :].rearrange("p t c -> p (t c)")[:, 0:E * H].rearrange("p (e h) -> p e h", h=H)
        expert_pick = sb("expert_pick", [2 * E, E, P], F32R)
        xs, xs_c = sb("xs", [P, C + 1]), sb("xs_c", [P, CT, P])
        flat_vals = keep["vals_t"][:, :, :, :].rearrange("p t j c -> p (t j c)")
        hid, hid_c = flat_vals[:, 0:H], flat_vals[:, H:2 * H].rearrange("p (k n) -> p k n", n=P)
        ys = sb("ys", [P, C])
        ids, id_in, id_out = sb("ids", [P, TILES], I32), sb("id_in", [P, 1], I32), sb("id_out", [P, 1], I32)
        t_rows, pause = sb("t_rows", [P, C]), sb("pause", [P, 5])

        ps_h, ps_t = ps("ps_h", [P, 2, HALF]), ps("ps_ht", [P, 2, HALF])
        ps_x, ps_y = ps("ps_x", [P, HALF]), ps("ps_y", [P, HALF])

        consts_in, bias_in = sems["table_in"], sems["bias_in"]
        scattered, last_scattered = sems["scattered"], sems["last_scattered"]
        xs_in, g_taken = sem("xs_in"), sem("g_taken")
        t_in, out_stored, g_ids = sem("t_in"), sem("out_stored"), sem("g_ids")
        g_pause, padded = sem("g_pause"), sem("padded")
        v_step, v_pad, v_start = sem("v_step2"), sem("v_pad"), sem("v_start")
        v_pick_all, v_bias = sem("v_pick_all"), sem("v_bias")
        v_xs, v_hid, v_ys = sem("v_xs"), sem("v_hid"), sem("v_ys")
        v_pick, pe_bias, v_biased = sem("v_pick"), sem("pe_bias"), sem("v_biased")
        a_spread, a_pick = sem("a_spread"), sem("a_pick")
        pe_xs, pe_hid, pe_hidt, pe_ys = sem("pe_xs"), sem("pe_hid"), sem("pe_hidt"), sem("pe_ys")
        a_gelu = sem("a_gelu")

        all_consts = 16 * len(TABLE_CONSTS)

        spread_from = [ps_h, ps_t]

        with nc.Block() as block:

            @block.sync
            def _(sp):
                sp.wait_ge(v_pad, 1)
                for e in range(E):
                    row = sp.value_load(pad_pos[0:1, e:e + 1], min_val=0, max_val=E * REGION - P)
                    sp.dma_start(io["xs_scr"][bass.ds(row, P), :], keep["padding"][:, :]).then_inc(padded, 16)
                sp.wait_ge(padded, 16 * E)
                sp.wait_ge(scattered, 16 * (TB - NB))
                sp.wait_ge(last_scattered, 16 * NB)
                sp.wait_ge(v_start, 1)

                def load(i):
                    row = sp.value_load(start_i[0:1, bass.ds(i, 1)], min_val=0, max_val=E * REGION - P)
                    sp.dma_start(xs[:, :], io["xs_scr"][bass.ds(row, P), :]).then_inc(xs_in, 16)

                load(0)
                with sp.Fori(1, TILES) as i:
                    sp.wait_ge(pe_xs, i)
                    sp.wait_ge(g_taken, i)
                    load(i)

            @block.gpsimd
            def _(pool):
                nc.gpsimd.memset(pause[:, :], 0.0).then_inc(g_pause, 1)
                pool.wait_ge(sems["v_pos"], B)
                rows_out(pool, io, keep, sems, B - 1)
                pool.wait_ge(g_pause, 1)
                pool.wait_ge(sems["zeroed"], 16)

                def hold(n):
                    nc.gpsimd.tensor_tensor(pause[:, n:n + 1], pause[:, 0:1], pause[:, 0:1], ALU.add)

                def gather():
                    pool.indirect_dma_start(t_rows[:, :], None, io["t_scr"][:, :],
                                            bass.IndirectOffsetOnAxis(ap=id_in[:, :], axis=0)).then_inc(t_in, 16)

                def scatter():
                    pool.indirect_dma_start(io["out"][:, :], bass.IndirectOffsetOnAxis(ap=id_out[:, :], axis=0),
                                            ys[:, :], None).then_inc(out_stored, 16)

                def take(i):
                    pool.wait_ge(xs_in, 16 * i + 16)
                    hold(3)
                    nc.gpsimd.tensor_copy(ids[:, bass.ds(i, 1)], xs[:, C:C + 1].bitcast(I32)).then_inc(g_taken, 1)
                    pool.wait_ge(g_taken, i + 1)
                    hold(4)

                def results(i, last=False):
                    pool.wait_ge(v_ys, i + 1)
                    hold(1)
                    nc.gpsimd.tensor_copy(id_out[:, :], ids[:, bass.ds(i, 1)]).then_inc(g_ids, 1)
                    if not last:
                        nc.gpsimd.tensor_copy(id_in[:, :], ids[:, bass.ds(i + 1, 1)]).then_inc(g_ids, 1)
                    pool.wait_ge(g_ids, 2 * i + 2 + (not last))
                    hold(2)
                    scatter()
                    if not last:
                        gather()

                def done(i, last=False):
                    pool.wait_ge(out_stored, 16 * i + 16)
                    if not last:
                        pool.wait_ge(t_in, 16 * i + 32)

                take(0)
                nc.gpsimd.tensor_copy(id_in[:, :], ids[:, 0:1]).then_inc(g_ids, 1)
                pool.wait_ge(g_ids, 1)
                gather()
                take(1)
                take(2)
                pool.wait_ge(t_in, 16)
                with pool.Fori(0, TILES - 3) as i:
                    results(i)
                    take(i + 3)
                    done(i)
                for i in range(TILES - 3, TILES):
                    results(i, last=(i == TILES - 1))
                    done(i, last=(i == TILES - 1))

            @block.vector
            def _(dve):
                st = Steps(dve, v_step)

                def step(ins):
                    st.did(ins)
                    st.wait()

                over_e = lambda ap, n: ap.rearrange("p (t o) -> p t o", o=1).to_broadcast([P, n, E])
                over_t = lambda ap, n: ap.rearrange("p (o e) -> p o e", o=1).to_broadcast([P, n, E])
                dve.wait_ge(consts_in, all_consts)
                nc.vector.tensor_copy(pad_pos[:, :], prior[:, TB, :]).then_inc(v_pad, 1)
                dve.wait_ge(bias_in, 96)
                step(nc.vector.tensor_copy(bias_hi, bias))
                nc.vector.scalar_tensor_tensor(bias_st[:, :], raw(bias_hi), bias_mask[:, :], bias,
                                               ALU.mult, ALU.add).then_inc(v_bias, 1)
                step(nc.vector.tensor_tensor(count[:, :], prior[:, TB, :], region[:, :], ALU.subtract))
                step(nc.vector.tensor_tensor(over[:, :, :], count[:, :].rearrange("p (e o) -> p e o", o=1).to_broadcast([P, E, TB]),
                                             steps128[:, :].rearrange("p (o t) -> p o t", o=1).to_broadcast([P, E, TB]), ALU.is_gt))
                step(nc.vector.tensor_reduce(ntile[:, :], over[:, :, :], AX.X, ALU.add))
                st.did(nc.vector.memset(base[0][:, 0:1], 0.0))
                step(nc.vector.tensor_copy(base[0][:, 1:E], ntile[:, 0:E - 1]))
                c, shift = 0, 1
                while shift < E:
                    st.did(nc.vector.tensor_copy(base[1 - c][:, 0:shift], base[c][:, 0:shift]))
                    step(nc.vector.tensor_tensor(base[1 - c][:, shift:E], base[c][:, shift:E], base[c][:, 0:E - shift], ALU.add))
                    c, shift = 1 - c, 2 * shift
                dve.wait_ge(v_pad, 1)
                step(nc.vector.tensor_tensor(end[:, :], base[c][:, :], ntile[:, :], ALU.add))
                step(nc.vector.tensor_tensor(tiled[:, :, :], over_e(tile_no[:, :], TILES), over_t(end[:, :], TILES), ALU.is_ge))
                step(nc.vector.tensor_reduce(texp[:, :], tiled[:, :, :], AX.X, ALU.add))
                step(nc.vector.tensor_scalar(texp[:, :], texp[:, :], float(E - 1), None, ALU.min))
                st.did(nc.vector.tensor_scalar(pick_all[:, :], texp[0:2 * E, :], expert_of[0:2 * E, :], None, ALU.is_equal))
                nc.vector.tensor_copy(texp_i[:, :], texp[:, :]).then_inc(v_pick_all, 1)
                st.wait()
                step(nc.vector.tensor_tensor(tiled[:, :, :], over_e(tile_no[:, :], TILES), over_t(base[c][:, :], TILES), ALU.subtract))
                step(nc.vector.tensor_scalar(end[:, :], ntile[:, :], -1.0, 0.0, ALU.add, ALU.max))
                step(nc.vector.tensor_tensor(tiled2[:, :, :], tiled[:, :, :], over_t(end[:, :], TILES), ALU.min))
                step(nc.vector.scalar_tensor_tensor(tiled[:, :, :], tiled2[:, :, :], float(P), over_t(region[:, :], TILES), ALU.mult, ALU.add))
                step(nc.vector.tensor_tensor(tiled2[:, :, :], over_e(texp[:, :], TILES), over_t(expert_no[:, :], TILES), ALU.is_equal))
                step(nc.vector.tensor_tensor(tiled[:, :, :], tiled[:, :, :], tiled2[:, :, :], ALU.mult))
                step(nc.vector.tensor_reduce(start[:, :], tiled[:, :, :], AX.X, ALU.add))
                nc.vector.tensor_copy(start_i[:, :], start[:, :]).then_inc(v_start, 1)

                def picked(i):
                    nc.vector.tensor_copy(pick[:, :], pick_all[:, bass.ds(i, 1)].to_broadcast([2 * E, P])).then_inc(v_pick, 1)

                def biased(i):
                    e = dve.value_load(texp_i[0:1, bass.ds(i, 1)], min_val=0, max_val=E - 1)
                    for half in range(2):
                        dve.wait_ge(pe_hid, 2 * i + half + 1)
                        nc.vector.tensor_tensor(ps_h[:, half, :], ps_h[:, half, :],
                                                bias1[:, bass.ds(e, 1), half * HALF:(half + 1) * HALF].rearrange("p o n -> p (o n)"),
                                                ALU.add).then_inc(v_biased, 1)

                def tokens(i):
                    dve.wait_ge(pe_xs, i + 1)
                    nc.vector.tensor_copy(xs_c[:, :, :], ps_x[:, 0:C].rearrange("p (t n) -> p t n", t=CT)).then_inc(v_xs, 1)

                def result(i, first=False):
                    dve.wait_ge(pe_ys, i + 1)
                    if not first:
                        dve.wait_ge(out_stored, 16 * i)
                    dve.wait_ge(t_in, 16 * i + 16)
                    nc.vector.tensor_tensor(ys[:, :], ps_y[:, 0:C], t_rows[:, :], ALU.add).then_inc(v_ys, 1)

                def tile(i, first=False, next_tile=True, ahead=True):
                    dve.wait_ge(pe_hidt, i + 1)
                    if not first:
                        dve.wait_ge(pe_ys, i)
                    nc.vector.tensor_copy(hid_c[:, :, :], flat(ps_t).rearrange("p (k n) -> p k n", n=P)).then_inc(v_hid, 1)
                    picked(i)
                    if next_tile:
                        biased(i + 1)
                    if ahead:
                        dve.wait_ge(pe_hid, 2 * i + 4)
                        tokens(i + 2)
                    result(i, first)

                dve.wait_ge(a_spread, E)
                dve.wait_ge(v_pick_all, 1)
                tokens(0)
                biased(0)
                tokens(1)
                tile(0, first=True)
                with dve.Fori(1, TILES - 2) as i:
                    tile(i)
                tile(TILES - 2, ahead=False)
                tile(TILES - 1, next_tile=False, ahead=False)

            @block.tensor
            def _(pe):
                pe.wait_ge(consts_in, all_consts)
                pe.wait_ge(sems["w_in"], 32 * E)
                pe.wait_ge(v_bias, 1)

                def tokens(i):
                    pe.wait_ge(xs_in, 16 * i + 16)
                    for t in range(CT):
                        last = nc.tensor.transpose(ps_x[:, t * P:(t + 1) * P], xs[:, t * P:(t + 1) * P], ident[:, :])
                    last.then_inc(pe_xs, 1)

                def first_layer(i):
                    e = pe.value_load(texp_i[0:1, bass.ds(i, 1)], min_val=0, max_val=E - 1)
                    pe.wait_ge(v_xs, i + 1)
                    for half in range(2):
                        cols = slice(half * HALF, (half + 1) * HALF)
                        for t in range(CT):
                            last = nc.tensor.matmul(ps_h[:, half, :], xs_c[:, t, :],
                                                    w1[:, bass.ds(e, 1), t, cols].rearrange("p o n -> p (o n)"),
                                                    start=(t == 0), stop=(t == CT - 1))
                        last.then_inc(pe_hid, 1)

                def turn_hidden(i):
                    pe.wait_ge(a_gelu, i + 1)
                    for k in range(KC):
                        last = nc.tensor.transpose(ps_t[:, k // 4, k % 4 * P:(k % 4 + 1) * P], hid[:, k * P:(k + 1) * P], ident[:, :])
                    last.then_inc(pe_hidt, 1)

                def second_layer(i, first=False):
                    e = pe.value_load(texp_i[0:1, bass.ds(i, 1)], min_val=0, max_val=E - 1)
                    if not first:
                        pe.wait_ge(v_ys, i)
                    pe.wait_ge(v_pick, i + 1)
                    nc.tensor.matmul(ps_y[:, 0:C], pick[:, :], bias_st[:, H:H + C], start=True, stop=False)
                    pe.wait_ge(v_hid, i + 1)
                    for k in range(KC):
                        last = nc.tensor.matmul(ps_y[:, 0:C], hid_c[:, k, :],
                                                w2[:, bass.ds(e, 1), k, :].rearrange("p o n -> p (o n)"),
                                                start=False, stop=(k == KC - 1))
                    last.then_inc(pe_ys, 1)

                def tile(i, first=False, next_tile=True, ahead=True):
                    turn_hidden(i)
                    if next_tile:
                        first_layer(i + 1)
                    if ahead:
                        tokens(i + 2)
                    second_layer(i, first)

                pe.wait_ge(a_pick, 1)
                for e in range(E):
                    if e >= 2:
                        pe.wait_ge(a_spread, e - 1)
                    for half in range(2):
                        last = nc.tensor.matmul(spread_from[e % 2][:, half, :], expert_pick[:, e, :],
                                                bias_st[:, half * HALF:(half + 1) * HALF], start=True, stop=True)
                    last.then_inc(pe_bias, 1)
                tokens(0)
                pe.wait_ge(v_pick_all, 1)
                pe.wait_ge(a_spread, E)
                first_layer(0)
                tokens(1)
                tile(0, first=True)
                with pe.Fori(1, TILES - 2) as i:
                    tile(i)
                tile(TILES - 2, ahead=False)
                tile(TILES - 1, next_tile=False, ahead=False)

            @block.scalar
            def _(act):
                def gelu(i, first=False):
                    act.wait_ge(v_biased, 2 * i + 2)
                    if not first:
                        act.wait_ge(pe_hidt, i)
                    nc.scalar.activation(hid[:, :], flat(ps_h), ACT.Gelu).then_inc(a_gelu, 1)

                act.wait_ge(bias_in, 96)
                nc.scalar.activation(expert_pick[:, :, :], row_expert[:, :].rearrange("p (e o) -> p e o", o=1).to_broadcast([2 * E, E, P]),
                                     ACT.Copy).then_inc(a_pick, 1)
                act.wait_ge(scattered, 16 * (TB - NB))
                for e in range(E):
                    act.wait_ge(pe_bias, e + 1)
                    if (e + 1) * H > (TB - NB) * (C + 1):
                        act.wait_ge(last_scattered, 16 * NB)
                    nc.scalar.activation(bias1[:, e, :], flat(spread_from[e % 2]), ACT.Copy).then_inc(a_spread, 1)
                gelu(0, first=True)
                with act.Fori(1, TILES) as i:
                    gelu(i)


def program(nc, io):
    for n, shape in (("qk_scr", [2, B * NH, 2, D, N]),
                     ("v_scr", [B * NH, P, NB * D]), ("o_scr", [B * CT, P, NB, P]),
                     ("r_scr", [B, N, C]), ("t_scr", [B * N + P, C]), ("xs_scr", [E * REGION, C + 1])):
        io[n] = nc.dram_tensor(n, shape, F32, kind="Internal").ap()
    with ExitStack() as ctx:
        def kept(names):
            return {n: ctx.enter_context(nc.sbuf_tensor(n, shape, F32)) for n, shape in names}

        keep = kept((("ident", [P, P]), ("res0", [P, NB, C])))
        during_heads = ctx.enter_context(ExitStack())
        heads = Heads(nc, ctx, during_heads)
        conv_phase(nc, io, keep, heads)
        sems = {n: ctx.enter_context(nc.semaphore(n)) for n in (
            "zeroed", "w_in", "scattered", "last_scattered", "v_pos", "consts_in", "vals_in", "res_in0", "res_in1",
            "table_in", "bias_in", "o_stored0", "o_stored1")}
        keep.update(kept((("w1", [P, E, CT, H]), ("w2", [P, E, KC, C]), ("padding", [P, C + 1]),
                           ("outh0", [P, NB, D]), ("outh1", [P, NB, D]))))
        keep.update(kept((("b_rt", [P, E]), ("w_pr", [P, CT, C]), ("w_rt", [P, CT, E]),
                          ("vals_t", [P, CT, NB, P]))))
        head_phase(nc, io, keep, sems, heads)
        during_heads.close()
        keep.update(kept((("lnt", [P, TB, C + 1]), ("prior", [P, TB + 1, E]),
                           ("bias_mask", [2 * E, 1]), ("row_expert", [2 * E, E])) + TABLE_CONSTS))
        keep["pos"] = ctx.enter_context(nc.sbuf_tensor("pos", [P, TB], I32))
        output_phase(nc, io, keep, sems)
        expert_phase(nc, io, keep, sems)


def kernel(**inputs):
    import numpy as _np
    import concourse.bacc as _bacc
    from concourse import mybir as _mybir
    from concourse.bass_utils import run_bass_kernel_spmd as _run

    x = _np.asarray(inputs["x"]).reshape(B, C, N)
    get = lambda n: _np.asarray(inputs[n])
    wqkv = get("L1_attn_w_qkv").reshape(C, NH, 3, D)
    bqkv = get("L1_attn_b_qkv").reshape(NH, 3, D)
    part = _np.arange(P)
    f = _np.float32
    arrays = {
        "x_c": x, "x_t": x.transpose(0, 2, 1),
        "w_qk0": _np.concatenate([get("L0_conv_wq"), get("L0_conv_wk")]).T, "w_v0": get("L0_conv_wv").T,
        "gamma": get("L0_conv_gamma"),
        "w_qk1": wqkv[:, :, 0:2].reshape(C, 2, HG, 2, D).transpose(0, 1, 3, 2, 4).reshape(C, 4, P),
        "b_qk1": bqkv[:, 0:2].reshape(2, HG, 2, D).transpose(0, 2, 1, 3).reshape(4, P).T,
        "w_v1": wqkv[:, :, 2].reshape(C, C), "b_v1": bqkv[:, 2].reshape(C),
        "gnw": _np.stack([get("L1_attn_gn_scale").reshape(CT, P), get("L1_attn_gn_bias").reshape(CT, P)], -1).transpose(1, 0, 2),
        "w_pr": get("L1_attn_w_proj"), "b_pr": get("L1_attn_b_proj"),
        "w_rt": get("L1_ffn_Wr"), "b_rt": get("L1_ffn_br"),
        "w1": get("L1_ffn_W1"), "b1": get("L1_ffn_b1"), "w2": get("L1_ffn_W2"), "b2": get("L1_ffn_b2"),
        "ident": _np.eye(P, dtype=f),
        "gmat": (part[:, None] // (C // GROUPS) == part[None, :] // (C // GROUPS)).astype(f) / f(C // GROUPS),
        "before": (part[:, None] < part[None, :]).astype(f), "allones": _np.ones((P, P), f),
        "expert_rev": _np.tile(_np.arange(E, 0, -1, dtype=f), (P, 1)),
        "expert_no": _np.tile(_np.arange(E, dtype=f), (P, 1)), "region": _np.tile(_np.arange(E, dtype=f) * REGION, (P, 1)),
        "expert_of": (part % E).astype(f)[:, None],
        "row_expert": (_np.arange(2 * E)[:, None] % E == _np.arange(E)).astype(f),
        "bias_mask": -(_np.arange(2 * E) >= E).astype(f)[:, None],
        "steps128": _np.tile(_np.arange(TB, dtype=f) * P, (P, 1)),
        "token_id": (part[:, None] + P * _np.arange(TB)[None, :]).astype(_np.int32),
        "pad_id": (B * N + part[:, None]).astype(_np.int32),
        "tile_no": _np.tile(_np.arange(TILES, dtype=f), (P, 1)),
    }
    nc = _bacc.Bacc("TRN2", target_bir_lowering=False, num_devices=1)
    feed, io = {}, {}
    for name, a in arrays.items():
        a = _np.ascontiguousarray(a)
        feed[f"in_{name}"] = a
        io[name] = nc.dram_tensor(f"in_{name}", a.shape, _mybir.dt.from_np(a.dtype), kind="ExternalInput").ap()
    io["out"] = nc.dram_tensor("out_tokens", (B * N + P, C), F32, kind="ExternalOutput").ap()
    program(nc, io)
    r = _run(nc, [feed], core_ids=[0])
    out = r.results[0]["out_tokens"]
    return out[:B * N].reshape(B, N, C).transpose(0, 2, 1).reshape(B, C, 32, 32)
```
